# Optimizing a Trainium2 kernel written in Bass

```python
import numpy as np
import jax
import jax.numpy as jnp

def _softmax(x, axis=-1):
    return jax.nn.softmax(x, axis=axis)

def _gelu(x):
    return jax.nn.gelu(x, approximate=True)

def _silu(x):
    return jax.nn.silu(x)

def _sigmoid(x):
    return jax.nn.sigmoid(x)

def _layernorm(x, axis=-1, eps=1e-05):
    m = jnp.mean(x, axis=axis, keepdims=True)
    v = jnp.var(x, axis=axis, keepdims=True)
    return (x - m) / jnp.sqrt(v + eps)

def _scatter_add(tgt, idx, src, axis=0):
    return tgt.at[idx].add(src)

def _segment_sum(src, seg, n):
    return jax.ops.segment_sum(src, seg, n)
kernel_name = 'mk_seq_preln_d1_jaxref_r8_52768e'

def setup_inputs(seed: int=0):
    np.random.seed(seed)
    _w = jnp.asarray

    def _L0_attn_setup():
        import math
        import jax, jax.numpy as jnp
        import numpy as np
        N_HEADS = 16
        NUM_BUCKETS = 32
        MAX_DISTANCE = 128
        ROTARY_BASE = 10000.0

        def rotate_half(x):
            x1, x2 = jnp.split(x, 2, axis=-1)
            return jnp.concatenate((-x2, x1), axis=-1)

        def rotary_freqs(T, dim):
            inv_freq = 1.0 / ROTARY_BASE ** (jnp.arange(0, dim, 2, dtype=jnp.float32) / dim)
            t = jnp.arange(T, dtype=jnp.float32)
            freqs = jnp.einsum('i,j->ij', t, inv_freq)
            return jnp.concatenate((freqs, freqs), axis=-1)

        def rel_pos_bucket_causal(rel_pos, num_buckets=NUM_BUCKETS, max_distance=MAX_DISTANCE):
            n = jnp.maximum(-rel_pos, 0)
            max_exact = num_buckets // 2
            is_small = n < max_exact
            n_safe = jnp.maximum(n, 1).astype(jnp.float32)
            val_if_large = max_exact + (jnp.log(n_safe / max_exact) / math.log(max_distance / max_exact) * (num_buckets - max_exact)).astype(jnp.int32)
            val_if_large = jnp.minimum(val_if_large, num_buckets - 1)
            return jnp.where(is_small, n, val_if_large)
        key = jax.random.key(seed)
        ks = jax.random.split(key, 10)
        B, T, C = (2, 256, 128)
        s = 0.02
        return {'x': jax.random.normal(ks[0], (B, T, C), dtype=jnp.float32), 'Wq': jax.random.normal(ks[1], (C, C), dtype=jnp.float32) * s, 'bq': jnp.zeros((C,), dtype=jnp.float32), 'Wk': jax.random.normal(ks[2], (C, C), dtype=jnp.float32) * s, 'bk': jnp.zeros((C,), dtype=jnp.float32), 'Wv': jax.random.normal(ks[3], (C, C), dtype=jnp.float32) * s, 'bv': jnp.zeros((C,), dtype=jnp.float32), 'Wp': jax.random.normal(ks[4], (C, C), dtype=jnp.float32) * s, 'bp': jnp.zeros((C,), dtype=jnp.float32), 'rel_bias_table': jax.random.normal(ks[5], (NUM_BUCKETS, N_HEADS), dtype=jnp.float32) * s}
    _L0_attn_in = _L0_attn_setup()

    def _L0_ffn_setup():
        import jax, jax.numpy as jnp
        import numpy as np
        TOP_K = 2
        CAPACITY = 512
        EPS = 1e-06
        W_SCALE = 0.02

        def _rms(x, w):
            return x * jax.lax.rsqrt(jnp.mean(x * x, axis=-1, keepdims=True) + EPS) * w
        key = jax.random.key(seed)
        ks = jax.random.split(key, 8)
        B, S, H, F, E = (8, 512, 128, 256, 8)
        F4 = F // 4
        return {'hidden_states': jax.random.normal(ks[0], (B, S, H), jnp.float32), 'Wr': jax.random.normal(ks[1], (H, E), jnp.float32) * W_SCALE, 'norm_w': jnp.ones((E, H), jnp.float32), 'Wg': jax.random.normal(ks[2], (E, H, F), jnp.float32) * W_SCALE, 'Wu': jax.random.normal(ks[3], (E, H, F), jnp.float32) * W_SCALE, 'Wd': jax.random.normal(ks[4], (E, F, H), jnp.float32) * W_SCALE, 'f_norm': jnp.ones((H,), jnp.float32), 'fWg': jax.random.normal(ks[5], (H, F4), jnp.float32) * W_SCALE, 'fWu': jax.random.normal(ks[6], (H, F4), jnp.float32) * W_SCALE, 'fWd': jax.random.normal(ks[7], (F4, H), jnp.float32) * W_SCALE}
    _L0_ffn_in = _L0_ffn_setup()
    _d = {'L0_attn_x': _L0_attn_in['x'], 'L0_attn_Wq': _L0_attn_in['Wq'], 'L0_attn_bq': _L0_attn_in['bq'], 'L0_attn_Wk': _L0_attn_in['Wk'], 'L0_attn_bk': _L0_attn_in['bk'], 'L0_attn_Wv': _L0_attn_in['Wv'], 'L0_attn_bv': _L0_attn_in['bv'], 'L0_attn_Wp': _L0_attn_in['Wp'], 'L0_attn_bp': _L0_attn_in['bp'], 'L0_attn_rel_bias_table': _L0_attn_in['rel_bias_table'], 'L0_ffn_Wr': _L0_ffn_in['Wr'], 'L0_ffn_norm_w': _L0_ffn_in['norm_w'], 'L0_ffn_Wg': _L0_ffn_in['Wg'], 'L0_ffn_Wu': _L0_ffn_in['Wu'], 'L0_ffn_Wd': _L0_ffn_in['Wd'], 'L0_ffn_f_norm': _L0_ffn_in['f_norm'], 'L0_ffn_fWg': _L0_ffn_in['fWg'], 'L0_ffn_fWu': _L0_ffn_in['fWu'], 'L0_ffn_fWd': _L0_ffn_in['fWd']}
    _x0 = _d['L0_attn_x']
    _d['L0_attn_x'] = jax.random.normal(jax.random.fold_in(jax.random.key(seed), 1), (2, 1024, 128), dtype=_x0.dtype)
    del _x0
    return _d

def reference(L0_attn_x, L0_attn_Wq, L0_attn_bq, L0_attn_Wk, L0_attn_bk, L0_attn_Wv, L0_attn_bv, L0_attn_Wp, L0_attn_bp, L0_attn_rel_bias_table, L0_ffn_Wr, L0_ffn_norm_w, L0_ffn_Wg, L0_ffn_Wu, L0_ffn_Wd, L0_ffn_f_norm, L0_ffn_fWg, L0_ffn_fWu, L0_ffn_fWd):

    def _L0_attn_ref(x, Wq, bq, Wk, bk, Wv, bv, Wp, bp, rel_bias_table):
        import math
        import jax, jax.numpy as jnp
        import numpy as np
        N_HEADS = 16
        NUM_BUCKETS = 32
        MAX_DISTANCE = 128
        ROTARY_BASE = 10000.0

        def rotate_half(x):
            x1, x2 = jnp.split(x, 2, axis=-1)
            return jnp.concatenate((-x2, x1), axis=-1)

        def rotary_freqs(T, dim):
            inv_freq = 1.0 / ROTARY_BASE ** (jnp.arange(0, dim, 2, dtype=jnp.float32) / dim)
            t = jnp.arange(T, dtype=jnp.float32)
            freqs = jnp.einsum('i,j->ij', t, inv_freq)
            return jnp.concatenate((freqs, freqs), axis=-1)

        def rel_pos_bucket_causal(rel_pos, num_buckets=NUM_BUCKETS, max_distance=MAX_DISTANCE):
            n = jnp.maximum(-rel_pos, 0)
            max_exact = num_buckets // 2
            is_small = n < max_exact
            n_safe = jnp.maximum(n, 1).astype(jnp.float32)
            val_if_large = max_exact + (jnp.log(n_safe / max_exact) / math.log(max_distance / max_exact) * (num_buckets - max_exact)).astype(jnp.int32)
            val_if_large = jnp.minimum(val_if_large, num_buckets - 1)
            return jnp.where(is_small, n, val_if_large)
        B, T, C = x.shape
        H = N_HEADS
        D = C // H

        def heads(y):
            return y.reshape(B, T, H, D).transpose(0, 2, 1, 3)
        q = heads(x @ Wq + bq)
        k = heads(x @ Wk + bk)
        v = heads(x @ Wv + bv)
        freqs = rotary_freqs(T, D)
        cos, sin = (jnp.cos(freqs), jnp.sin(freqs))
        q = q * cos + rotate_half(q) * sin
        k = k * cos + rotate_half(k) * sin
        pos = jnp.arange(T)
        rel_pos = pos[None, :] - pos[:, None]
        bucket = rel_pos_bucket_causal(rel_pos)
        bias = rel_bias_table[bucket]
        bias = bias.transpose(2, 0, 1)
        att = jnp.einsum('bhid,bhjd->bhij', q, k) + bias[None]
        att = att * (1.0 / math.sqrt(D))
        causal = pos[None, :] <= pos[:, None]
        att = jnp.where(causal[None, None], att, -jnp.inf)
        att = jax.nn.softmax(att, axis=-1)
        y = jnp.einsum('bhij,bhjd->bhid', att, v)
        y = y.transpose(0, 2, 1, 3).reshape(B, T, C)
        return y @ Wp + bp

    def _L0_ffn_ref(hidden_states, Wr, norm_w, Wg, Wu, Wd, f_norm, fWg, fWu, fWd):
        import jax, jax.numpy as jnp
        import numpy as np
        TOP_K = 2
        CAPACITY = 512
        EPS = 1e-06
        W_SCALE = 0.02

        def _rms(x, w):
            return x * jax.lax.rsqrt(jnp.mean(x * x, axis=-1, keepdims=True) + EPS) * w
        B, S, H = hidden_states.shape
        E = Wr.shape[1]
        N = B * S
        x = hidden_states.reshape(N, H)
        probs = jax.nn.softmax(x @ Wr, axis=-1)
        w_topk, e_topk = jax.lax.top_k(probs, TOP_K)
        e_flat = e_topk.reshape(-1)
        oh = jax.nn.one_hot(e_flat, E, dtype=jnp.int32)
        pos = jnp.take_along_axis(jnp.cumsum(oh, axis=0) - 1, e_flat[:, None], axis=1)[:, 0]
        keep = pos < CAPACITY
        x_rep = jnp.repeat(x, TOP_K, axis=0)
        buf = jnp.zeros((E, CAPACITY, H), x.dtype).at[e_flat, pos].set(x_rep, mode='drop')
        h = _rms(buf, norm_w[:, None, :])
        gate = jax.nn.gelu(jnp.einsum('ech,ehf->ecf', h, Wg), approximate=False)
        up = jnp.einsum('ech,ehf->ecf', h, Wu)
        buf_out = jnp.einsum('ecf,efh->ech', gate * up, Wd) + buf
        exp_out = buf_out[e_flat, jnp.minimum(pos, CAPACITY - 1)]
        contrib = w_topk.reshape(-1)[:, None] * exp_out * keep[:, None].astype(x.dtype)
        combined = x + contrib.reshape(N, TOP_K, H).sum(axis=1)
        overflow = (~keep).reshape(N, TOP_K).any(axis=1)
        fh = _rms(x, f_norm)
        fout = jax.nn.gelu(fh @ fWg, approximate=False) * (fh @ fWu) @ fWd + x
        out = jnp.where(overflow[:, None], fout, combined)
        return out.reshape(B, S, H)
    x = L0_attn_x
    x = x + _L0_attn_ref(_layernorm(x, axis=-1), L0_attn_Wq, L0_attn_bq, L0_attn_Wk, L0_attn_bk, L0_attn_Wv, L0_attn_bv, L0_attn_Wp, L0_attn_bp, L0_attn_rel_bias_table)
    x = x + _L0_ffn_ref(_layernorm(x, axis=-1), L0_ffn_Wr, L0_ffn_norm_w, L0_ffn_Wg, L0_ffn_Wu, L0_ffn_Wd, L0_ffn_f_norm, L0_ffn_fWg, L0_ffn_fWu, L0_ffn_fWd)
    return x

_drawn_inputs = setup_inputs


def setup_inputs(seed=0):
    import zlib

    import numpy as np

    out = dict(_drawn_inputs(seed))
    spreads = {'L0_attn_bq': (0.0, 0.8),
     'L0_attn_bk': (0.0, 0.8),
     'L0_attn_bv': (0.0, 0.327),
     'L0_attn_bp': (0.0, 0.1),
     'L0_ffn_norm_w': (1.0, 0.6),
     'L0_ffn_f_norm': (1.0, 0.6)}
    factors = {'L0_attn_Wq': 8.0,
     'L0_attn_Wk': 8.0,
     'L0_attn_Wv': 8.0,
     'L0_attn_rel_bias_table': 8.0,
     'L0_ffn_Wg': 8.0,
     'L0_ffn_Wu': 8.0,
     'L0_ffn_Wd': 8.0,
     'L0_ffn_fWg': 8.0,
     'L0_ffn_fWu': 8.0,
     'L0_ffn_fWd': 8.0}
    for name, (base, spread) in spreads.items():
        noise = np.random.default_rng([zlib.crc32(name.encode()), seed]).standard_normal(out[name].shape)
        drawn = base * np.exp(spread * noise) if base else spread * noise
        out[name] = jnp.asarray(drawn.astype(out[name].dtype))
    for name, factor in factors.items():
        out[name] = (out[name] * factor).astype(out[name].dtype)
    return out
```

```python
from contextlib import ExitStack

import concourse.bass as bass
from concourse import mybir

F32 = mybir.dt.float32
BF16 = mybir.dt.bfloat16
U32 = mybir.dt.uint32
I32 = mybir.dt.int32
ALU = mybir.AluOpType
ACT = mybir.ActivationFunctionType
AX = mybir.AxisListType

P = 128
B, T, C = 2, 1024, 128
H, D = 16, 8
TPB = T // P
TT = B * TPB
HG = 4
NG = B * H // HG
CH = 4
NCH = TT // CH
CW = CH * P
NB = 32
NV = 3 * P
QK_ROWS = 9 * D
M_ROW = 96
ST_ROWS = M_ROW + 3
VW = 32
E_NUM, FF, F4, CAP = 8, 256, 64, 512
NBUF = 3
PBUF = 4
ROW = C + 4
SCALE = float(D) ** -0.5
LN_EPS, RMS_EPS = 1e-5, 1e-6
FAR = 1.0e6
BIG = 3.0e38

UNITS = [(0, 0), (0, 1), (0, 2), (0, 3), (1, 0), (1, 4), (1, 1), (1, 5), (1, 2), (1, 6), (1, 3), (1, 7)]
NU = len(UNITS)
SUNITS = [(0, (0, 1, 2, 3))] + [(t, hs) for t in (1, 2, 3) for hs in ((0, 1), (2, 3))] \
    + [(t, (g,)) for t in (4, 5, 6, 7) for g in range(HG)]
S_AT = [3, 3, 3, 3, 3, 3, 3, 2]


def first_col(qb, kt):
    return max(0, kt - CH * qb) * P


def near(qb, kt):
    lo, hi = max(kt, CH * qb), min(kt + 2, CH * qb + CH)
    return (lo - CH * qb) * P, (hi - CH * qb) * P, (lo - kt) * P


NEAR = [n for n, u in enumerate(UNITS) if near(*u)[0] < near(*u)[1]]
NN = len(NEAR)


def s_offset(t, k):
    return k * (t + 1) * P if t < 2 else k * 512


def plan(prev, do_s, do_t, last):
    out, su = [], 0
    for u in range(NU):
        if do_t:
            out.append(("ST", u))
        if u < 2 and prev:
            out.append(("AV", NU - 2 + u, -1))
        if u >= 2 and do_t:
            out.append(("AV", u - 2, 0))
        if u == 1 and prev:
            out.append(("EVAC", 1, -1))
        if u == 5 and do_t:
            out.append(("EVAC", 0, 0))
        if u == 2 and prev:
            out.append(("Y", 1, -1))
        if do_s and u < len(S_AT):
            for _ in range(S_AT[u]):
                out.append(("S", su))
                su += 1
        if u == 7 and do_t:
            out.append(("Y", 0, 0))
        if u == 10 and do_s:
            out.append(("M",))
    if last:
        out += [("AV", NU - 2, 0), ("AV", NU - 1, 0), ("EVAC", 1, 0), ("Y", 1, 0)]
    return out


def positive(v):
    return not isinstance(v, int) or v > 0


def layer_kernel(nc, x, Wq, bq, Wk, bk, Wv, bv, Wp, bp, table, Wr, norm_w, Wg, Wu, Wd, f_norm,
                 fWg, fWu, fWd, c_wide, c_onehot, c_mask, c_rows, out):
    ctx = ExitStack()
    with ctx:
        def sb(name, shape, dt=F32):
            return ctx.enter_context(nc.sbuf_tensor(name, shape, dt))

        def sem(name):
            return ctx.enter_context(nc.semaphore(name))

        q_parts = nc.dram_tensor("q_parts", [NG, 3, D, HG * T], BF16, kind="Internal")
        k_parts = nc.dram_tensor("k_parts", [NG, 3, D, HG * T], BF16, kind="Internal")
        g_vec = nc.dram_tensor("g_vec", [H, P, NV], F32, kind="Internal")
        r_vec = nc.dram_tensor("r_vec", [H, P, NV], BF16, kind="Internal")
        slots = nc.dram_tensor("slots", [E_NUM * CAP, ROW], F32, kind="Internal")

        ps_slot = ctx.enter_context(nc.psum_tensor("ps_slot", [P, 2, 1024], F32))
        ps_st = ctx.enter_context(nc.psum_tensor("ps_st", [P, 3, 512], F32))
        ps_av = ctx.enter_context(nc.psum_tensor("ps_av", [P, 512], F32))

        wide = sb("wide", [P, 2 * T + 4 * P + E_NUM + TT])
        cos_t, sin_t = wide[:, 0:T], wide[:, T:2 * T]
        ident = wide[:, 2 * T:2 * T + P]
        below = wide[:, 2 * T + P:2 * T + 2 * P]
        swap = wide[:, 2 * T + 2 * P:2 * T + 4 * P]
        expert_no = wide[:, 2 * T + 4 * P:2 * T + 4 * P + E_NUM]
        token_no = wide[:, 2 * T + 4 * P + E_NUM:2 * T + 4 * P + E_NUM + TT]
        onehot = sb("onehot", [NB, 2 * NV])
        vmask = sb("vmask", [H, 2, NV])
        tab = sb("tab", [NB, H])
        ident_b = sb("ident_b", [P, P], BF16)
        below_b = sb("below_b", [P, P], BF16)
        ones_b = sb("ones_b", [P, P], BF16)
        x_sb = sb("x_sb", [P, TT, C])
        w_attn = sb("w_attn", [P, 8, C])
        bcol = sb("bcol", [P, 2])
        bcol_perm = sb("bcol_perm", [P, 4])
        bv_row = sb("bv_row", [P, C])
        bp_row = sb("bp_row", [P, C])
        stats = sb("stats", [P, TT, 6])
        mv = sb("mv", [P, TT, 2])
        rstd = sb("rstd", [P, TT])
        newton = sb("newton", [P, 2 * CH])
        q_stack = sb("q_stack", [P, NBUF, HG, T], BF16)
        k_stack = sb("k_stack", [P, NBUF, HG, T], BF16)
        v_all = sb("v_all", [P, NG, TPB * HG * D])
        v_grp = sb("v_grp", [P, NBUF, TPB, HG, VW])
        f_all = sb("f_all", [P, H * 2 * P])
        b_all = sb("b_all", [P, H * 2 * P], BF16)
        f_grp = sb("f_grp", [P, NBUF, HG, 2 * P])
        b_grp = sb("b_grp", [P, NBUF, HG, 2 * P], BF16)
        probs = sb("probs", [P, PBUF, HG, 512])
        neg_max = sb("neg_max", [P, HG, TPB])
        max_rest = sb("max_rest", [P, HG * TPB])
        max_parts = sb("max_parts", [P, 3, HG * TPB], BF16)
        max_rows = sb("max_rows", [3 * HG * TPB, P], BF16)
        y_raw = sb("y_raw", [P, 2, 512])
        y_rcp = sb("y_rcp", [P, 2, CH, HG])
        y_all = sb("y_all", [P, TT, H // HG, HG * D])

        pro = probs[:, :, :, :].rearrange("p a b c -> p (a b c)")
        xn = pro[:, 0:CW].rearrange("p (t c) -> p t c", t=CH)
        xnT = [pro[:, CW * (1 + i):CW * (2 + i)] for i in range(2)]
        rope_a, rope_b = pro[:, 3 * CW:4 * CW], pro[:, 4 * CW:5 * CW]
        qk_f = [pro[:, (5 + i) * CW:(6 + i) * CW] for i in range(2)]
        qk_rest = [pro[:, (7 + i) * CW:(8 + i) * CW] for i in range(2)]
        part_f = [pro[:, (9 + 2 * i) * CW:(11 + 2 * i) * CW].bitcast(BF16).rearrange("p (a n) -> p a n", n=CW)
                  for i in range(2)]
        g_sb = pro[0:H, 13 * CW:13 * CW + NV]
        r_sb = pro[0:H, 14 * CW:14 * CW + NV // 2].bitcast(BF16)

        end_a = q_stack[:, :, :, :].rearrange("p a b c -> p (a b c)").bitcast(F32)
        end_b = k_stack[:, :, :, :].rearrange("p a b c -> p (a b c)").bitcast(F32)
        u_rows = end_a[:, 0:TT * ROW].rearrange("p (t c) -> p t c", c=ROW)
        uT = end_a[:, TT * ROW:TT * ROW + TT * P]
        yT = [end_a[:, TT * ROW + TT * P + i * CW:TT * ROW + TT * P + (i + 1) * CW] for i in range(2)]
        x1 = end_b[:, 0:TT * C].rearrange("p (t c) -> p t c", c=C)
        fw = end_b[:, TT * C:TT * C + 2 * F4 + C]
        f_act = [end_b[:, TT * C + 2 * F4 + C + i * CW:TT * C + 2 * F4 + C + (i + 1) * CW] for i in range(2)]
        at = TT * C + 2 * F4 + C + 2 * CW
        small = end_b[:, at:at + 64 * TT]

        def col(i, n=1):
            return small[:, i * TT:(i + n) * TT].rearrange("p (t k) -> p t k", k=n)

        wgu = [pro[:, i * 768:i * 768 + 512] for i in range(2)]
        wdn = [pro[:, i * 768 + 512:i * 768 + 768].rearrange("p (c n) -> p c n", c=2) for i in range(2)]
        e0 = 1536
        slot_in = [pro[:, e0 + i * 4 * ROW:e0 + (i + 1) * 4 * ROW].rearrange("p (j c) -> p j c", c=ROW) for i in range(2)]
        e1 = e0 + 8 * ROW
        slotT = [pro[:, e1 + i * 512:e1 + (i + 1) * 512] for i in range(2)]
        e2 = e1 + 1024
        gated = [pro[:, e2 + i * 1024:e2 + (i + 1) * 1024].rearrange("p (c n) -> p c n", c=2) for i in range(2)]
        e3 = e2 + 2048
        e_out = [pro[:, e3 + i * 512:e3 + (i + 1) * 512].rearrange("p (j c) -> p j c", c=C) for i in range(2)]
        tmp_g = y_raw[:, :, :]
        router = sb("router", [P, E_NUM])
        e_norm = sb("e_norm", [P, E_NUM])
        e_wt = sb("e_wt", [P, 2, 3, 4])
        e_tok = sb("e_tok", [P, 2, 4], U32)
        fn_col = sb("fn_col", [P, 1])
        slot_no = sb("slot_no", [P, 2, TT], U32)
        mx8 = sb("mx8", [P, TT, 8])
        ix8 = sb("ix8", [P, TT, 8], U32)
        sel_b = sb("sel_b", [P, TT * E_NUM], BF16)

        x_in = [sem(f"x_in{i}") for i in range(NCH)]
        w_in = sem("w_in")
        c_in = sem("c_in")
        t_in = sem("t_in")
        late_in = sem("late_in")
        const_b = sem("const_b")
        swapped = sem("swapped")
        zeroed = sem("zeroed")
        fixed = sem("fixed")
        st_done = sem("st_done")
        mv_done = sem("mv_done")
        xn_done = sem("xn_done")
        xnT_ps = sem("xnT_ps")
        xnT_sb = sem("xnT_sb")
        qk_ps = sem("qk_ps")
        rope_half = sem("rope_half")
        rope_done = sem("rope_done")
        part_hi = sem("part_hi")
        rest_done = sem("rest_done")
        part_mid = sem("part_mid")
        part_lo = sem("part_lo")
        parts_out = [sem(f"parts_out{i}") for i in range(2)]
        v_ps = sem("v_ps")
        v_done = sem("v_done")
        bswap_ps = sem("bswap_ps")
        bswap_sb = sem("bswap_sb")
        vec_ps = sem("vec_ps")
        vec_exp = sem("vec_exp")
        vec_done = sem("vec_done")
        vec_out = sem("vec_out")
        toep_in = sem("toep_in")
        xb_done = sem("xb_done")
        stack_in = [sem(f"stack_in{i}") for i in range(NBUF)]
        slot_full = sem("slot_full")
        slot_used = sem("slot_used")
        scores = sem("scores")
        exp_done = sem("exp_done")
        near_done = sem("near_done")
        av_done = sem("av_done")
        y_evac = sem("y_evac")
        y_rcp_done = sem("y_rcp_done")
        max_done = sem("max_done")
        msplit = sem("msplit")
        mrows_sb = sem("mrows_sb")
        mrows_in = sem("mrows_in")
        masked = sem("masked")
        v_copied = sem("v_copied")
        yT_ps = sem("yT_ps")
        yT_sb = sem("yT_sb")
        pr_ps = sem("pr_ps")
        x1_done = sem("x1_done")
        ln2 = sem("ln2")
        u_done = sem("u_done")
        uT_ps = sem("uT_ps")
        uT_sb = sem("uT_sb")
        lg_ps = sem("lg_ps")
        in_order = sem("in_order")
        ex_ready = sem("ex_ready")
        ex_done = sem("ex_done")
        sel_done = sem("sel_done")
        pos_ps = sem("pos_ps")
        rows_ready = sem("rows_ready")
        fw_in = sem("fw_in")
        fw_done = sem("fw_done")
        fgu_ps = sem("fgu_ps")
        f_gelu = sem("f_gelu")
        f_act_done = sem("f_act_done")
        f_ps = sem("f_ps")
        base1 = sem("base1")
        base_done = sem("base_done")
        init_out = sem("init_out")
        trash_out = sem("trash_out")
        dispatched = sem("dispatched")
        base_out = sem("base_out")
        ew_in = [sem(f"ew_in{i}") for i in range(2)]
        es_in = [sem(f"es_in{i}") for i in range(2)]
        ew_done = sem("ew_done")
        eT_ps = sem("eT_ps")
        eT_sb = sem("eT_sb")
        gu_ps = sem("gu_ps")
        e_gelu = sem("e_gelu")
        e_gated = sem("e_gated")
        eo_ps = sem("eo_ps")
        ewt = sem("ewt")
        ewt_done = sem("ewt_done")
        eo_done = sem("eo_done")
        added = sem("added")
        tile_seen = sem("tile_seen")
        stack_free = sem("stack_free")
        add_turn = sem("add_turn")

        x_tiles = x.rearrange("b (t p) c -> p (b t) c", p=P)
        out_tiles = out[0:B * T, :].rearrange("(t p) c -> p t c", p=P)

        block = ctx.enter_context(nc.Block())

        def step_args(i):
            return [(2 + 3 * i + j, (2 + j) % NBUF, i + (2 + j) // NBUF) for j in range(3)]

        def slot_base(s):
            if isinstance(s, int) and s < 2:
                return 24 * s
            return 26 * s - 3

        def base_parity(s):
            return slot_base(s) % 2 if isinstance(s, int) else 1

        @block.sync
        def _(sp):
            for c in range(NCH):
                sp.dma_start(x_sb[:, c * CH:(c + 1) * CH, :], x_tiles[:, c * CH:(c + 1) * CH, :]).then_inc(x_in[c], 16)
                if c == 0:
                    for i, w in enumerate((Wq, Wk, Wv, Wp)):
                        sp.dma_start(w_attn[:, i, :], w[:, :]).then_inc(w_in, 16)
            for c in range(NCH):
                for i, dst in enumerate((q_parts, k_parts)):
                    sp.wait_ge(part_lo, 2 * c + i + 1)
                    for a in range(3):
                        n0, tok = (c // 2) * 4, (c % 2) * CW
                        ap = bass.AP(tensor=dst, offset=(n0 * 3 + a) * HG * D * T + tok,
                                     ap=[[3 * HG * D * T, 4], [T, HG * D], [1, CW]])
                        sp.dma_start(ap, part_f[i][:, a, :]).then_inc(parts_out[i], 16)
            sp.wait_ge(vec_done, 2)
            for dst, vec in ((r_vec, r_sb), (g_vec, g_sb)):
                src = bass.AP(tensor=vec.tensor, offset=vec.offset, ap=[list(vec.ap[0]), [0, P], [1, NV]])
                sp.dma_start(dst[:, :, :], src).then_inc(vec_out, 16)
            sp.wait_ge(vec_out, 32)
            for dst, vec in ((b_all, r_vec), (f_all, g_vec)):
                src = bass.AP(tensor=vec, offset=P - 1, ap=[[NV - 1, P], [P * NV, H], [1, 2 * P]])
                sp.dma_start(dst[:, :].rearrange("p (h c) -> p h c", h=H), src).then_inc(toep_in, 16)

            def load_stack(n, buf):
                for a in range(3):
                    sp.dma_start(q_stack[24 * a:24 * a + 24, buf, :, :].rearrange("p g t -> p (g t)"),
                                 bass.AP(tensor=q_parts, offset=n * (3 * HG * D * T) + a * (HG * D * T),
                                         ap=[[0, 3], [HG * T, D], [1, HG * T]])).then_inc(stack_in[buf], 16)
                sp.dma_start(k_stack[0:QK_ROWS, buf, :, :].rearrange("p g t -> p (g t)"),
                             bass.AP(tensor=k_parts, offset=n * (3 * HG * D * T),
                                     ap=[[0, 3], [HG * T, 3 * D], [1, HG * T]])).then_inc(stack_in[buf], 16)
                w = HG * 2 * P
                for dst, src in ((b_grp, b_all), (f_grp, f_all)):
                    sp.dma_start(dst[:, buf, :, :].rearrange("p g c -> p (g c)"),
                                 src[:, bass.ds((n % (H // HG)) * w, w)]).then_inc(stack_in[buf], 16)

            sp.wait_ge(parts_out[0], NCH * 48)
            sp.wait_ge(parts_out[1], NCH * 48)
            sp.wait_ge(fixed, 2)
            sp.wait_ge(toep_in, 32)
            load_stack(0, 0)

            def step(s, buf, fill, more=True):
                if more:
                    if positive(48 * (s - 1)):
                        sp.wait_ge(near_done, NN * (s - 1))
                        sp.sem_inc(stack_free, 1)
                    load_stack((s + 1) % NG, (buf + 1) % NBUF)
                sp.wait_ge(mrows_sb, s + 1)
                sp.dma_start(q_stack[M_ROW:M_ROW + 3, buf, :, :].rearrange("a g (t p) -> a (g t) p", p=P),
                             max_rows[:, :]).then_inc(mrows_in, 16)

            step(0, 0, 0)
            step(1, 1, 0)
            with sp.Fori(0, 2) as i:
                for a in step_args(i):
                    step(*a)

            sp.wait_ge(av_done, NU * NG)
            sp.wait_ge(init_out, 16 * E_NUM)

            def load_weights(e, i):
                sp.dma_start(wgu[i][:, 0:FF], Wg[bass.ds(e, 1), :, :].rearrange("a h f -> (a h) f")).then_inc(ew_in[i], 16)
                sp.dma_start(wgu[i][:, FF:2 * FF], Wu[bass.ds(e, 1), :, :].rearrange("a h f -> (a h) f")).then_inc(ew_in[i], 16)
                sp.dma_start(wdn[i], Wd[bass.ds(e, 1), :, :].rearrange("a (c p) h -> (a p) c h", p=P)).then_inc(ew_in[i], 16)

            def load_slots(e, i):
                src = slots[bass.ds(e * CAP, CAP), :].rearrange("(p j) c -> p j c", j=4)
                sp.dma_start(slot_in[i], src).then_inc(es_in[i], 16)

            load_weights(0, 0)
            load_weights(1, 1)
            sp.wait_ge(base_done, TT)
            sp.dma_start(out_tiles, x1).then_inc(base_out, 16)
            sp.wait_ge(dispatched, 2 * TT * 16)
            load_slots(0, 0)
            load_slots(1, 1)

            def expert(e, i):
                sp.wait_ge(eT_ps, e + 1)
                sp.wait_ge(ewt_done, 2 * e + 2)
                load_slots(e + 2, i)
                sp.wait_ge(eo_ps, e + 1)
                load_weights(e + 2, i)

            with sp.Fori(0, (E_NUM - 2) // 2) as k:
                for i in range(2):
                    expert(2 * k + i, i)

        @block.gpsimd
        def _(pool):
            zero_views = [st[:, :, :, :].rearrange("p a b c -> p (a b c)").bitcast(F32) for st in (q_stack, k_stack)]
            pool.memset(ones_b[:, :], 1.0).then_inc(const_b, 1)
            pool.wait_ge(w_in, 64)
            for i in range(2):
                src = w_attn[:, i, :].rearrange("p (n g d) -> p n d g", g=HG, d=D)
                plain = w_attn[:, 4 + i, :].rearrange("p (n d g) -> p n d g", g=HG, d=D)
                other = w_attn[:, 6 + i, :].rearrange("p (n d g) -> p n d g", g=HG, d=D)
                pool.tensor_copy(plain, src).then_inc(swapped, 1)
                for a in range(2):
                    d0, d1 = a * D // 2, (1 - a) * D // 2
                    pool.tensor_copy(other[:, :, d0:d0 + D // 2, :], src[:, :, d1:d1 + D // 2, :]).then_inc(swapped, 1)
            for v in zero_views:
                pool.memset(v, 0.0).then_inc(zeroed, 1)
            pool.memset(v_grp[:, :, :, :, :], 0.0).then_inc(zeroed, 1)
            pool.wait_ge(zeroed, 3)
            pool.memset(v_grp[:, :, :, :, D:D + 1], 1.0).then_inc(fixed, 1)
            pool.wait_ge(fixed, 1)
            pool.memset(k_stack[M_ROW:M_ROW + 3, :, :, :], 1.0).then_inc(fixed, 1)
            pool.wait_ge(fixed, 2)

            for c in range(NCH):
                for i in range(2):
                    pool.wait_ge(part_hi, 2 * c + i + 1)
                    pool.tensor_tensor(qk_rest[i], qk_f[i], part_f[i][:, 0, :], ALU.subtract).then_inc(rest_done, 1)
                for i in range(2):
                    pool.wait_ge(part_mid, 2 * c + i + 1)
                    pool.tensor_tensor(part_f[i][:, 2, :], qk_rest[i], part_f[i][:, 1, :], ALU.subtract).then_inc(part_lo, 1)

            def step(s, buf, fill):
                fbuf = (buf - 1) % NBUF
                pool.wait_ge(stack_in[fbuf], 96 * (fill + 1))
                for r, u in enumerate(NEAR):
                    qb, kt = UNITS[u]
                    lo, hi, fo = near(qb, kt)
                    pr = probs[:, u % PBUF, :, lo:hi]
                    pool.wait_ge(exp_done, 48 * (s - 1) + HG * (u + 1))
                    if fo == 0:
                        diag = probs[:, u % PBUF, :, lo:lo + P]
                        pool.sem_inc(tile_seen, 1)
                        pool.affine_select(out=diag, in_=diag, compare_op=ALU.is_ge, fill=0.0, base=0,
                                           pattern=[[0, HG], [1, P]], channel_multiplier=-1).then_inc(masked, 1)
                        pool.wait_ge(masked, TPB * (s - 1) + kt + 1)
                    pool.tensor_tensor(pr, pr, f_grp[:, fbuf, :, fo:fo + hi - lo], ALU.mult).then_inc(near_done, 1)

            step(1, 1, 0)
            with pool.Fori(0, 2) as i:
                for j, (s, buf, _) in enumerate(step_args(i)):
                    step(s, buf, i + (1 + j) // NBUF)
            step(NG, NG % NBUF, (NG - 1) // NBUF)

            pool.wait_ge(rows_ready, 1)
            pool.wait_ge(init_out, 16 * E_NUM)
            for t in range(TT):
                for k in range(2):
                    pool.indirect_dma_start(slots[:, :], bass.IndirectOffsetOnAxis(ap=slot_no[:, k, t:t + 1], axis=0),
                                            u_rows[:, t, :], None, bounds_check=E_NUM * CAP - 1,
                                            oob_is_err=False).then_inc(dispatched, 16)
            pool.wait_ge(base_out, 16)
            pool.wait_ge(trash_out, 16)

            def add_rows(e, i):
                pool.wait_ge(eo_done, 4 * (e + 1))
                if positive(e):
                    pool.wait_ge(added, 64 * e)
                    pool.sem_inc(add_turn, 1)
                for j in range(4):
                    pool.indirect_dma_start(out[:, :], bass.IndirectOffsetOnAxis(ap=e_tok[:, i, j:j + 1], axis=0),
                                            e_out[i][:, j, :], None, bounds_check=B * T + CAP - 1,
                                            oob_is_err=True, compute_op=ALU.add).then_inc(added, 16)

            add_rows(0, 0)
            add_rows(1, 1)
            with pool.Fori(1, E_NUM // 2) as k:
                for i in range(2):
                    add_rows(2 * k + i, i)
            pool.wait_ge(added, 64 * E_NUM)

        @block.scalar
        def _(act):
            act.dma_start(wide[:, :], c_wide[:, :]).then_inc(c_in, 16)
            act.dma_start(bcol[:, 0:1], bq.rearrange("(p a) -> p a", a=1)).then_inc(c_in, 16)
            act.dma_start(bcol[:, 1:2], bk.rearrange("(p a) -> p a", a=1)).then_inc(c_in, 16)
            act.dma_start(bv_row[:, :], bass.AP(tensor=bv.tensor, offset=0, ap=[[0, P], [1, C]])).then_inc(c_in, 16)
            act.dma_start(onehot[:, :], c_onehot[:, :]).then_inc(t_in, 16)
            act.dma_start(vmask[:, :, :], c_mask[:, :, :]).then_inc(t_in, 16)
            act.dma_start(tab[:, :], table[:, :]).then_inc(t_in, 16)
            act.dma_start(bp_row[:, :], bass.AP(tensor=bp.tensor, offset=0, ap=[[0, P], [1, C]])).then_inc(late_in, 16)
            act.dma_start(e_norm[:, :], norm_w.rearrange("e h -> h e"), allow_slow_non_contiguous=True).then_inc(late_in, 16)
            act.dma_start(router[:, :], Wr[:, :]).then_inc(late_in, 16)
            act.dma_start(fn_col[:, :], f_norm.rearrange("(p a) -> p a", a=1)).then_inc(late_in, 16)
            for e in range(E_NUM):
                act.dma_start(slots[e * CAP:(e + 1) * CAP, :], c_rows[:, :]).then_inc(init_out, 16)
            act.dma_start(out[B * T:B * T + CAP, :], c_rows[:, 0:C]).then_inc(trash_out, 16)

            for c in range(NCH):
                act.wait_ge(xnT_ps, c + 1)
                if c >= 2:
                    act.wait_ge(v_ps, c - 1)
                act.activation(xnT[c % 2], ps_av[:, :], ACT.Copy).then_inc(xnT_sb, 1)
                if c == 0:
                    act.wait_ge(vec_ps, 2)
                    act.activation(g_sb, ps_st[0:H, 1, 0:NV], ACT.Exp, scale=SCALE).then_inc(vec_exp, 1)
                for i in range(2):
                    act.wait_ge(rope_done, 2 * c + i + 1)
                    if c >= 1:
                        act.wait_ge(parts_out[i], 48 * c)
                    act.activation(part_f[i][:, 0, :], qk_f[i], ACT.Copy).then_inc(part_hi, 1)
                for i in range(2):
                    act.wait_ge(rest_done, 2 * c + i + 1)
                    act.activation(part_f[i][:, 1, :], qk_rest[i], ACT.Copy).then_inc(part_mid, 1)

            def copy_v(n, buf):
                act.activation(v_grp[:, buf, :, :, 0:D],
                               v_all[:, bass.ds(n, 1), :].rearrange("p a (t g d) -> p (a t) g d", g=HG, d=D),
                               ACT.Copy).then_inc(v_copied, 1)

            def step(s, buf, fill, prev=True, do_s=True, last=False):
                for what in plan(prev, do_s, True, last):
                    if what[0] == "M":
                        if positive(NU * (s - 2)):
                            act.wait_ge(av_done, NU * (s - 2))
                        copy_v(s, buf)
                    if what[0] == "ST":
                        u = what[1]
                        qb, kt = UNITS[u]
                        c0 = first_col(qb, kt)
                        if u >= PBUF or positive(NU * (s - 1)):
                            act.wait_ge(av_done, NU * (s - 1) + u - PBUF + 1)
                        for g in range(HG):
                            n = HG * u + g
                            act.wait_ge(scores, 48 * (s - 1) + n + 1)
                            act.activation(probs[:, u % PBUF, g, c0:512], ps_st[:, n % 3, c0:512], ACT.Exp,
                                           scale=SCALE).then_inc(exp_done, 1)
                    if what[0] == "EVAC":
                        qb, back = what[1:]
                        act.wait_ge(av_done, NU * (s + back) - (NU - 4 if qb == 0 else 0))
                        old = 2 * (s + back - 2) + qb + 1
                        if positive(old):
                            act.wait_ge(y_rcp_done, old)
                        act.activation(y_raw[:, qb, :], ps_av[:, :], ACT.Copy).then_inc(y_evac, 1)

            act.wait_ge(part_lo, 2 * NCH)
            act.wait_ge(parts_out[0], 48 * NCH)
            act.wait_ge(parts_out[1], 48 * NCH)
            act.wait_ge(vec_out, 32)
            act.wait_ge(v_done, NCH)
            act.wait_ge(fixed, 2)
            copy_v(0, 0)
            step(1, 1, 0, prev=False)
            with act.Fori(0, 2) as i:
                for a in step_args(i):
                    step(*a)
            step(NG, NG % NBUF, 0, do_s=False, last=True)

            act.wait_ge(stack_in[NG % NBUF], 96 * (NG // NBUF + 1))
            act.dma_start(fw[:, 0:F4], fWg[:, :]).then_inc(fw_in, 16)
            act.dma_start(fw[:, F4:2 * F4], fWu[:, :]).then_inc(fw_in, 16)
            act.dma_start(fw[0:F4, 2 * F4:2 * F4 + C], fWd[:, :]).then_inc(fw_in, 16)
            for c in range(NCH):
                act.wait_ge(yT_ps, c + 1)
                if c >= 2:
                    act.wait_ge(pr_ps, c - 1)
                act.activation(yT[c % 2], ps_slot[:, c % 2, 0:CW], ACT.Copy).then_inc(yT_sb, 1)
                act.wait_ge(uT_ps, c + 1)
                act.activation(uT[:, c * CW:(c + 1) * CW], ps_st[:, 0, :], ACT.Copy).then_inc(uT_sb, 1)
            act.wait_ge(ex_ready, 1)
            act.activation(col(16, 9), col(16, 9), ACT.Exp).then_inc(ex_done, 1)
            for c in range(NCH):
                act.wait_ge(fgu_ps, c + 1)
                if c >= 2:
                    act.wait_ge(f_act_done, c - 1)
                act.activation(tmp_g[0:F4, c % 2, :], ps_st[0:F4, 2, :], ACT.Gelu).then_inc(f_gelu, 1)

            def expert(e, i):
                act.wait_ge(eT_ps, e + 1)
                if positive(e - 1):
                    act.wait_ge(gu_ps, 2 * (e - 1))
                act.activation(slotT[i], ps_slot[:, 0, 0:512], ACT.Copy).then_inc(eT_sb, 1)
                for c in range(2):
                    act.wait_ge(gu_ps, 2 * e + c + 1)
                    if positive(2 * e + c - 1):
                        act.wait_ge(e_gated, 2 * e + c - 1)
                    act.activation(tmp_g[:, c, :], ps_st[:, c, :], ACT.Gelu).then_inc(e_gelu, 1)

            act.wait_ge(f_act_done, NCH)
            expert(0, 0)
            expert(1, 1)
            with act.Fori(1, E_NUM // 2) as k:
                for i in range(2):
                    expert(2 * k + i, i)

        @block.tensor
        def _(pe):
            pe.wait_ge(t_in, 48)
            for v in range(2):
                pe.matmul(ps_st[0:H, 1 + v, 0:NV], tab[:, :], onehot[:, v * NV:(v + 1) * NV],
                          start=True, stop=True).then_inc(vec_ps, 1)
            pe.wait_ge(c_in, 64)
            for i in range(2):
                mm = pe.matmul(ps_st[:, 0, 2 * i:2 * i + 2], swap[:, i * P:(i + 1) * P], bcol[:, :], start=True, stop=True)
            mm.then_inc(bswap_ps, 1)
            pe.wait_ge(swapped, 6)
            pe.wait_ge(bswap_sb, 1)

            for c in range(NCH):
                pe.wait_ge(xn_done, CH * (c + 1))
                if c >= 1:
                    pe.wait_ge(xnT_sb, c)
                for t in range(CH):
                    mm = pe.transpose(ps_av[:, t * P:(t + 1) * P], xn[:, t, :], ident)
                mm.then_inc(xnT_ps, 1)
                pe.wait_ge(xnT_sb, c + 1)
                for i in range(2):
                    if c >= 1:
                        pe.wait_ge(rope_half, 4 * (c - 1) + 2 * i + 2)
                    pe.matmul(ps_slot[:, i, 0:512], w_attn[:, 4 + i, :], xnT[c % 2], start=True, stop=True)
                    pe.matmul(ps_slot[:, i, 512:1024], w_attn[:, 6 + i, :], xnT[c % 2], start=True,
                              stop=True).then_inc(qk_ps, 1)
                if c >= 1:
                    pe.wait_ge(v_done, c)
                for t in range(CH):
                    mm = pe.matmul(ps_st[:, 0, t * P:(t + 1) * P], xnT[c % 2][:, t * P:(t + 1) * P], w_attn[:, 2, :],
                                   start=True, stop=True)
                mm.then_inc(v_ps, 1)

            def s_unit(s, buf, k, slot, su):
                t, heads = SUNITS[su]
                w = (t + 1) * P
                if positive(k - 1):
                    pe.wait_ge(slot_used, k - 1)
                for j, g in enumerate(heads):
                    o = s_offset(t, j)
                    b0 = max(0, (t - 1) * P)
                    for lo in range(0, w, 512):
                        hi = min(w, lo + 512)
                        nlo, nhi = max(lo, b0), hi
                        pe.matmul(ps_slot[:, slot, o + lo:o + hi], q_stack[0:QK_ROWS, buf, g, t * P:(t + 1) * P],
                                  k_stack[0:QK_ROWS, buf, g, lo:hi], start=True, stop=(nlo >= nhi))
                        if nlo < nhi:
                            f0 = nlo - (t - 1) * P
                            mm = pe.matmul(ps_slot[:, slot, o + nlo:o + nhi], ident_b[:, :],
                                           b_grp[:, buf, g, f0:f0 + nhi - nlo], start=False, stop=True)
                mm.then_inc(slot_full, 1)

            def step(s, buf, fill, prev=True, do_s=True, do_t=True, last=False):
                tbuf = (buf - 1) % NBUF
                k, slot = slot_base(s), base_parity(s)
                n_slot = 0
                if do_s:
                    pe.wait_ge(stack_in[buf], 96 * (fill + 1))
                if do_t:
                    pe.wait_ge(mrows_in, 16 * s)
                    pe.wait_ge(v_copied, s)
                for what in plan(prev, do_s, do_t, last):
                    if what[0] == "ST":
                        u = what[1]
                        qb, kt = UNITS[u]
                        c0 = first_col(qb, kt)
                        for g in range(HG):
                            n = HG * u + g
                            if n >= 3 or positive(48 * (s - 1)):
                                pe.wait_ge(exp_done, 48 * (s - 1) + n - 2)
                            pe.matmul(ps_st[:, n % 3, c0:512], k_stack[0:ST_ROWS, tbuf, g, kt * P:(kt + 1) * P],
                                      q_stack[0:ST_ROWS, tbuf, g, qb * 512 + c0:qb * 512 + 512],
                                      start=True, stop=True).then_inc(scores, 1)
                    elif what[0] == "AV":
                        u, back = what[1:]
                        qb, kt = UNITS[u]
                        c0 = first_col(qb, kt)
                        vb = (tbuf + back) % NBUF
                        n = s - 1 + back
                        if u in NEAR:
                            pe.wait_ge(near_done, NN * n + NEAR.index(u) + 1)
                        else:
                            pe.wait_ge(exp_done, 48 * n + HG * (u + 1))
                        if u in (0, 4) and positive(2 * n + (u == 4)):
                            pe.wait_ge(y_evac, 2 * n + (1 if u == 4 else 0))
                        for g in range(HG):
                            mm = pe.matmul(ps_av[32 * g:32 * g + VW, c0:512], v_grp[:, vb, kt, g, :],
                                           probs[:, u % PBUF, g, c0:512], start=(u in (0, 4)), stop=(u in (3, 11)),
                                           skip_group_check=True)
                        mm.then_inc(av_done, 1)
                    elif what[0] == "S":
                        s_unit(s, buf, k + n_slot, (slot + n_slot) % 2, what[1])
                        n_slot += 1
                    elif what[0] == "Y":
                        qb, back = what[1:]
                        pe.wait_ge(y_evac, 2 * (s - 1 + back) + qb + 1)
                        pe.wait_ge(slot_used, k + n_slot - 1)
                        for t in range(CH):
                            mm = pe.transpose(ps_slot[:, (slot + n_slot) % 2, t * P:(t + 1) * P],
                                              y_raw[:, qb, t * P:(t + 1) * P], ident)
                        mm.then_inc(slot_full, 1)
                        n_slot += 1
                    elif what[0] == "M":
                        pe.wait_ge(msplit, 4 * (s + 1))
                        pe.wait_ge(slot_used, k + n_slot - 1)
                        pe.transpose(ps_slot[0:3 * HG * TPB, (slot + n_slot) % 2, 0:P // 2].bitcast(BF16),
                                     max_parts[:, :, :].rearrange("p a n -> p (a n)"), ident_b[:, :]).then_inc(slot_full, 1)
                        n_slot += 1

            pe.wait_ge(const_b, 3)
            pe.wait_ge(rope_half, 4 * NCH)
            pe.wait_ge(v_done, NCH)
            pe.wait_ge(vec_done, 2)
            step(0, 0, 0, prev=False, do_t=False)
            step(1, 1, 0, prev=False)
            with pe.Fori(0, 2) as i:
                for a in step_args(i):
                    step(*a)
            step(NG, NG % NBUF, 0, do_s=False, last=True)

            for c in range(NCH):
                if c == 0:
                    pe.wait_ge(slot_used, slot_base(NG) + 2)
                if c >= 2:
                    pe.wait_ge(yT_sb, c - 1)
                for t in range(CH):
                    tile = c * CH + t
                    mm = pe.transpose(ps_slot[:, c % 2, t * P:(t + 1) * P], y_all[:, tile, :, :].rearrange("p a c -> p (a c)"), ident)
                mm.then_inc(yT_ps, 1)
                pe.wait_ge(yT_sb, c + 1)
                if c >= 2:
                    pe.wait_ge(x1_done, c - 1)
                for t in range(CH):
                    mm = pe.matmul(ps_slot[:, c % 2, 512 + t * P:512 + (t + 1) * P], yT[c % 2][:, t * P:(t + 1) * P],
                                   w_attn[:, 3, :], start=True, stop=True)
                mm.then_inc(pr_ps, 1)
                pe.wait_ge(u_done, CH * (c + 1))
                if c >= 1:
                    pe.wait_ge(uT_sb, c)
                for t in range(CH):
                    mm = pe.transpose(ps_st[:, 0, t * P:(t + 1) * P], u_rows[:, c * CH + t, 0:C], ident)
                mm.then_inc(uT_ps, 1)
                pe.wait_ge(uT_sb, c + 1)
                for t in range(CH):
                    tile = c * CH + t
                    mm = pe.matmul(ps_st[:, 1, tile * E_NUM:(tile + 1) * E_NUM], uT[:, tile * P:(tile + 1) * P],
                                   router[:, :], start=True, stop=True)
                mm.then_inc(lg_ps, 1)
            pe.wait_ge(fw_done, 3)
            for c in range(NCH):
                if c >= 1:
                    pe.wait_ge(f_act_done, c)
                pe.matmul(ps_st[0:F4, 2, :], fw[:, 0:F4], uT[:, c * CW:(c + 1) * CW], start=True, stop=True)
                pe.matmul(ps_av[0:F4, :], fw[:, F4:2 * F4], uT[:, c * CW:(c + 1) * CW], start=True,
                          stop=True).then_inc(fgu_ps, 1)
                if c == 0:
                    pe.wait_ge(sel_done, 1)
                    pe.matmul(ps_st[:, 1, 256:384], below_b[:, :], sel_b[:, :], start=True, stop=False)
                    for t in range(1, TT):
                        mm = pe.matmul(ps_st[:, 1, 256 + E_NUM * t:384], ones_b[:, :], sel_b[:, 0:(TT - t) * E_NUM],
                                       start=False, stop=(t == TT - 1))
                    mm.then_inc(pos_ps, 1)
                pe.wait_ge(f_act_done, c + 1)
                if c == 0:
                    pe.wait_ge(x1_done, NCH)
                for t in range(CH):
                    tile = c * CH + t
                    mm = pe.matmul(ps_slot[:, tile // 8, (tile % 8) * C:(tile % 8 + 1) * C],
                                   f_act[c % 2][:, t * P:(t + 1) * P], fw[:, 2 * F4:2 * F4 + C], start=True, stop=True)
                mm.then_inc(f_ps, 1)

            def turn(e, i, n):
                pe.wait_ge(es_in[i], 16 * (n + 1))
                if positive(e):
                    pe.wait_ge(eT_sb, e)
                for j in range(4):
                    mm = pe.transpose(ps_slot[:, 0, j * P:(j + 1) * P], slot_in[i][:, j, 0:C], ident)
                mm.then_inc(eT_ps, 1)

            def gate_up(e, i):
                pe.wait_ge(eT_sb, e + 1)
                pe.wait_ge(ew_done, 2 * (e + 1))
                for c in range(2):
                    if positive(2 * e + c - 1):
                        pe.wait_ge(e_gated, 2 * e + c - 1)
                    pe.matmul(ps_st[:, c, :], wgu[i][:, c * P:(c + 1) * P], slotT[i], start=True, stop=True)
                    up = ps_st[:, 2, :] if c == 0 else ps_av[:, :]
                    pe.matmul(up, wgu[i][:, FF + c * P:FF + (c + 1) * P], slotT[i], start=True,
                              stop=True).then_inc(gu_ps, 1)

            def down(e, i):
                pe.wait_ge(e_gated, 2 * (e + 1))
                if positive(e):
                    pe.wait_ge(eo_done, 4 * e)
                for j in range(4):
                    for c in range(2):
                        mm = pe.matmul(ps_slot[:, 1, j * C:(j + 1) * C], gated[i][:, c, j * P:(j + 1) * P], wdn[i][:, c, :],
                                       start=(c == 0), stop=(c == 1))
                mm.then_inc(eo_ps, 1)

            pe.wait_ge(base_done, TT)
            turn(0, 0, 0)
            gate_up(0, 0)
            turn(1, 1, 0)
            with pe.Fori(0, E_NUM // 2 - 1) as k:
                gate_up(2 * k + 1, 1)
                turn(2 * k + 2, 0, k + 1)
                down(2 * k, 0)
                gate_up(2 * k + 2, 0)
                turn(2 * k + 3, 1, k + 1)
                down(2 * k + 1, 1)
            gate_up(E_NUM - 1, 1)
            down(E_NUM - 2, 0)
            down(E_NUM - 1, 1)

        @block.vector
        def _(dve):
            dve.wait_ge(c_in, 64)
            dve.tensor_copy(ident_b[:, :], ident).then_inc(const_b, 1)
            dve.tensor_copy(below_b[:, :], below).then_inc(const_b, 1)

            own = [0]

            def after(ins):
                own[0] += 1
                ins.then_inc(in_order, 1)
                dve.wait_ge(in_order, own[0])

            def rsqrt(dst, src, eps):
                v, t = newton[:, 0:CH], newton[:, CH:2 * CH]
                after(dve.tensor_scalar(v, src, eps, None, ALU.add))
                after(dve.tensor_scalar(dst.bitcast(U32), v.bitcast(U32), 1, None, ALU.logical_shift_right))
                after(dve.tensor_scalar(dst.bitcast(I32), dst.bitcast(I32), -1.0, float(0x5F3759DF), ALU.mult, ALU.add))
                for _ in range(3):
                    after(dve.tensor_tensor(t, dst, dst, ALU.mult))
                    after(dve.scalar_tensor_tensor(out=t, in0=t, scalar=-0.5, in1=v, op0=ALU.mult, op1=ALU.mult))
                    after(dve.scalar_tensor_tensor(out=dst, in0=t, scalar=1.5, in1=dst, op0=ALU.add, op1=ALU.mult))

            def norm_stats(src, c, n):
                for t in range(CH):
                    dve.bn_stats(stats[:, c * CH + t, :], src[:, c * CH + t, :]).then_inc(st_done, 1)
                dve.wait_ge(st_done, CH * (n + 1))
                for t in range(CH):
                    dve.bn_aggr(mv[:, c * CH + t, :], stats[:, c * CH + t, :]).then_inc(mv_done, 1)
                dve.wait_ge(mv_done, CH * (n + 1))
                rsqrt(rstd[:, c * CH:(c + 1) * CH], mv[:, c * CH:(c + 1) * CH, 1], LN_EPS)

            def ln1(c):
                dve.wait_ge(x_in[c], 16)
                norm_stats(x_sb, c, c)
                if c >= 1:
                    dve.wait_ge(xnT_ps, c)
                for t in range(CH):
                    tile = c * CH + t
                    dve.tensor_scalar(xn[:, t, :], x_sb[:, tile, :], mv[:, tile, 0:1], rstd[:, tile:tile + 1],
                                      ALU.subtract, ALU.mult).then_inc(xn_done, 1)

            ln1(0)
            dve.wait_ge(bswap_ps, 1)
            dve.tensor_copy(bcol_perm[:, :], ps_st[:, 0, 0:4]).then_inc(bswap_sb, 1)
            dve.wait_ge(bswap_sb, 1)
            for c in range(NCH):
                tok = (c % 2) * CW
                for i in range(2):
                    n = 2 * c + i
                    dve.wait_ge(qk_ps, n + 1)
                    if n >= 1:
                        dve.wait_ge(rope_done, n)
                    dve.scalar_tensor_tensor(out=rope_a, in0=ps_slot[:, i, 0:512], scalar=bcol_perm[:, i:i + 1],
                                             in1=cos_t[:, tok:tok + CW], op0=ALU.add, op1=ALU.mult).then_inc(rope_half, 1)
                    dve.scalar_tensor_tensor(out=rope_b, in0=ps_slot[:, i, 512:1024], scalar=bcol_perm[:, 2 + i:3 + i],
                                             in1=sin_t[:, tok:tok + CW], op0=ALU.add, op1=ALU.mult).then_inc(rope_half, 1)
                    dve.wait_ge(rope_half, 2 * n + 2)
                    if c >= 1:
                        dve.wait_ge(rest_done, 2 * (c - 1) + i + 1)
                    dve.tensor_tensor(qk_f[i], rope_a, rope_b, ALU.add).then_inc(rope_done, 1)
                    if c + 1 < NCH and i == 0:
                        ln1(c + 1)
                    if c == 0 and i == 1:
                        dve.wait_ge(vec_exp, 1)
                        dve.tensor_tensor(g_sb, g_sb, vmask[:, 0, :], ALU.mult).then_inc(vec_done, 1)
                        dve.wait_ge(vec_ps, 2)
                        dve.tensor_tensor(r_sb, ps_st[0:H, 2, 0:NV], vmask[:, 1, :], ALU.add).then_inc(vec_done, 1)
                dve.wait_ge(v_ps, c + 1)
                for t in range(CH):
                    tile = c * CH + t
                    b, kt = tile // TPB, tile % TPB
                    dst = v_all[:, b * 4:b * 4 + 4, kt * HG * D:(kt + 1) * HG * D]
                    ins = dve.tensor_tensor(dst, ps_st[:, 0, t * P:(t + 1) * P].rearrange("p (n c) -> p n c", n=4),
                                            bv_row[:, :].rearrange("p (n c) -> p n c", n=4), ALU.add)
                ins.then_inc(v_done, 1)
            dve.wait_ge(late_in, 64)
            for t in range(TT):
                dve.tensor_tensor(x_sb[:, t, :], x_sb[:, t, :], bp_row[:, :], ALU.add).then_inc(xb_done, 1)

            def step(s, buf, fill, prev=True, do_s=True, do_t=True, last=False):
                k, slot = slot_base(s), base_parity(s)
                n_slot, n_max = 0, 0
                for what in plan(prev, do_s, do_t, last):
                    if what[0] not in ("S", "Y", "M"):
                        continue
                    here = (slot + n_slot) % 2
                    if what[0] == "S":
                        t, heads = SUNITS[what[1]]
                        w = (t + 1) * P
                        pitch = s_offset(t, 1)
                        src = ps_slot[:, here, 0:pitch * len(heads)].rearrange("p (g w) -> p g w", w=pitch)[:, :, 0:w] \
                            if len(heads) > 1 else ps_slot[:, here, 0:w]
                        dve.wait_ge(slot_full, k + n_slot + 1)
                        dve.tensor_reduce(neg_max[:, heads[0]:heads[-1] + 1, t], src, AX.X, ALU.max,
                                          negate=True).then_inc(slot_used, 1)
                        n_max += 1
                        if n_max == len(SUNITS):
                            flat = neg_max[:, :, :].rearrange("p g t -> p (g t)")
                            dve.wait_ge(slot_used, k + n_slot + 1)
                            dve.tensor_copy(max_parts[:, 0, :], flat).then_inc(msplit, 1)
                            dve.wait_ge(msplit, 4 * s + 1)
                            dve.tensor_tensor(max_rest[:, :], flat, max_parts[:, 0, :], ALU.subtract).then_inc(msplit, 1)
                            dve.wait_ge(msplit, 4 * s + 2)
                            dve.tensor_copy(max_parts[:, 1, :], max_rest[:, :]).then_inc(msplit, 1)
                            dve.wait_ge(msplit, 4 * s + 3)
                            dve.tensor_tensor(max_parts[:, 2, :], max_rest[:, :], max_parts[:, 1, :],
                                              ALU.subtract).then_inc(msplit, 1)
                    elif what[0] == "M":
                        dve.wait_ge(slot_full, k + n_slot + 1)
                        if positive(16 * s):
                            dve.wait_ge(mrows_in, 16 * s)
                        dve.tensor_copy(max_rows[:, :], ps_slot[0:3 * HG * TPB, here, 0:P // 2].bitcast(BF16))\
                           .then_inc(mrows_sb, 1)
                        dve.wait_ge(mrows_sb, s + 1)
                        dve.sem_inc(slot_used, 1)
                    else:
                        qb, back = what[1:]
                        n = s - 1 + back
                        src = ps_slot[:, here, 0:512].rearrange("p (t g c) -> p t g c", t=CH, g=HG)
                        dve.wait_ge(slot_full, k + n_slot + 1)
                        dve.reciprocal(y_rcp[:, qb, :, :], src[:, :, :, D]).then_inc(y_rcp_done, 1)
                        dve.wait_ge(y_rcp_done, 2 * n + qb + 1)
                        hg = n % (H // HG)
                        dst = y_all[:, bass.ds((n // (H // HG)) * TPB + CH * qb, CH), bass.ds(hg, 1), :]
                        rc = y_rcp[:, qb, :, :].rearrange("p t (g a) -> p t g a", a=1)
                        rc = bass.AP(tensor=rc.tensor, offset=rc.offset, ap=[list(a) for a in rc.ap[:-1]] + [[0, D]])
                        dve.tensor_tensor(dst.rearrange("p t a (g d) -> p t (a g) d", g=HG), src[:, :, :, 0:D], rc,
                                          ALU.mult).then_inc(slot_used, 1)
                    n_slot += 1

            dve.wait_ge(xb_done, TT)
            step(0, 0, 0, prev=False, do_t=False)
            step(1, 1, 0, prev=False)
            with dve.Fori(0, 2) as i:
                for a in step_args(i):
                    step(*a)
            step(NG, NG % NBUF, 0, do_s=False, last=True)

            dve.wait_ge(stack_in[NG % NBUF], 96 * (NG // NBUF + 1))
            def wide_col(a, n):
                return bass.AP(tensor=a.tensor, offset=a.offset, ap=[list(d) for d in a.ap[:-1]] + [[0, n]])

            dve.memset(f_act[0][F4:P, :], 0.0).then_inc(fw_done, 1)
            dve.memset(f_act[1][F4:P, :], 0.0).then_inc(fw_done, 1)
            after(dve.memset(fw[F4:P, 2 * F4:2 * F4 + C], 0.0))
            dve.wait_ge(fw_in, 48)
            dve.tensor_scalar(fw[:, 0:2 * F4], fw[:, 0:2 * F4], fn_col[:, 0:1], None, ALU.mult).then_inc(fw_done, 1)
            RATIO, RINV, RMS, W1, W2, KEEP, S1, OVF, IDX1, IDX2, POS1, POS2, O1, O2, SUM, RS = range(16)
            EXPS, ONE1, ONE2, LG = 16, 25, 33, 41

            for c in range(NCH):
                dve.wait_ge(pr_ps, c + 1)
                dve.tensor_tensor(x1[:, c * CH:(c + 1) * CH, :],
                                  ps_slot[:, c % 2, 512:1024].rearrange("p (t c) -> p t c", t=CH),
                                  x_sb[:, c * CH:(c + 1) * CH, :], ALU.add).then_inc(x1_done, 1)
                dve.wait_ge(x1_done, c + 1)
                norm_stats(x1, c, NCH + c)
                r = slice(c * CH, (c + 1) * CH)
                var = mv[:, r, 1]
                after(dve.tensor_tensor(small[:, RINV * TT:(RINV + 1) * TT][:, r], rstd[:, r], rstd[:, r], ALU.mult))
                after(dve.tensor_tensor(small[:, RATIO * TT:(RATIO + 1) * TT][:, r],
                                        small[:, RINV * TT:(RINV + 1) * TT][:, r], var, ALU.mult))
                rsqrt(small[:, RMS * TT:(RMS + 1) * TT][:, r], small[:, RATIO * TT:(RATIO + 1) * TT][:, r], RMS_EPS)
                dve.tensor_tensor(small[:, RINV * TT:(RINV + 1) * TT][:, r], newton[:, 0:CH],
                                  small[:, RMS * TT:(RMS + 1) * TT][:, r], ALU.mult)
                after(dve.tensor_tensor(small[:, SUM * TT:(SUM + 1) * TT][:, r], rstd[:, r],
                                        small[:, RMS * TT:(RMS + 1) * TT][:, r], ALU.mult))
                for t in range(CH):
                    tile = c * CH + t
                    dve.tensor_scalar(u_rows[:, tile, 0:C], x1[:, tile, :], mv[:, tile, 0:1],
                                      small[:, SUM * TT + tile:SUM * TT + tile + 1],
                                      ALU.subtract, ALU.mult).then_inc(u_done, 1)

            def arr(i):
                return small[:, i * TT:(i + 1) * TT]

            def arr3(i):
                return small[:, i * TT:(i + 1) * TT].rearrange("p (t a) -> p t a", a=1)

            def arr8(i):
                return col(i, 8)

            dve.wait_ge(lg_ps, NCH)
            after(dve.tensor_tensor(arr8(LG), ps_st[:, 1, 0:TT * E_NUM].rearrange("p (t e) -> p t e", e=E_NUM),
                                    wide_col(arr3(RINV), E_NUM), ALU.mult))
            for t in range(TT):
                ins = dve.max(mx8[:, t, :], arr8(LG)[:, t, :])
            after(ins)
            for t in range(TT):
                ins = dve.max_index(ix8[:, t, :], mx8[:, t, :], arr8(LG)[:, t, :])
            ex = col(EXPS, 9)
            dve.tensor_tensor(ex[:, :, 0:8], arr8(LG), wide_col(mx8[:, :, 0:1], E_NUM), ALU.subtract)
            after(dve.tensor_tensor(ex[:, :, 8:9], mx8[:, :, 1:2], mx8[:, :, 0:1], ALU.subtract))
            dve.sem_inc(ex_ready, 1)
            dve.tensor_copy(arr3(IDX1), ix8[:, :, 0:1])
            after(dve.tensor_copy(arr3(IDX2), ix8[:, :, 1:2]))
            eno = bass.AP(tensor=expert_no.tensor, offset=expert_no.offset,
                          ap=[list(expert_no.ap[0]), [0, TT], [1, E_NUM]])
            dve.tensor_tensor(arr8(ONE1), wide_col(arr3(IDX1), E_NUM), eno, ALU.is_equal)
            after(dve.tensor_tensor(arr8(ONE2), wide_col(arr3(IDX2), E_NUM), eno, ALU.is_equal))
            dve.tensor_tensor(sel_b[:, :], small[:, ONE1 * TT:(ONE1 + 8) * TT], small[:, ONE2 * TT:(ONE2 + 8) * TT],
                              ALU.add).then_inc(sel_done, 1)
            dve.wait_ge(ex_done, 1)
            after(dve.tensor_reduce(arr(SUM), ex[:, :, 0:8], AX.X, ALU.add))
            after(dve.reciprocal(arr(W1), arr(SUM)))
            after(dve.tensor_tensor(arr3(W2), ex[:, :, 8:9], arr3(W1), ALU.mult))

            def fallback_act(c):
                dve.wait_ge(f_gelu, c + 1)
                if c >= 2:
                    dve.wait_ge(f_ps, c - 1)
                dve.tensor_tensor(f_act[c % 2][0:F4, :], tmp_g[0:F4, c % 2, :], ps_av[0:F4, :], ALU.mult)\
                   .then_inc(f_act_done, 1)

            dve.wait_ge(pos_ps, 1)
            pos = ps_st[:, 1, 256:384].rearrange("p (t e) -> p t e", e=E_NUM)
            dve.tensor_tensor(arr8(ONE1), arr8(ONE1), pos, ALU.mult)
            after(dve.tensor_tensor(arr8(ONE2), arr8(ONE2), pos, ALU.mult))
            dve.tensor_reduce(arr(POS1), arr8(ONE1), AX.X, ALU.add)
            after(dve.tensor_reduce(arr(POS2), arr8(ONE2), AX.X, ALU.add))
            dve.tensor_scalar(arr(O1), arr(POS1), float(CAP), None, ALU.is_ge)
            after(dve.tensor_scalar(arr(O2), arr(POS2), float(CAP), None, ALU.is_ge))
            after(dve.tensor_tensor(arr(OVF), arr(O1), arr(O2), ALU.max))
            after(dve.tensor_scalar(arr(KEEP), arr(OVF), -1.0, 1.0, ALU.mult, ALU.add))
            urow = u_rows
            dve.tensor_tensor(urow[:, :, C:C + 1], arr3(W1), arr3(KEEP), ALU.mult)
            after(dve.tensor_tensor(urow[:, :, C + 1:C + 2], arr3(W2), arr3(KEEP), ALU.mult))
            dve.tensor_copy(urow[:, :, C + 2:C + 3], arr3(IDX1))
            dve.tensor_copy(urow[:, :, C + 3:C + 4], token_no.rearrange("p (t a) -> p t a", a=1))
            for pos_i, idx_i, o_i in ((POS1, IDX1, O1), (POS2, IDX2, O2)):
                after(dve.scalar_tensor_tensor(out=arr(pos_i), in0=arr(idx_i), scalar=float(CAP), in1=arr(pos_i),
                                               op0=ALU.mult, op1=ALU.add))
                after(dve.scalar_tensor_tensor(out=arr(pos_i), in0=arr(o_i), scalar=FAR, in1=arr(pos_i),
                                               op0=ALU.mult, op1=ALU.add))
            dve.tensor_copy(slot_no[:, 0, :], arr(POS1))
            after(dve.tensor_copy(slot_no[:, 1, :], arr(POS2)))
            dve.sem_inc(rows_ready, 1)
            for c in range(NCH):
                fallback_act(c)
            after(dve.tensor_tensor(arr3(S1), urow[:, :, C:C + 1], urow[:, :, C + 1:C + 2], ALU.add))
            after(dve.tensor_scalar(arr(S1), arr(S1), 1.0, None, ALU.add))
            after(dve.tensor_tensor(arr(S1), arr(S1), arr(RINV), ALU.mult))
            for t in range(TT):
                dve.scalar_tensor_tensor(out=x1[:, t, :], in0=urow[:, t, 0:C], scalar=arr(S1)[:, t:t + 1],
                                         in1=x1[:, t, :], op0=ALU.mult, op1=ALU.add).then_inc(base1, 1)
            dve.wait_ge(f_ps, NCH)
            for t in range(TT):
                dve.wait_ge(base1, t + 1)
                dve.scalar_tensor_tensor(out=x1[:, t, :], in0=ps_slot[:, t // 8, (t % 8) * C:(t % 8 + 1) * C],
                                         scalar=arr(OVF)[:, t:t + 1], in1=x1[:, t, :], op0=ALU.mult,
                                         op1=ALU.add).then_inc(base_done, 1)

            def fold_norm(e, i, n):
                dve.wait_ge(ew_in[i], 48 * (n + 1))
                for half in range(2):
                    dve.tensor_scalar(wgu[i][:, half * FF:(half + 1) * FF], wgu[i][:, half * FF:(half + 1) * FF],
                                      e_norm[:, bass.ds(e, 1)], None, ALU.mult).then_inc(ew_done, 1)

            def weights_of_rows(e, i, n):
                dve.wait_ge(es_in[i], 16 * (n + 1))
                if positive(e - 1):
                    dve.wait_ge(added, 64 * (e - 1))
                a1, a2 = slot_in[i][:, :, C], slot_in[i][:, :, C + 1]
                dve.tensor_copy(e_tok[:, i, :], slot_in[i][:, :, C + 3]).then_inc(ewt, 1)
                dve.tensor_scalar(e_wt[:, i, 0, :], slot_in[i][:, :, C + 2], expert_no[:, bass.ds(e, 1)], None,
                                  ALU.is_equal).then_inc(ewt, 1)
                dve.tensor_tensor(e_wt[:, i, 1, :], a1, a2, ALU.subtract).then_inc(ewt, 1)
                dve.wait_ge(ewt, 3 * e + 3)
                dve.tensor_tensor(e_wt[:, i, 2, :], e_wt[:, i, 0, :], e_wt[:, i, 1, :], ALU.mult).then_inc(ewt_done, 1)
                dve.wait_ge(ewt_done, 2 * e + 1)
                dve.tensor_tensor(e_wt[:, i, 2, :], e_wt[:, i, 2, :], a2, ALU.add).then_inc(ewt_done, 1)
                dve.wait_ge(ewt_done, 2 * e + 2)

            def gate(e, i):
                for c in range(2):
                    dve.wait_ge(e_gelu, 2 * e + c + 1)
                    up = ps_st[:, 2, :] if c == 0 else ps_av[:, :]
                    dve.tensor_tensor(gated[i][:, c, :], tmp_g[:, c, :], up, ALU.mult).then_inc(e_gated, 1)

            def scale_rows(e, i):
                dve.wait_ge(eo_ps, e + 1)
                for j in range(4):
                    dve.tensor_scalar(e_out[i][:, j, :], ps_slot[:, 1, j * C:(j + 1) * C], e_wt[:, i, 2, j:j + 1], None,
                                      ALU.mult).then_inc(eo_done, 1)

            fold_norm(0, 0, 0)
            fold_norm(1, 1, 0)
            weights_of_rows(0, 0, 0)
            gate(0, 0)
            with dve.Fori(0, E_NUM // 2 - 1) as k:
                weights_of_rows(2 * k + 1, 1, k)
                gate(2 * k + 1, 1)
                scale_rows(2 * k, 0)
                fold_norm(2 * k + 2, 0, k + 1)
                weights_of_rows(2 * k + 2, 0, k + 1)
                gate(2 * k + 2, 0)
                scale_rows(2 * k + 1, 1)
                fold_norm(2 * k + 3, 1, k + 1)
            weights_of_rows(E_NUM - 1, 1, E_NUM // 2 - 1)
            gate(E_NUM - 1, 1)
            scale_rows(E_NUM - 2, 0)
            scale_rows(E_NUM - 1, 1)


def shape_constants():
    import math

    import numpy as np

    inv = (1.0 / np.float32(10000.0) ** (np.arange(0, D, 2, dtype=np.float32) / np.float32(D))).astype(np.float32)
    ang = np.arange(T, dtype=np.float32)[None, :] * inv[:, None]
    d_of = (np.arange(P) % (HG * D)) // HG
    ang = ang[d_of % (D // 2)]
    sign = np.where(d_of < D // 2, -1.0, 1.0)[:, None]
    k, m = np.arange(P)[:, None], np.arange(P)[None, :]
    head = m // (HG * D) * HG + m % HG
    d_m = (m % (HG * D)) // HG
    plain, swap = k == head * D + d_m, k == head * D + (d_m + D // 2) % D
    wide = np.concatenate([np.cos(ang), np.sin(ang) * sign, k == m, k < m, plain, swap,
                           np.broadcast_to(np.arange(E_NUM), (P, E_NUM)),
                           np.arange(TT)[None, :] * P + k], axis=1).astype(np.float32)

    def bucket(n):
        big = 16 + int(math.log(max(n, 1) / 16) / math.log(8) * 16) if n >= 16 else n
        return min(big, NB - 1)

    onehot = np.zeros((NB, 2, NV), np.float32)
    mask = np.zeros((H, 2, NV), np.float32)
    for y in range(NV):
        for v, n in ((0, y - (P - 1)), (1, 2 * P - 1 - y)):
            if n >= 0:
                onehot[bucket(n), v, y] += 1
                onehot[NB - 1, v, y] -= 1
                mask[:, v, y] = 1 - v
            else:
                mask[:, v, y] = -1e30 * v
    rows = np.zeros((CAP, ROW), np.float32)
    rows[:, C + 2] = -1
    rows[:, C + 3] = B * T + np.arange(CAP)
    return {"c_wide": wide, "c_onehot": onehot.reshape(NB, 2 * NV), "c_mask": mask, "c_rows": rows}


_INS = ["L0_attn_x", "L0_attn_Wq", "L0_attn_bq", "L0_attn_Wk", "L0_attn_bk", "L0_attn_Wv", "L0_attn_bv",
        "L0_attn_Wp", "L0_attn_bp", "L0_attn_rel_bias_table", "L0_ffn_Wr", "L0_ffn_norm_w", "L0_ffn_Wg",
        "L0_ffn_Wu", "L0_ffn_Wd", "L0_ffn_f_norm", "L0_ffn_fWg", "L0_ffn_fWu", "L0_ffn_fWd"]


def kernel(**inputs):
    import numpy as _np
    import concourse.bacc as _bacc
    from concourse import mybir as _mybir
    from concourse.bass_utils import run_bass_kernel_spmd as _run

    nc = _bacc.Bacc("TRN2", target_bir_lowering=False, num_devices=1)
    arrays, args = {}, []
    for name, a in [(n, inputs[n]) for n in _INS] + list(shape_constants().items()):
        a = _np.ascontiguousarray(a)
        arrays[f"in_{name}_dram"] = a
        args.append(nc.dram_tensor(f"in_{name}_dram", a.shape, _mybir.dt.from_np(a.dtype), kind="ExternalInput").ap())
    args.append(nc.dram_tensor("out_0_dram", (B * T + CAP, C), _mybir.dt.float32, kind="ExternalOutput").ap())
    layer_kernel(nc, *args)
    r = _run(nc, [arrays], core_ids=[0])
    return r.results[0]["out_0_dram"][0:B * T].reshape(B, T, C)
```

```python
from contextlib import ExitStack

import concourse.bass as bass
from concourse import mybir

F32 = mybir.dt.float32
BF16 = mybir.dt.bfloat16
U32 = mybir.dt.uint32
I32 = mybir.dt.int32
ALU = mybir.AluOpType
ACT = mybir.ActivationFunctionType
AX = mybir.AxisListType

P = 128
B, T, C = 2, 1024, 128
H, D = 16, 8
TPB = T // P
TT = B * TPB
HG = 4
NG = B * H // HG
CH = 4
NCH = TT // CH
CW = CH * P
NB = 32
NV = 3 * P
QK_ROWS = 9 * D
M_ROW = QK_ROWS
ST_ROWS = M_ROW + 3
VW = 32
E_NUM, FF, F4, CAP = 8, 256, 64, 512
NBUF = 3
PBUF = 4
ROW = C + 4
SCALE = float(D) ** -0.5
LN_EPS, RMS_EPS = 1e-5, 1e-6
FAR = 1.0e6
BIG = 3.0e38

UNITS = [(0, 0), (0, 1), (0, 2), (0, 3), (1, 0), (1, 4), (1, 1), (1, 5), (1, 2), (1, 6), (1, 3), (1, 7)]
NU = len(UNITS)
SUNITS = [(0, (0, 1, 2, 3))] + [(t, hs) for t in (1, 2, 3) for hs in ((0, 1), (2, 3))] \
    + [(t, (g,)) for t in (4, 5, 6, 7) for g in range(HG)]
S_HEAD, S_SPAN = 2, 0.85


def first_col(qb, kt):
    return max(0, kt - CH * qb) * P


def near(qb, kt):
    lo, hi = max(kt, CH * qb), min(kt + 2, CH * qb + CH)
    return (lo - CH * qb) * P, (hi - CH * qb) * P, (lo - kt) * P


NEAR = [n for n, u in enumerate(UNITS) if near(*u)[0] < near(*u)[1]]
NN = len(NEAR)


def s_offset(t, k):
    return k * (t + 1) * P if t < 2 else k * 512


def token_plan(b):
    c = 2 * b
    return [("A", c), ("A", c + 1), ("B", c), ("B", c + 1), ("C", c), ("C", c + 1), ("D", b), ("X", b), ("E", b)]


TOKENS_AT = {1: token_plan(0)[0:2], 3: token_plan(0)[2:4], 6: token_plan(0)[4:6], 8: token_plan(0)[6:7],
             10: token_plan(0)[7:8], 11: token_plan(0)[8:9]}


def exp_plan(prev, last):
    out = []
    for u in range(NU):
        w = 512 - first_col(*UNITS[u])
        if u == 0 and prev:
            out.append((("AV", NU - 2, -1), 256))
        out += [(("ST", u, g), w) for g in range(HG)]
        if u == 1 and prev:
            out += [(("AV", NU - 1, -1), 256), (("EVAC", 1, -1), 0)]
        if u >= 2:
            out.append((("AV", u - 2, 0), 2 * (512 - first_col(*UNITS[u - 2]))))
        if u == 5:
            out.append((("EVAC", 0, 0), 0))
        if u == 2 and prev:
            out.append((("Y", 1, -1), 256))
        if u == 7:
            out.append((("Y", 0, 0), 256))
        if last:
            out += [(item, 256) for item in TOKENS_AT.get(u, ())]
    if last:
        out += [(("AV", NU - 2, 0), 0), (("AV", NU - 1, 0), 0), (("EVAC", 1, 0), 0), (("Y", 1, 0), 0)]
    return out


def s_columns(su):
    t, heads = SUNITS[su]
    return len(heads) * (t + 1) * P


def plan(prev, do_s, do_t, last):
    work = exp_plan(prev, last) if do_t else []
    out, su, at, done = [], 0, 0, 0
    total = max(1, sum(w for _, w in work))
    s_rest = sum(s_columns(k) for k in range(S_HEAD, len(SUNITS)))
    turned = not do_s
    for item, w in work + [(None, 0)]:
        while do_s and su < len(SUNITS) and (item is None or su < S_HEAD or done / s_rest * S_SPAN <= at / total):
            out.append(("S", su))
            if su >= S_HEAD:
                done += s_columns(su)
            su += 1
        if not turned and (item is None or (su == len(SUNITS) and at / total > S_SPAN + 0.08)):
            out.append(("M",))
            turned = True
        if item:
            out.append(item)
            at += w
    return out


def positive(v):
    return not isinstance(v, int) or v > 0


def layer_kernel(nc, x, Wq, bq, Wk, bk, Wv, bv, Wp, bp, table, Wr, norm_w, Wg, Wu, Wd, f_norm,
                 fWg, fWu, fWd, c_wide, c_onehot, c_mask, c_rows, c_ones, out):
    ctx = ExitStack()
    with ctx:
        def sb(name, shape, dt=F32):
            return ctx.enter_context(nc.sbuf_tensor(name, shape, dt))

        def sem(name):
            return ctx.enter_context(nc.semaphore(name))

        q_parts = nc.dram_tensor("q_parts", [NG, 3, D, HG * T], BF16, kind="Internal")
        k_parts = nc.dram_tensor("k_parts", [NG, 3, D, HG * T], BF16, kind="Internal")
        g_vec = nc.dram_tensor("g_vec", [H, P, NV], F32, kind="Internal")
        r_vec = nc.dram_tensor("r_vec", [H, P, NV], BF16, kind="Internal")
        slots = nc.dram_tensor("slots", [E_NUM * CAP, ROW], F32, kind="Internal")

        ps_slot = ctx.enter_context(nc.psum_tensor("ps_slot", [P, 2, 1024], F32))
        ps_st = ctx.enter_context(nc.psum_tensor("ps_st", [P, 3, 512], F32))
        ps_av = ctx.enter_context(nc.psum_tensor("ps_av", [P, 512], F32))

        wide = sb("wide", [P, 2 * T + 4 * P + E_NUM + TT])
        cos_t, sin_t = wide[:, 0:T], wide[:, T:2 * T]
        ident = wide[:, 2 * T:2 * T + P]
        below = wide[:, 2 * T + P:2 * T + 2 * P]
        swap = wide[:, 2 * T + 2 * P:2 * T + 4 * P]
        expert_no = wide[:, 2 * T + 4 * P:2 * T + 4 * P + E_NUM]
        token_no = wide[:, 2 * T + 4 * P + E_NUM:2 * T + 4 * P + E_NUM + TT]
        onehot = sb("onehot", [NB, 2 * NV])
        vmask = sb("vmask", [H, 2, NV])
        tab = sb("tab", [NB, H])
        ident_b = sb("ident_b", [P, P], BF16)
        below_b = sb("below_b", [P, P], BF16)
        ones_b = sb("ones_b", [P, P], BF16)
        x_sb = sb("x_sb", [P, TT, C])
        w_attn = sb("w_attn", [P, 8, C])
        bcol = sb("bcol", [P, 2])
        bcol_perm = sb("bcol_perm", [P, 4])
        bv_row = sb("bv_row", [P, C])
        bp_row = sb("bp_row", [P, C])
        stats = sb("stats", [P, TT, 6])
        mv = sb("mv", [P, TT, 2])
        rstd = sb("rstd", [P, TT])
        newton = sb("newton", [P, 2, TT])
        q_stack = sb("q_stack", [P, NBUF, HG, T], BF16)
        k_stack = sb("k_stack", [P, NBUF, HG, T], BF16)
        v_all = sb("v_all", [P, NG, TPB * HG * D])
        v_grp = sb("v_grp", [P, NBUF, TPB, HG, VW])
        f_all = sb("f_all", [P, H * 2 * P])
        b_all = sb("b_all", [P, H * 2 * P], BF16)
        f_grp = sb("f_grp", [P, NBUF, HG, 2 * P])
        b_grp = sb("b_grp", [P, NBUF, HG, 2 * P], BF16)
        probs = sb("probs", [P, PBUF, HG, 512])
        neg_max = sb("neg_max", [P, HG, TPB])
        max_rest = sb("max_rest", [P, HG * TPB])
        max_parts = sb("max_parts", [P, 3, HG * TPB], BF16)
        max_rows = sb("max_rows", [3 * HG * TPB, P], BF16)
        y_raw = sb("y_raw", [P, 2, 512])
        y_rcp = sb("y_rcp", [P, 2, CH, HG])
        y_all = sb("y_all", [P, TT, H // HG, HG * D])

        pro = probs[:, :, :, :].rearrange("p a b c -> p (a b c)")
        xn = [pro[:, i * CW:(i + 1) * CW].rearrange("p (t c) -> p t c", t=CH) for i in range(2)]
        xnT = [pro[:, CW * (2 + i):CW * (3 + i)] for i in range(2)]
        rope_a, rope_b = pro[:, 4 * CW:5 * CW], pro[:, 5 * CW:6 * CW]
        qk_f = [pro[:, (6 + i) * CW:(7 + i) * CW] for i in range(2)]
        qk_rest = [pro[:, (8 + i) * CW:(9 + i) * CW] for i in range(2)]
        w = 3 * CW // 2
        part_f = [[pro[:, 10 * CW + (2 * i + j) * w:10 * CW + (2 * i + j + 1) * w].bitcast(BF16)
                   .rearrange("p (a n) -> p a n", n=CW) for j in range(2)] for i in range(2)]
        g_sb = y_raw[0:H, 0, 0:NV]
        r_sb = y_raw[0:H, 1, 0:NV // 2].bitcast(BF16)

        uT = wide[:, 0:TT * P]
        u_rows = f_all[:, 0:TT * ROW].rearrange("p (t c) -> p t c", c=ROW)
        small = f_all[:, TT * ROW:TT * ROW + 57 * TT]
        v_flat = v_all[:, :, :].rearrange("p a b -> p (a b)")
        yT = [v_flat[:, i * CW:(i + 1) * CW] for i in range(2)]
        f_act = [v_flat[:, (2 + i) * CW:(3 + i) * CW] for i in range(2)]
        x1 = x_sb

        def stack_floats(st, buf, n):
            return st[:, buf, :, :].rearrange("p g t -> p (g t)").bitcast(F32).rearrange("p (e f) -> p e f", e=n)

        wg_all, wu_all = stack_floats(q_stack, 2, E_NUM), stack_floats(k_stack, 2, E_NUM)
        wd_all = stack_floats(k_stack, 0, 2 * E_NUM)

        def col(i, n=1):
            return small[:, i * TT:(i + n) * TT].rearrange("p (t k) -> p t k", k=n)

        wgu = [pro[:, i * 512:(i + 1) * 512] for i in range(2)]
        e0 = 1024
        slot_in = [pro[:, e0 + i * 4 * ROW:e0 + (i + 1) * 4 * ROW].rearrange("p (j c) -> p j c", c=ROW) for i in range(2)]
        e1 = e0 + 8 * ROW
        slotT = [pro[:, e1 + i * 512:e1 + (i + 1) * 512] for i in range(2)]
        e2 = e1 + 1024
        gated = [pro[:, e2 + i * 1024:e2 + (i + 1) * 1024].rearrange("p (c n) -> p c n", c=2) for i in range(2)]
        e3 = e2 + 2048
        e_out = [pro[:, e3 + i * 512:e3 + (i + 1) * 512].rearrange("p (j c) -> p j c", c=C) for i in range(2)]
        tmp_g = y_raw[:, :, :]
        fw = sb("fw", [P, 2 * F4 + C])
        router = sb("router", [P, E_NUM])
        e_norm = sb("e_norm", [P, E_NUM])
        e_wt = sb("e_wt", [P, 2, 3, 4])
        e_tok = sb("e_tok", [P, 2, 4], U32)
        fn_col = sb("fn_col", [P, 1])
        slot_no = sb("slot_no", [P, 2, TT], U32)
        mx8 = sb("mx8", [P, TT, 8])
        ix8 = sb("ix8", [P, TT, 8], U32)
        sel_b = sb("sel_b", [P, TT * E_NUM], BF16)

        x_in = [sem(f"x_in{i}") for i in range(NCH)]
        w_in = sem("w_in")
        c_in = sem("c_in")
        t_in = sem("t_in")
        rope_in = sem("rope_in")
        ones_in = sem("ones_in")
        late_in = sem("late_in")
        const_b = sem("const_b")
        swapped = sem("swapped")
        zeroed = sem("zeroed")
        fixed = sem("fixed")
        st_done = sem("st_done")
        mv_done = sem("mv_done")
        xn_done = sem("xn_done")
        xnT_ps = sem("xnT_ps")
        xnT_sb = sem("xnT_sb")
        qk_ps = sem("qk_ps")
        rope_half = sem("rope_half")
        rope_done = sem("rope_done")
        part_hi = sem("part_hi")
        rest_done = sem("rest_done")
        part_mid = sem("part_mid")
        part_lo = sem("part_lo")
        parts_out = [[sem(f"parts_out{i}{j}") for j in range(2)] for i in range(2)]
        v_ps = sem("v_ps")
        v_done = sem("v_done")
        bswap_ps = sem("bswap_ps")
        bswap_sb = sem("bswap_sb")
        vec_ps = sem("vec_ps")
        vec_exp = sem("vec_exp")
        vec_done = sem("vec_done")
        vec_out = sem("vec_out")
        toep_in = sem("toep_in")
        xb_done = sem("xb_done")
        stack_in = [sem(f"stack_in{i}") for i in range(NBUF)]
        slot_full = sem("slot_full")
        slot_used = sem("slot_used")
        scores = sem("scores")
        exp_done = sem("exp_done")
        near_done = sem("near_done")
        av_done = sem("av_done")
        y_evac = sem("y_evac")
        y_rcp_done = sem("y_rcp_done")
        max_done = sem("max_done")
        msplit = sem("msplit")
        mrows_sb = sem("mrows_sb")
        mrows_in = sem("mrows_in")
        masked = sem("masked")
        v_copied = sem("v_copied")
        ln2 = sem("ln2")
        u_done = sem("u_done")
        in_order = sem("in_order")
        ex_ready = sem("ex_ready")
        ex_done = sem("ex_done")
        sel_done = sem("sel_done")
        rows_ready = sem("rows_ready")
        fw_in = sem("fw_in")
        fw_done = sem("fw_done")
        fgu_ps = sem("fgu_ps")
        f_gelu = sem("f_gelu")
        f_act_done = sem("f_act_done")
        f_ps = sem("f_ps")
        base1 = sem("base1")
        base_done = sem("base_done")
        init_out = sem("init_out")
        trash_out = sem("trash_out")
        dispatched = sem("dispatched")
        base_out = sem("base_out")
        ew_in = sem("ew_in")
        es_in = [sem(f"es_in{i}") for i in range(2)]
        ew_done = sem("ew_done")
        eT_ps = sem("eT_ps")
        eT_sb = sem("eT_sb")
        gu_ps = sem("gu_ps")
        e_gelu = sem("e_gelu")
        e_gated = sem("e_gated")
        eo_ps = sem("eo_ps")
        ewt = sem("ewt")
        ewt_done = sem("ewt_done")
        eo_done = sem("eo_done")
        added = sem("added")
        tile_seen = sem("tile_seen")
        stack_free = sem("stack_free")
        add_turn = sem("add_turn")
        slots_free = sem("slots_free")

        x_tiles = x.rearrange("b (t p) c -> p (b t) c", p=P)
        out_tiles = out[0:B * T, :].rearrange("(t p) c -> p t c", p=P)

        block = ctx.enter_context(nc.Block())

        def step_args(i):
            return [(2 + 3 * i + j, (2 + j) % NBUF, i + (2 + j) // NBUF) for j in range(3)]

        def slot_base(s):
            if isinstance(s, int) and s < 2:
                return 24 * s
            return 26 * s - 3

        def base_parity(s):
            return slot_base(s) % 2 if isinstance(s, int) else 1

        @block.sync
        def _(sp):
            sp.dma_start(x_sb[:, 0:CH, :], x_tiles[:, 0:CH, :]).then_inc(x_in[0], 16)
            for i, w in enumerate((Wq, Wk, Wv, Wp)):
                sp.dma_start(w_attn[:, i, :], w[:, :]).then_inc(w_in, 16)
            for c in range(1, NCH):
                sp.dma_start(x_sb[:, c * CH:(c + 1) * CH, :], x_tiles[:, c * CH:(c + 1) * CH, :]).then_inc(x_in[c], 16)
            sp.dma_start(k_stack[M_ROW:M_ROW + 3, :, :, :].rearrange("p a b c -> p (a b c)").bitcast(F32),
                         c_ones[:, :]).then_inc(ones_in, 16)

            def store_parts(c):
                for i, dst in enumerate((q_parts, k_parts)):
                    sp.wait_ge(part_lo, 2 * c + i + 1)
                    for a in range(3):
                        n0, tok = (c // 2) * 4, (c % 2) * CW
                        ap = bass.AP(tensor=dst, offset=(n0 * 3 + a) * HG * D * T + tok,
                                     ap=[[3 * HG * D * T, 4], [T, HG * D], [1, CW]])
                        sp.dma_start(ap, part_f[i][c % 2][:, a, :]).then_inc(parts_out[i][c % 2], 16)

            sp.dma_start(bp_row[:, :], bass.AP(tensor=bp.tensor, offset=0, ap=[[0, P], [1, C]])).then_inc(late_in, 16)
            sp.dma_start(e_norm[:, :], norm_w.rearrange("e h -> h e"), allow_slow_non_contiguous=True).then_inc(late_in, 16)
            sp.dma_start(router[:, :], Wr[:, :]).then_inc(late_in, 16)
            sp.dma_start(fn_col[:, :], f_norm.rearrange("(p a) -> p a", a=1)).then_inc(late_in, 16)
            sp.dma_start(fw[:, 0:F4], fWg[:, :]).then_inc(fw_in, 16)
            sp.dma_start(fw[:, F4:2 * F4], fWu[:, :]).then_inc(fw_in, 16)
            sp.dma_start(fw[0:F4, 2 * F4:2 * F4 + C], fWd[:, :]).then_inc(fw_in, 16)
            sp.wait_ge(vec_done, 2)
            for dst, vec in ((r_vec, r_sb), (g_vec, g_sb)):
                src = bass.AP(tensor=vec.tensor, offset=vec.offset, ap=[list(vec.ap[0]), [0, P], [1, NV]])
                sp.dma_start(dst[:, :, :], src).then_inc(vec_out, 16)
            store_parts(0)
            sp.wait_ge(vec_out, 32)
            for dst, vec in ((b_all, r_vec), (f_all, g_vec)):
                src = bass.AP(tensor=vec, offset=P - 1, ap=[[NV - 1, P], [P * NV, H], [1, 2 * P]])
                sp.dma_start(dst[:, :].rearrange("p (h c) -> p h c", h=H), src).then_inc(toep_in, 16)
            store_parts(1)

            def load_stack(n, buf):
                for a in range(3):
                    sp.dma_start(q_stack[24 * a:24 * a + 24, buf, :, :].rearrange("p g t -> p (g t)"),
                                 bass.AP(tensor=q_parts, offset=n * (3 * HG * D * T) + a * (HG * D * T),
                                         ap=[[0, 3], [HG * T, D], [1, HG * T]])).then_inc(stack_in[buf], 16)
                sp.dma_start(k_stack[0:QK_ROWS, buf, :, :].rearrange("p g t -> p (g t)"),
                             bass.AP(tensor=k_parts, offset=n * (3 * HG * D * T),
                                     ap=[[0, 3], [HG * T, 3 * D], [1, HG * T]])).then_inc(stack_in[buf], 16)
                w = HG * 2 * P
                for dst, src in ((b_grp, b_all), (f_grp, f_all)):
                    sp.dma_start(dst[:, buf, :, :].rearrange("p g c -> p (g c)"),
                                 src[:, bass.ds((n % (H // HG)) * w, w)]).then_inc(stack_in[buf], 16)

            for i in range(2):
                for j in range(2):
                    sp.wait_ge(parts_out[i][j], 1 * 48)
            sp.wait_ge(toep_in, 32)
            load_stack(0, 0)
            load_stack(1, 1)
            store_parts(2)
            store_parts(3)
            for e in range(E_NUM):
                sp.dma_start(slots[e * CAP:(e + 1) * CAP, :], c_rows[:, :]).then_inc(init_out, 16)
            sp.dma_start(out[B * T:B * T + CAP, :], c_rows[:, 0:C]).then_inc(trash_out, 16)
            for i in range(2):
                for j in range(2):
                    sp.wait_ge(parts_out[i][j], 2 * 48)

            def step(s, buf, fill, more=True):
                if more:
                    if positive(48 * (s - 1)):
                        sp.wait_ge(near_done, NN * (s - 1))
                        sp.sem_inc(stack_free, 1)
                    load_stack((s + 1) % NG, (buf + 1) % NBUF)
                sp.wait_ge(mrows_sb, s + 1)
                sp.dma_start(q_stack[M_ROW:M_ROW + 3, buf, :, :].rearrange("a g (t p) -> a (g t) p", p=P),
                             max_rows[:, :]).then_inc(mrows_in, 16)

            step(0, 0, 0, more=False)
            step(1, 1, 0)
            for s in range(2, NG):
                step(s, s % NBUF, s // NBUF, more=(s + 1 < NG))

            sp.wait_ge(near_done, NN * (NG - 1))
            for dst, src in ((wg_all, Wg), (wu_all, Wu)):
                sp.dma_start(dst, src.rearrange("e h f -> h e f")).then_inc(ew_in, 16)
            sp.dma_start(wd_all, Wd.rearrange("e (c p) h -> p (e c) h", p=P)).then_inc(ew_in, 16)

            def load_slots(e, i):
                src = slots[bass.ds(e * CAP, CAP), :].rearrange("(p j) c -> p j c", j=4)
                sp.dma_start(slot_in[i], src).then_inc(es_in[i], 16)

            sp.wait_ge(base_done, TT)
            sp.dma_start(out_tiles, x1[:, :, :]).then_inc(base_out, 16)
            sp.wait_ge(dispatched, 2 * TT * 16)
            load_slots(0, 0)
            load_slots(1, 1)

            def more_slots(e, i):
                sp.wait_ge(ewt_done, 2 * (e - 1))
                sp.sem_inc(slots_free, 1)
                load_slots(e, i)

            with sp.Fori(0, E_NUM // 2 - 1) as k:
                for i in range(2):
                    more_slots(2 * k + 2 + i, i)

        @block.gpsimd
        def _(pool):
            pool.memset(ones_b[:, :], 1.0).then_inc(const_b, 1)
            pool.wait_ge(w_in, 64)
            for i in range(2):
                src = w_attn[:, i, :].rearrange("p (n g d) -> p n d g", g=HG, d=D)
                plain = w_attn[:, 4 + i, :].rearrange("p (n d g) -> p n d g", g=HG, d=D)
                other = w_attn[:, 6 + i, :].rearrange("p (n d g) -> p n d g", g=HG, d=D)
                pool.tensor_copy(plain, src).then_inc(swapped, 1)
                for a in range(2):
                    d0, d1 = a * D // 2, (1 - a) * D // 2
                    pool.tensor_copy(other[:, :, d0:d0 + D // 2, :], src[:, :, d1:d1 + D // 2, :]).then_inc(swapped, 1)
            pool.memset(v_grp[:, :, :, :, :], 0.0).then_inc(zeroed, 1)
            pool.wait_ge(zeroed, 1)
            pool.memset(v_grp[:, :, :, :, D:D + 1], 1.0).then_inc(fixed, 1)

            for c in range(NCH):
                for i in range(2):
                    pool.wait_ge(part_hi, 2 * c + i + 1)
                    if c >= 1:
                        pool.wait_ge(part_lo, 2 * (c - 1) + i + 1)
                    pool.tensor_tensor(qk_rest[i], qk_f[i], part_f[i][c % 2][:, 0, :], ALU.subtract).then_inc(rest_done, 1)
                for i in range(2):
                    pool.wait_ge(part_mid, 2 * c + i + 1)
                    pool.tensor_tensor(part_f[i][c % 2][:, 2, :], qk_rest[i], part_f[i][c % 2][:, 1, :],
                                       ALU.subtract).then_inc(part_lo, 1)
            pool.wait_ge(late_in, 64)
            pool.wait_ge(xn_done, TT)
            bp_all = bass.AP(tensor=bp_row, offset=0, ap=[[C, P], [0, TT], [1, C]])
            pool.tensor_tensor(x_sb[:, :, :], x_sb[:, :, :], bp_all, ALU.add).then_inc(xb_done, 1)

            def step(s, buf, fill):
                fbuf = (buf - 1) % NBUF
                pool.wait_ge(stack_in[fbuf], 96 * (fill + 1))
                for r, u in enumerate(NEAR):
                    qb, kt = UNITS[u]
                    lo, hi, fo = near(qb, kt)
                    pr = probs[:, u % PBUF, :, lo:hi]
                    pool.wait_ge(exp_done, 48 * (s - 1) + HG * (u + 1))
                    if fo == 0:
                        diag = probs[:, u % PBUF, :, lo:lo + P]
                        pool.sem_inc(tile_seen, 1)
                        pool.affine_select(out=diag, in_=diag, compare_op=ALU.is_ge, fill=0.0, base=0,
                                           pattern=[[0, HG], [1, P]], channel_multiplier=-1).then_inc(masked, 1)
                        pool.wait_ge(masked, TPB * (s - 1) + kt + 1)
                    pool.tensor_tensor(pr, pr, f_grp[:, fbuf, :, fo:fo + hi - lo], ALU.mult).then_inc(near_done, 1)

            step(1, 1, 0)
            with pool.Fori(0, 2) as i:
                for j, (s, buf, _) in enumerate(step_args(i)):
                    step(s, buf, i + (1 + j) // NBUF)
            step(NG, NG % NBUF, (NG - 1) // NBUF)

            pool.wait_ge(init_out, 16 * E_NUM)
            for t in range(TT):
                if t % TPB == 0:
                    pool.wait_ge(rows_ready, t // TPB + 1)
                for k in range(2):
                    pool.indirect_dma_start(slots[:, :], bass.IndirectOffsetOnAxis(ap=slot_no[:, k, t:t + 1], axis=0),
                                            u_rows[:, t, :], None, bounds_check=E_NUM * CAP - 1,
                                            oob_is_err=False).then_inc(dispatched, 16)
            pool.wait_ge(base_out, 16)
            pool.wait_ge(trash_out, 16)

            def add_rows(e, i):
                pool.wait_ge(eo_done, 4 * (e + 1))
                if positive(e):
                    pool.wait_ge(added, 64 * e)
                    pool.sem_inc(add_turn, 1)
                for j in range(4):
                    pool.indirect_dma_start(out[:, :], bass.IndirectOffsetOnAxis(ap=e_tok[:, i, j:j + 1], axis=0),
                                            e_out[i][:, j, :], None, bounds_check=B * T + CAP - 1,
                                            oob_is_err=True, compute_op=ALU.add).then_inc(added, 16)

            add_rows(0, 0)
            add_rows(1, 1)
            with pool.Fori(1, E_NUM // 2) as k:
                for i in range(2):
                    add_rows(2 * k + i, i)
            pool.wait_ge(added, 64 * E_NUM)

        @block.scalar
        def _(act):
            act.dma_start(wide[:, 2 * T:], c_wide[:, 2 * T:]).then_inc(c_in, 16)
            act.dma_start(bcol[:, 0:1], bq.rearrange("(p a) -> p a", a=1)).then_inc(c_in, 16)
            act.dma_start(bcol[:, 1:2], bk.rearrange("(p a) -> p a", a=1)).then_inc(c_in, 16)
            act.dma_start(onehot[:, :], c_onehot[:, :]).then_inc(t_in, 16)
            act.dma_start(tab[:, :], table[:, :]).then_inc(t_in, 16)
            act.dma_start(vmask[:, :, :], c_mask[:, :, :]).then_inc(t_in, 16)
            act.dma_start(wide[:, 0:2 * T], c_wide[:, 0:2 * T]).then_inc(rope_in, 16)
            act.dma_start(bv_row[:, :], bass.AP(tensor=bv.tensor, offset=0, ap=[[0, P], [1, C]])).then_inc(rope_in, 16)
            def copy_xnT(c):
                act.wait_ge(xnT_ps, c + 1)
                if c >= 2:
                    act.wait_ge(v_ps, c - 1)
                act.activation(xnT[c % 2], ps_av[:, :], ACT.Copy).then_inc(xnT_sb, 1)

            act.wait_ge(vec_ps, 2)
            act.activation(g_sb, ps_st[0:H, 1, 0:NV], ACT.Exp, scale=SCALE).then_inc(vec_exp, 1)
            copy_xnT(0)
            for c in range(NCH):
                for i in range(2):
                    act.wait_ge(rope_done, 2 * c + i + 1)
                    if c >= 2:
                        act.wait_ge(parts_out[i][c % 2], 48 * (c // 2))
                    act.activation(part_f[i][c % 2][:, 0, :], qk_f[i], ACT.Copy).then_inc(part_hi, 1)
                if c + 1 < NCH:
                    copy_xnT(c + 1)
                for i in range(2):
                    act.wait_ge(rest_done, 2 * c + i + 1)
                    act.activation(part_f[i][c % 2][:, 1, :], qk_rest[i], ACT.Copy).then_inc(part_mid, 1)

            def copy_v(n, buf):
                act.activation(v_grp[:, buf, :, :, 0:D],
                               v_all[:, bass.ds(n, 1), :].rearrange("p a (t g d) -> p (a t) g d", g=HG, d=D),
                               ACT.Copy).then_inc(v_copied, 1)

            def token_exp(b):
                act.wait_ge(ex_ready, b + 1)
                part = col(16, 9)[:, b * TPB:(b + 1) * TPB, :]
                act.activation(part, part, ACT.Exp).then_inc(ex_done, 1)

            def step(s, buf, fill, prev=True, do_s=True, last=False):
                for what in plan(prev, do_s, True, last):
                    if what[0] == "X":
                        token_exp(what[1])
                    if what[0] == "M":
                        if positive(NU * (s - 2)):
                            act.wait_ge(av_done, NU * (s - 2))
                        copy_v(s, buf)
                    if what[0] == "ST":
                        u, g = what[1:]
                        qb, kt = UNITS[u]
                        c0 = first_col(qb, kt)
                        if g == 0 and (u >= PBUF or positive(NU * (s - 1))):
                            act.wait_ge(av_done, NU * (s - 1) + u - PBUF + 1)
                        n = HG * u + g
                        act.wait_ge(scores, 48 * (s - 1) + n + 1)
                        act.activation(probs[:, u % PBUF, g, c0:512], ps_st[:, n % 3, c0:512], ACT.Exp,
                                       scale=SCALE).then_inc(exp_done, 1)
                    if what[0] == "EVAC":
                        qb, back = what[1:]
                        act.wait_ge(av_done, NU * (s + back) - (NU - 4 if qb == 0 else 0))
                        old = 2 * (s + back - 2) + qb + 1
                        if positive(old):
                            act.wait_ge(y_rcp_done, old)
                        act.activation(y_raw[:, qb, :], ps_av[:, :], ACT.Copy).then_inc(y_evac, 1)

            act.wait_ge(part_lo, 2 * NCH)
            for i in range(2):
                for j in range(2):
                    act.wait_ge(parts_out[i][j], 48 * NCH // 2)
            act.wait_ge(vec_out, 32)
            act.wait_ge(v_done, NCH)
            act.wait_ge(fixed, 1)
            copy_v(0, 0)
            step(1, 1, 0, prev=False)
            with act.Fori(0, 2) as i:
                for a in step_args(i):
                    step(*a)
            step(NG, NG % NBUF, 0, do_s=False, last=True)

            token_exp(1)
            for c in range(NCH):
                act.wait_ge(fgu_ps, c + 1)
                if c >= 2:
                    act.wait_ge(f_act_done, c - 1)
                act.activation(tmp_g[0:F4, c % 2, :], ps_st[0:F4, 2, :], ACT.Gelu).then_inc(f_gelu, 1)

            def turned(e, i):
                act.wait_ge(eT_ps, e + 1)
                if positive(e - 1):
                    act.wait_ge(gu_ps, 2 * (e - 1))
                act.activation(slotT[i], ps_slot[:, 0, i * 512:(i + 1) * 512], ACT.Copy).then_inc(eT_sb, 1)

            def gelu(e, i):
                for c in range(2):
                    act.wait_ge(gu_ps, 2 * e + c + 1)
                    if positive(2 * e + c - 1):
                        act.wait_ge(e_gated, 2 * e + c - 1)
                    act.activation(tmp_g[:, c, :], ps_st[:, c, :], ACT.Gelu).then_inc(e_gelu, 1)

            act.wait_ge(f_act_done, NCH)
            turned(0, 0)
            gelu(0, 0)
            with act.Fori(0, E_NUM // 2 - 1) as k:
                turned(2 * k + 1, 1)
                gelu(2 * k + 1, 1)
                turned(2 * k + 2, 0)
                gelu(2 * k + 2, 0)
            turned(E_NUM - 1, 1)
            gelu(E_NUM - 1, 1)

        @block.tensor
        def _(pe):
            pe.wait_ge(t_in, 48)
            for v in range(2):
                pe.matmul(ps_st[0:H, 1 + v, 0:NV], tab[:, :], onehot[:, v * NV:(v + 1) * NV],
                          start=True, stop=True).then_inc(vec_ps, 1)
            pe.wait_ge(c_in, 48)
            for i in range(2):
                mm = pe.matmul(ps_st[:, 0, 2 * i:2 * i + 2], swap[:, i * P:(i + 1) * P], bcol[:, :], start=True, stop=True)
            mm.then_inc(bswap_ps, 1)
            pe.wait_ge(swapped, 6)
            pe.wait_ge(bswap_sb, 1)

            def turn_xn(c):
                pe.wait_ge(xn_done, CH * (c + 1))
                if c >= 1:
                    pe.wait_ge(xnT_sb, c)
                for t in range(CH):
                    mm = pe.transpose(ps_av[:, t * P:(t + 1) * P], xn[c % 2][:, t, :], ident)
                mm.then_inc(xnT_ps, 1)

            turn_xn(0)
            for c in range(NCH):
                pe.wait_ge(xnT_sb, c + 1)
                for i in range(2):
                    if c >= 1:
                        pe.wait_ge(rope_half, 4 * (c - 1) + 2 * i + 2)
                    pe.matmul(ps_slot[:, i, 0:512], w_attn[:, 4 + i, :], xnT[c % 2], start=True, stop=True)
                    pe.matmul(ps_slot[:, i, 512:1024], w_attn[:, 6 + i, :], xnT[c % 2], start=True,
                              stop=True).then_inc(qk_ps, 1)
                if c + 1 < NCH:
                    turn_xn(c + 1)
                if c >= 1:
                    pe.wait_ge(v_done, c)
                for t in range(CH):
                    mm = pe.matmul(ps_st[:, 0, t * P:(t + 1) * P], xnT[c % 2][:, t * P:(t + 1) * P], w_attn[:, 2, :],
                                   start=True, stop=True)
                mm.then_inc(v_ps, 1)

            def s_unit(s, buf, k, slot, su):
                t, heads = SUNITS[su]
                w = (t + 1) * P
                if positive(k - 1):
                    pe.wait_ge(slot_used, k - 1)
                for j, g in enumerate(heads):
                    o = s_offset(t, j)
                    b0 = max(0, (t - 1) * P)
                    for lo in range(0, w, 512):
                        hi = min(w, lo + 512)
                        nlo, nhi = max(lo, b0), hi
                        pe.matmul(ps_slot[:, slot, o + lo:o + hi], q_stack[0:QK_ROWS, buf, g, t * P:(t + 1) * P],
                                  k_stack[0:QK_ROWS, buf, g, lo:hi], start=True, stop=(nlo >= nhi))
                        if nlo < nhi:
                            f0 = nlo - (t - 1) * P
                            mm = pe.matmul(ps_slot[:, slot, o + nlo:o + nhi], ident_b[:, :],
                                           b_grp[:, buf, g, f0:f0 + nhi - nlo], start=False, stop=True)
                mm.then_inc(slot_full, 1)

            unit_at = {}

            def token_unit(what, k, slot):
                kind, c = what
                unit_at[what] = k
                pe.wait_ge(slot_used, k - 1)
                if kind == "A":
                    for t in range(CH):
                        mm = pe.transpose(ps_slot[:, slot, t * P:(t + 1) * P],
                                          y_all[:, c * CH + t, :, :].rearrange("p a c -> p (a c)"), ident)
                elif kind == "B":
                    pe.wait_ge(slot_used, unit_at["A", c] + 1)
                    for t in range(CH):
                        mm = pe.matmul(ps_slot[:, slot, t * P:(t + 1) * P], yT[c % 2][:, t * P:(t + 1) * P],
                                       w_attn[:, 3, :], start=True, stop=True)
                elif kind == "C":
                    pe.wait_ge(u_done, CH * (c + 1))
                    for t in range(CH):
                        mm = pe.transpose(ps_slot[:, slot, t * P:(t + 1) * P], u_rows[:, c * CH + t, 0:C], ident)
                elif kind == "D":
                    pe.wait_ge(slot_used, unit_at["C", 2 * c + 1] + 1)
                    for t in range(TPB):
                        tile = c * TPB + t
                        mm = pe.matmul(ps_slot[:, slot, t * E_NUM:(t + 1) * E_NUM], uT[:, tile * P:(tile + 1) * P],
                                       router[:, :], start=True, stop=True)
                else:
                    pe.wait_ge(sel_done, c + 1)
                    first, end = c * TPB, (c + 1) * TPB
                    pe.matmul(ps_slot[:, slot, 0:TPB * E_NUM], below_b[:, :], sel_b[:, first * E_NUM:end * E_NUM],
                              start=True, stop=False)
                    for t in range(1, end):
                        lo = max(first, t)
                        mm = pe.matmul(ps_slot[:, slot, (lo - first) * E_NUM:TPB * E_NUM], ones_b[:, :],
                                       sel_b[:, (lo - t) * E_NUM:(end - t) * E_NUM], start=False, stop=(t == end - 1))
                mm.then_inc(slot_full, 1)

            def step(s, buf, fill, prev=True, do_s=True, do_t=True, last=False):
                tbuf = (buf - 1) % NBUF
                k, slot = slot_base(s), base_parity(s)
                n_slot = 0
                if do_s:
                    pe.wait_ge(stack_in[buf], 96 * (fill + 1))
                for what in plan(prev, do_s, do_t, last):
                    if what[0] == "ST":
                        u, g = what[1:]
                        qb, kt = UNITS[u]
                        c0 = first_col(qb, kt)
                        n = HG * u + g
                        if n == 0:
                            pe.wait_ge(mrows_in, 16 * s)
                        if n >= 3 or positive(48 * (s - 1)):
                            pe.wait_ge(exp_done, 48 * (s - 1) + n - 2)
                        pe.matmul(ps_st[:, n % 3, c0:512], k_stack[0:ST_ROWS, tbuf, g, kt * P:(kt + 1) * P],
                                  q_stack[0:ST_ROWS, tbuf, g, qb * 512 + c0:qb * 512 + 512],
                                  start=True, stop=True).then_inc(scores, 1)
                    elif what[0] == "AV":
                        u, back = what[1:]
                        qb, kt = UNITS[u]
                        c0 = first_col(qb, kt)
                        vb = (tbuf + back) % NBUF
                        n = s - 1 + back
                        if u in NEAR:
                            pe.wait_ge(near_done, NN * n + NEAR.index(u) + 1)
                        else:
                            pe.wait_ge(exp_done, 48 * n + HG * (u + 1))
                        if u in (0, 4) and positive(2 * n + (u == 4)):
                            pe.wait_ge(y_evac, 2 * n + (1 if u == 4 else 0))
                        if u == 0:
                            pe.wait_ge(v_copied, n + 1)
                        for g in range(HG):
                            mm = pe.matmul(ps_av[32 * g:32 * g + VW, c0:512], v_grp[:, vb, kt, g, :],
                                           probs[:, u % PBUF, g, c0:512], start=(u in (0, 4)), stop=(u in (3, 11)),
                                           skip_group_check=True)
                        mm.then_inc(av_done, 1)
                    elif what[0] == "S":
                        s_unit(s, buf, k + n_slot, (slot + n_slot) % 2, what[1])
                        n_slot += 1
                    elif what[0] == "Y":
                        qb, back = what[1:]
                        pe.wait_ge(y_evac, 2 * (s - 1 + back) + qb + 1)
                        pe.wait_ge(slot_used, k + n_slot - 1)
                        for t in range(CH):
                            mm = pe.transpose(ps_slot[:, (slot + n_slot) % 2, t * P:(t + 1) * P],
                                              y_raw[:, qb, t * P:(t + 1) * P], ident)
                        mm.then_inc(slot_full, 1)
                        n_slot += 1
                    elif what[0] in "ABCDE":
                        token_unit(what, k + n_slot, (slot + n_slot) % 2)
                        n_slot += 1
                    elif what[0] == "M":
                        pe.wait_ge(msplit, 4 * (s + 1))
                        pe.wait_ge(slot_used, k + n_slot - 1)
                        pe.transpose(ps_slot[0:3 * HG * TPB, (slot + n_slot) % 2, 0:P // 2].bitcast(BF16),
                                     max_parts[:, :, :].rearrange("p a n -> p (a n)"), ident_b[:, :]).then_inc(slot_full, 1)
                        n_slot += 1
                return k + n_slot

            pe.wait_ge(const_b, 3)
            pe.wait_ge(rope_half, 4 * NCH)
            pe.wait_ge(v_done, NCH)
            pe.wait_ge(vec_done, 2)
            pe.wait_ge(ones_in, 16)
            step(0, 0, 0, prev=False, do_t=False)
            step(1, 1, 0, prev=False)
            with pe.Fori(0, 2) as i:
                for a in step_args(i):
                    step(*a)
            k = step(NG, NG % NBUF, 0, do_s=False, last=True)

            pe.wait_ge(slot_used, k)
            for what in token_plan(1):
                if what[0] != "X":
                    token_unit(what, k, k % 2)
                    k += 1
            pe.wait_ge(fw_done, 4)
            for c in range(NCH):
                if c >= 1:
                    pe.wait_ge(f_act_done, c)
                pe.matmul(ps_st[0:F4, 2, :], fw[:, 0:F4], uT[:, c * CW:(c + 1) * CW], start=True, stop=True)
                pe.matmul(ps_av[0:F4, :], fw[:, F4:2 * F4], uT[:, c * CW:(c + 1) * CW], start=True,
                          stop=True).then_inc(fgu_ps, 1)
                pe.wait_ge(f_act_done, c + 1)
                if c == 0:
                    pe.wait_ge(slot_used, k)
                for t in range(CH):
                    tile = c * CH + t
                    mm = pe.matmul(ps_slot[:, tile // 8, (tile % 8) * C:(tile % 8 + 1) * C],
                                   f_act[c % 2][:, t * P:(t + 1) * P], fw[:, 2 * F4:2 * F4 + C], start=True, stop=True)
                mm.then_inc(f_ps, 1)

            def turn(e, i, n):
                pe.wait_ge(es_in[i], 16 * (n + 1))
                if positive(e - 1):
                    pe.wait_ge(eT_sb, e - 1)
                for j in range(4):
                    mm = pe.transpose(ps_slot[:, 0, i * 512 + j * P:i * 512 + (j + 1) * P], slot_in[i][:, j, 0:C], ident)
                mm.then_inc(eT_ps, 1)

            def gate_up(e, i):
                pe.wait_ge(eT_sb, e + 1)
                pe.wait_ge(ew_done, 2 * (e + 1))
                for c in range(2):
                    if positive(2 * e + c - 1):
                        pe.wait_ge(e_gated, 2 * e + c - 1)
                    pe.matmul(ps_st[:, c, :], wgu[i][:, c * P:(c + 1) * P], slotT[i], start=True, stop=True)
                    up = ps_st[:, 2, :] if c == 0 else ps_av[:, :]
                    pe.matmul(up, wgu[i][:, FF + c * P:FF + (c + 1) * P], slotT[i], start=True,
                              stop=True).then_inc(gu_ps, 1)

            def down(e, i):
                pe.wait_ge(e_gated, 2 * (e + 1))
                for j in range(4):
                    for c in range(2):
                        mm = pe.matmul(ps_slot[:, 1, i * 512 + j * C:i * 512 + (j + 1) * C],
                                       gated[i][:, c, j * P:(j + 1) * P],
                                       wd_all[:, bass.ds(2 * e + c, 1), :].rearrange("p a c -> p (a c)"),
                                       start=(c == 0), stop=(c == 1))
                mm.then_inc(eo_ps, 1)

            pe.wait_ge(base_done, TT)
            turn(0, 0, 0)
            gate_up(0, 0)
            turn(1, 1, 0)
            with pe.Fori(0, E_NUM // 2 - 1) as k:
                gate_up(2 * k + 1, 1)
                turn(2 * k + 2, 0, k + 1)
                down(2 * k, 0)
                gate_up(2 * k + 2, 0)
                turn(2 * k + 3, 1, k + 1)
                down(2 * k + 1, 1)
            gate_up(E_NUM - 1, 1)
            down(E_NUM - 2, 0)
            down(E_NUM - 1, 1)

        @block.vector
        def _(dve):
            dve.wait_ge(c_in, 48)
            dve.tensor_copy(ident_b[:, :], ident).then_inc(const_b, 1)
            dve.tensor_copy(below_b[:, :], below).then_inc(const_b, 1)

            own = [0]

            def after(ins):
                own[0] += 1
                ins.then_inc(in_order, 1)
                dve.wait_ge(in_order, own[0])

            def rsqrt(dst, src, eps, n):
                v, t = newton[:, 0, 0:n], newton[:, 1, 0:n]
                after(dve.tensor_scalar(v, src, eps, None, ALU.add))
                after(dve.tensor_scalar(dst.bitcast(U32), v.bitcast(U32), 1, None, ALU.logical_shift_right))
                after(dve.tensor_scalar(dst.bitcast(I32), dst.bitcast(I32), -1.0, float(0x5F3759DF), ALU.mult, ALU.add))
                for _ in range(3):
                    after(dve.tensor_tensor(t, dst, dst, ALU.mult))
                    after(dve.scalar_tensor_tensor(out=t, in0=t, scalar=-0.5, in1=v, op0=ALU.mult, op1=ALU.mult))
                    after(dve.scalar_tensor_tensor(out=dst, in0=t, scalar=1.5, in1=dst, op0=ALU.add, op1=ALU.mult))

            stat_count = [0]

            def norm_stats(src, tiles):
                for t in tiles:
                    dve.bn_stats(stats[:, t, :], src[:, t, :]).then_inc(st_done, 1)
                stat_count[0] += len(tiles)
                dve.wait_ge(st_done, stat_count[0])
                for t in tiles:
                    dve.bn_aggr(mv[:, t, :], stats[:, t, :]).then_inc(mv_done, 1)
                dve.wait_ge(mv_done, stat_count[0])
                r = slice(tiles[0], tiles[-1] + 1)
                rsqrt(rstd[:, r], mv[:, r, 1], LN_EPS, len(tiles))

            def normalise(c):
                if c >= 2:
                    dve.wait_ge(xnT_ps, c - 1)
                for t in range(CH):
                    tile = c * CH + t
                    dve.tensor_scalar(xn[c % 2][:, t, :], x_sb[:, tile, :], mv[:, tile, 0:1], rstd[:, tile:tile + 1],
                                      ALU.subtract, ALU.mult).then_inc(xn_done, 1)

            dve.wait_ge(x_in[0], 16)
            norm_stats(x_sb, range(CH))
            normalise(0)
            dve.wait_ge(vec_exp, 1)
            dve.wait_ge(t_in, 48)
            dve.tensor_tensor(g_sb, g_sb, vmask[:, 0, :], ALU.mult).then_inc(vec_done, 1)
            dve.tensor_tensor(r_sb, ps_st[0:H, 2, 0:NV], vmask[:, 1, :], ALU.add).then_inc(vec_done, 1)
            dve.wait_ge(bswap_ps, 1)
            dve.tensor_copy(bcol_perm[:, :], ps_st[:, 0, 0:4]).then_inc(bswap_sb, 1)
            for c in range(1, NCH):
                dve.wait_ge(x_in[c], 16)
            norm_stats(x_sb, range(CH, TT))
            normalise(1)
            dve.wait_ge(bswap_sb, 1)
            dve.wait_ge(rope_in, 32)
            for c in range(NCH):
                tok = (c % 2) * CW
                for i in range(2):
                    n = 2 * c + i
                    dve.wait_ge(qk_ps, n + 1)
                    if n >= 1:
                        dve.wait_ge(rope_done, n)
                    dve.scalar_tensor_tensor(out=rope_a, in0=ps_slot[:, i, 0:512], scalar=bcol_perm[:, i:i + 1],
                                             in1=cos_t[:, tok:tok + CW], op0=ALU.add, op1=ALU.mult).then_inc(rope_half, 1)
                    dve.scalar_tensor_tensor(out=rope_b, in0=ps_slot[:, i, 512:1024], scalar=bcol_perm[:, 2 + i:3 + i],
                                             in1=sin_t[:, tok:tok + CW], op0=ALU.add, op1=ALU.mult).then_inc(rope_half, 1)
                    dve.wait_ge(rope_half, 2 * n + 2)
                    if c >= 1:
                        dve.wait_ge(rest_done, 2 * (c - 1) + i + 1)
                    dve.tensor_tensor(qk_f[i], rope_a, rope_b, ALU.add).then_inc(rope_done, 1)
                if c + 2 < NCH:
                    normalise(c + 2)
                dve.wait_ge(v_ps, c + 1)
                b, kt = c // 2, (c % 2) * CH
                dst = v_all[:, b * 4:b * 4 + 4, kt * HG * D:(kt + CH) * HG * D].rearrange("p n (t c) -> p t n c", t=CH)
                dve.tensor_tensor(dst, ps_st[:, 0, :].rearrange("p (t n c) -> p t n c", t=CH, n=4),
                                  bass.AP(tensor=bv_row, offset=0, ap=[[C, P], [0, CH], [HG * D, 4], [1, HG * D]]),
                                  ALU.add).then_inc(v_done, 1)

            def step(s, buf, fill, prev=True, do_s=True, do_t=True, last=False):
                k, slot = slot_base(s), base_parity(s)
                n_slot, n_max = 0, 0
                for what in plan(prev, do_s, do_t, last):
                    if what[0] not in "SYMABCDE":
                        continue
                    here = (slot + n_slot) % 2
                    if what[0] in "ABCDE":
                        token_unit(what, k + n_slot, here)
                    elif what[0] == "S":
                        t, heads = SUNITS[what[1]]
                        w = (t + 1) * P
                        pitch = s_offset(t, 1)
                        src = ps_slot[:, here, 0:pitch * len(heads)].rearrange("p (g w) -> p g w", w=pitch)[:, :, 0:w] \
                            if len(heads) > 1 else ps_slot[:, here, 0:w]
                        dve.wait_ge(slot_full, k + n_slot + 1)
                        dve.tensor_reduce(neg_max[:, heads[0]:heads[-1] + 1, t], src, AX.X, ALU.max,
                                          negate=True).then_inc(slot_used, 1)
                        n_max += 1
                        if n_max == len(SUNITS):
                            flat = neg_max[:, :, :].rearrange("p g t -> p (g t)")
                            dve.wait_ge(slot_used, k + n_slot + 1)
                            dve.tensor_copy(max_parts[:, 0, :], flat).then_inc(msplit, 1)
                            dve.wait_ge(msplit, 4 * s + 1)
                            dve.tensor_tensor(max_rest[:, :], flat, max_parts[:, 0, :], ALU.subtract).then_inc(msplit, 1)
                            dve.wait_ge(msplit, 4 * s + 2)
                            dve.tensor_copy(max_parts[:, 1, :], max_rest[:, :]).then_inc(msplit, 1)
                            dve.wait_ge(msplit, 4 * s + 3)
                            dve.tensor_tensor(max_parts[:, 2, :], max_rest[:, :], max_parts[:, 1, :],
                                              ALU.subtract).then_inc(msplit, 1)
                    elif what[0] == "M":
                        dve.wait_ge(slot_full, k + n_slot + 1)
                        if positive(16 * s):
                            dve.wait_ge(mrows_in, 16 * s)
                        dve.tensor_copy(max_rows[:, :], ps_slot[0:3 * HG * TPB, here, 0:P // 2].bitcast(BF16))\
                           .then_inc(mrows_sb, 1)
                        dve.wait_ge(mrows_sb, s + 1)
                        dve.sem_inc(slot_used, 1)
                    else:
                        qb, back = what[1:]
                        n = s - 1 + back
                        src = ps_slot[:, here, 0:512].rearrange("p (t g c) -> p t g c", t=CH, g=HG)
                        dve.wait_ge(slot_full, k + n_slot + 1)
                        dve.reciprocal(y_rcp[:, qb, :, :], src[:, :, :, D]).then_inc(y_rcp_done, 1)
                        dve.wait_ge(y_rcp_done, 2 * n + qb + 1)
                        hg = n % (H // HG)
                        dst = y_all[:, bass.ds((n // (H // HG)) * TPB + CH * qb, CH), bass.ds(hg, 1), :]
                        rc = y_rcp[:, qb, :, :].rearrange("p t (g a) -> p t g a", a=1)
                        rc = bass.AP(tensor=rc.tensor, offset=rc.offset, ap=[list(a) for a in rc.ap[:-1]] + [[0, D]])
                        dve.tensor_tensor(dst.rearrange("p t a (g d) -> p t (a g) d", g=HG), src[:, :, :, 0:D], rc,
                                          ALU.mult).then_inc(slot_used, 1)
                    n_slot += 1
                return k + n_slot

            def wide_col(a, n):
                return bass.AP(tensor=a.tensor, offset=a.offset, ap=[list(d) for d in a.ap[:-1]] + [[0, n]])

            RATIO, RINV, RMS, W1, W2, KEEP, S1, OVF, IDX1, IDX2, POS1, POS2, O1, O2, SUM = range(15)
            EXPS, ONE1, ONE2, LG = 16, 25, 33, 41

            def token_unit(what, k, slot):
                kind, c = what
                src = ps_slot[:, slot, 0:CW]
                dve.wait_ge(slot_full, k + 1)
                if kind == "A":
                    dve.tensor_copy(yT[c % 2], src).then_inc(slot_used, 1)
                elif kind == "B":
                    x_c = x_sb[:, c * CH:(c + 1) * CH, :]
                    dve.wait_ge(xb_done, 1)
                    dve.tensor_tensor(x_c, src.rearrange("p (t c) -> p t c", t=CH), x_c, ALU.add).then_inc(slot_used, 1)
                    if c % 2:
                        dve.wait_ge(slot_used, k + 1)
                        second_norm(c // 2)
                elif kind == "C":
                    dve.tensor_copy(uT[:, c * CW:(c + 1) * CW], src).then_inc(slot_used, 1)
                elif kind == "D":
                    choose(c, k, ps_slot[:, slot, 0:TPB * E_NUM])
                else:
                    positions(c, k, ps_slot[:, slot, 0:TPB * E_NUM])

            def second_norm(b):
                r = slice(b * TPB, (b + 1) * TPB)

                def arr(i):
                    return small[:, i * TT:(i + 1) * TT][:, r]

                tiles = range(b * TPB, (b + 1) * TPB)
                norm_stats(x_sb, tiles)
                after(dve.tensor_tensor(arr(RINV), rstd[:, r], rstd[:, r], ALU.mult))
                after(dve.tensor_tensor(arr(RATIO), arr(RINV), mv[:, r, 1], ALU.mult))
                rsqrt(arr(RMS), arr(RATIO), RMS_EPS, TPB)
                dve.tensor_tensor(arr(RINV), newton[:, 0, 0:TPB], arr(RMS), ALU.mult)
                after(dve.tensor_tensor(arr(SUM), rstd[:, r], arr(RMS), ALU.mult))
                for t in tiles:
                    dve.tensor_scalar(u_rows[:, t, 0:C], x_sb[:, t, :], mv[:, t, 0:1],
                                      small[:, SUM * TT + t:SUM * TT + t + 1], ALU.subtract, ALU.mult).then_inc(u_done, 1)

            def views(b):
                r = slice(b * TPB, (b + 1) * TPB)
                return (lambda i: small[:, i * TT:(i + 1) * TT][:, r],
                        lambda i: small[:, i * TT:(i + 1) * TT][:, r].rearrange("p (t a) -> p t a", a=1),
                        lambda i: col(i, 8)[:, r, :])

            def choose(b, k, logits):
                arr, arr3, arr8 = views(b)
                r = slice(b * TPB, (b + 1) * TPB)
                ins = dve.tensor_tensor(arr8(LG), logits.rearrange("p (t e) -> p t e", e=E_NUM),
                                        wide_col(arr3(RINV), E_NUM), ALU.mult)
                ins.then_inc(slot_used, 1)
                dve.wait_ge(slot_used, k + 1)
                for t in range(TPB):
                    ins = dve.max(mx8[:, b * TPB + t, :], arr8(LG)[:, t, :])
                after(ins)
                for t in range(TPB):
                    ins = dve.max_index(ix8[:, b * TPB + t, :], mx8[:, b * TPB + t, :], arr8(LG)[:, t, :])
                ex = col(EXPS, 9)[:, r, :]
                dve.tensor_tensor(ex[:, :, 0:8], arr8(LG), wide_col(mx8[:, r, 0:1], E_NUM), ALU.subtract)
                after(dve.tensor_tensor(ex[:, :, 8:9], mx8[:, r, 1:2], mx8[:, r, 0:1], ALU.subtract))
                dve.sem_inc(ex_ready, 1)
                dve.tensor_copy(arr3(IDX1), ix8[:, r, 0:1])
                after(dve.tensor_copy(arr3(IDX2), ix8[:, r, 1:2]))
                eno = bass.AP(tensor=expert_no.tensor, offset=expert_no.offset,
                              ap=[list(expert_no.ap[0]), [0, TPB], [1, E_NUM]])
                dve.tensor_tensor(arr8(ONE1), wide_col(arr3(IDX1), E_NUM), eno, ALU.is_equal)
                after(dve.tensor_tensor(arr8(ONE2), wide_col(arr3(IDX2), E_NUM), eno, ALU.is_equal))
                dve.tensor_tensor(sel_b[:, b * TPB * E_NUM:(b + 1) * TPB * E_NUM].rearrange("p (t e) -> p t e", e=E_NUM),
                                  arr8(ONE1), arr8(ONE2), ALU.add).then_inc(sel_done, 1)

            def positions(b, k, counts):
                arr, arr3, arr8 = views(b)
                r = slice(b * TPB, (b + 1) * TPB)
                pos = counts.rearrange("p (t e) -> p t e", e=E_NUM)
                dve.tensor_tensor(arr8(ONE1), arr8(ONE1), pos, ALU.mult)
                after(dve.tensor_tensor(arr8(ONE2), arr8(ONE2), pos, ALU.mult))
                dve.sem_inc(slot_used, 1)
                dve.tensor_reduce(arr(POS1), arr8(ONE1), AX.X, ALU.add)
                after(dve.tensor_reduce(arr(POS2), arr8(ONE2), AX.X, ALU.add))
                dve.tensor_scalar(arr(O1), arr(POS1), float(CAP), None, ALU.is_ge)
                after(dve.tensor_scalar(arr(O2), arr(POS2), float(CAP), None, ALU.is_ge))
                after(dve.tensor_tensor(arr(OVF), arr(O1), arr(O2), ALU.max))
                after(dve.tensor_scalar(arr(KEEP), arr(OVF), -1.0, 1.0, ALU.mult, ALU.add))
                dve.wait_ge(ex_done, b + 1)
                after(dve.tensor_reduce(arr(SUM), col(EXPS, 9)[:, r, 0:8], AX.X, ALU.add))
                after(dve.reciprocal(arr(W1), arr(SUM)))
                after(dve.tensor_tensor(arr3(W2), col(EXPS, 9)[:, r, 8:9], arr3(W1), ALU.mult))
                urow = u_rows[:, r, :]
                dve.tensor_tensor(urow[:, :, C:C + 1], arr3(W1), arr3(KEEP), ALU.mult)
                dve.tensor_tensor(urow[:, :, C + 1:C + 2], arr3(W2), arr3(KEEP), ALU.mult)
                dve.tensor_copy(urow[:, :, C + 2:C + 3], arr3(IDX1))
                dve.tensor_copy(urow[:, :, C + 3:C + 4], token_no[:, r].rearrange("p (t a) -> p t a", a=1))
                pairs = ((POS1, IDX1, O1), (POS2, IDX2, O2))
                for pos_i, idx_i, _ in pairs:
                    ins = dve.scalar_tensor_tensor(out=arr(pos_i), in0=arr(idx_i), scalar=float(CAP), in1=arr(pos_i),
                                                   op0=ALU.mult, op1=ALU.add)
                after(ins)
                for pos_i, _, o_i in pairs:
                    ins = dve.scalar_tensor_tensor(out=arr(pos_i), in0=arr(o_i), scalar=FAR, in1=arr(pos_i),
                                                   op0=ALU.mult, op1=ALU.add)
                after(ins)
                dve.tensor_copy(slot_no[:, 0, r], arr(POS1))
                after(dve.tensor_copy(slot_no[:, 1, r], arr(POS2)))
                dve.sem_inc(rows_ready, 1)

            step(0, 0, 0, prev=False, do_t=False)
            step(1, 1, 0, prev=False)
            with dve.Fori(0, 2) as i:
                for a in step_args(i):
                    step(*a)

            dve.wait_ge(v_copied, NG)
            dve.wait_ge(stack_in[(NG - 1) % NBUF], 96 * ((NG - 1) // NBUF + 1))
            dve.memset(f_act[0][F4:P, :], 0.0).then_inc(fw_done, 1)
            dve.memset(f_act[1][F4:P, :], 0.0).then_inc(fw_done, 1)
            dve.memset(fw[F4:P, 2 * F4:2 * F4 + C], 0.0).then_inc(fw_done, 1)
            dve.wait_ge(fw_in, 48)
            dve.wait_ge(late_in, 64)
            dve.tensor_scalar(fw[:, 0:2 * F4], fw[:, 0:2 * F4], fn_col[:, 0:1], None, ALU.mult).then_inc(fw_done, 1)
            k = step(NG, NG % NBUF, 0, do_s=False, last=True)
            for what in token_plan(1):
                if what[0] != "X":
                    token_unit(what, k, k % 2)
                    k += 1

            def arr(i):
                return small[:, i * TT:(i + 1) * TT]

            def arr3(i):
                return small[:, i * TT:(i + 1) * TT].rearrange("p (t a) -> p t a", a=1)

            def fallback_act(c):
                dve.wait_ge(f_gelu, c + 1)
                if c >= 2:
                    dve.wait_ge(f_ps, c - 1)
                dve.tensor_tensor(f_act[c % 2][0:F4, :], tmp_g[0:F4, c % 2, :], ps_av[0:F4, :], ALU.mult)\
                   .then_inc(f_act_done, 1)

            for c in range(NCH):
                fallback_act(c)
            after(dve.tensor_tensor(arr3(S1), u_rows[:, :, C:C + 1], u_rows[:, :, C + 1:C + 2], ALU.add))
            after(dve.tensor_scalar(arr(S1), arr(S1), 1.0, None, ALU.add))
            after(dve.tensor_tensor(arr(S1), arr(S1), arr(RINV), ALU.mult))
            for t in range(TT):
                dve.scalar_tensor_tensor(out=x1[:, t, :], in0=u_rows[:, t, 0:C], scalar=arr(S1)[:, t:t + 1],
                                         in1=x1[:, t, :], op0=ALU.mult, op1=ALU.add).then_inc(base1, 1)
            dve.wait_ge(f_ps, NCH)
            for t in range(TT):
                dve.wait_ge(base1, t + 1)
                dve.scalar_tensor_tensor(out=x1[:, t, :], in0=ps_slot[:, t // 8, (t % 8) * C:(t % 8 + 1) * C],
                                         scalar=arr(OVF)[:, t:t + 1], in1=x1[:, t, :], op0=ALU.mult,
                                         op1=ALU.add).then_inc(base_done, 1)

            def fold_norm(e, i):
                if positive(e - 1):
                    dve.wait_ge(gu_ps, 2 * (e - 1))
                for half, src in ((0, wg_all), (1, wu_all)):
                    dve.tensor_scalar(wgu[i][:, half * FF:(half + 1) * FF],
                                      src[:, bass.ds(e, 1), :].rearrange("p a f -> p (a f)"),
                                      e_norm[:, bass.ds(e, 1)], None, ALU.mult).then_inc(ew_done, 1)

            def weights_of_rows(e, i, n):
                dve.wait_ge(es_in[i], 16 * (n + 1))
                if positive(e - 1):
                    dve.wait_ge(added, 64 * (e - 1))
                a1, a2 = slot_in[i][:, :, C], slot_in[i][:, :, C + 1]
                dve.tensor_copy(e_tok[:, i, :], slot_in[i][:, :, C + 3]).then_inc(ewt, 1)
                dve.tensor_scalar(e_wt[:, i, 0, :], slot_in[i][:, :, C + 2], expert_no[:, bass.ds(e, 1)], None,
                                  ALU.is_equal).then_inc(ewt, 1)
                dve.tensor_tensor(e_wt[:, i, 1, :], a1, a2, ALU.subtract).then_inc(ewt, 1)
                dve.wait_ge(ewt, 3 * e + 3)
                dve.tensor_tensor(e_wt[:, i, 2, :], e_wt[:, i, 0, :], e_wt[:, i, 1, :], ALU.mult).then_inc(ewt_done, 1)
                dve.wait_ge(ewt_done, 2 * e + 1)
                dve.tensor_tensor(e_wt[:, i, 2, :], e_wt[:, i, 2, :], a2, ALU.add).then_inc(ewt_done, 1)
                dve.wait_ge(ewt_done, 2 * e + 2)

            def gate(e, i):
                for c in range(2):
                    dve.wait_ge(e_gelu, 2 * e + c + 1)
                    up = ps_st[:, 2, :] if c == 0 else ps_av[:, :]
                    dve.tensor_tensor(gated[i][:, c, :], tmp_g[:, c, :], up, ALU.mult).then_inc(e_gated, 1)

            def scale_rows(e, i):
                dve.wait_ge(eo_ps, e + 1)
                for j in range(4):
                    dve.tensor_scalar(e_out[i][:, j, :], ps_slot[:, 1, i * 512 + j * C:i * 512 + (j + 1) * C], e_wt[:, i, 2, j:j + 1], None,
                                      ALU.mult).then_inc(eo_done, 1)

            dve.wait_ge(ew_in, 48)
            fold_norm(0, 0)
            fold_norm(1, 1)
            gate(0, 0)
            weights_of_rows(0, 0, 0)
            with dve.Fori(0, E_NUM // 2 - 1) as k:
                fold_norm(2 * k + 2, 0)
                gate(2 * k + 1, 1)
                scale_rows(2 * k, 0)
                weights_of_rows(2 * k + 1, 1, k)
                fold_norm(2 * k + 3, 1)
                gate(2 * k + 2, 0)
                scale_rows(2 * k + 1, 1)
                weights_of_rows(2 * k + 2, 0, k + 1)
            gate(E_NUM - 1, 1)
            scale_rows(E_NUM - 2, 0)
            weights_of_rows(E_NUM - 1, 1, E_NUM // 2 - 1)
            scale_rows(E_NUM - 1, 1)


def shape_constants():
    import math

    import numpy as np

    inv = (1.0 / np.float32(10000.0) ** (np.arange(0, D, 2, dtype=np.float32) / np.float32(D))).astype(np.float32)
    ang = np.arange(T, dtype=np.float32)[None, :] * inv[:, None]
    d_of = (np.arange(P) % (HG * D)) // HG
    ang = ang[d_of % (D // 2)]
    sign = np.where(d_of < D // 2, -1.0, 1.0)[:, None]
    k, m = np.arange(P)[:, None], np.arange(P)[None, :]
    head = m // (HG * D) * HG + m % HG
    d_m = (m % (HG * D)) // HG
    plain, swap = k == head * D + d_m, k == head * D + (d_m + D // 2) % D
    wide = np.concatenate([np.cos(ang), np.sin(ang) * sign, k == m, k < m, plain, swap,
                           np.broadcast_to(np.arange(E_NUM), (P, E_NUM)),
                           np.arange(TT)[None, :] * P + k], axis=1).astype(np.float32)

    def bucket(n):
        big = 16 + int(math.log(max(n, 1) / 16) / math.log(8) * 16) if n >= 16 else n
        return min(big, NB - 1)

    onehot = np.zeros((NB, 2, NV), np.float32)
    mask = np.zeros((H, 2, NV), np.float32)
    for y in range(NV):
        for v, n in ((0, y - (P - 1)), (1, 2 * P - 1 - y)):
            if n >= 0:
                onehot[bucket(n), v, y] += 1
                onehot[NB - 1, v, y] -= 1
                mask[:, v, y] = 1 - v
            else:
                mask[:, v, y] = -1e30 * v
    rows = np.zeros((CAP, ROW), np.float32)
    rows[:, C + 2] = -1
    rows[:, C + 3] = B * T + np.arange(CAP)
    ones = np.full((3, NBUF * HG * T // 2), 0x3F803F80, np.uint32).view(np.float32)
    return {"c_wide": wide, "c_onehot": onehot.reshape(NB, 2 * NV), "c_mask": mask, "c_rows": rows, "c_ones": ones}


_INS = ["L0_attn_x", "L0_attn_Wq", "L0_attn_bq", "L0_attn_Wk", "L0_attn_bk", "L0_attn_Wv", "L0_attn_bv",
        "L0_attn_Wp", "L0_attn_bp", "L0_attn_rel_bias_table", "L0_ffn_Wr", "L0_ffn_norm_w", "L0_ffn_Wg",
        "L0_ffn_Wu", "L0_ffn_Wd", "L0_ffn_f_norm", "L0_ffn_fWg", "L0_ffn_fWu", "L0_ffn_fWd"]


def kernel(**inputs):
    import numpy as _np
    import concourse.bacc as _bacc
    from concourse import mybir as _mybir
    from concourse.bass_utils import run_bass_kernel_spmd as _run

    nc = _bacc.Bacc("TRN2", target_bir_lowering=False, num_devices=1)
    arrays, args = {}, []
    for name, a in [(n, inputs[n]) for n in _INS] + list(shape_constants().items()):
        a = _np.ascontiguousarray(a)
        arrays[f"in_{name}_dram"] = a
        args.append(nc.dram_tensor(f"in_{name}_dram", a.shape, _mybir.dt.from_np(a.dtype), kind="ExternalInput").ap())
    args.append(nc.dram_tensor("out_0_dram", (B * T + CAP, C), _mybir.dt.float32, kind="ExternalOutput").ap())
    layer_kernel(nc, *args)
    r = _run(nc, [arrays], core_ids=[0])
    return r.results[0]["out_0_dram"][0:B * T].reshape(B, T, C)
```

```python
from contextlib import ExitStack

import concourse.bass as bass
from concourse import mybir

F32 = mybir.dt.float32
BF16 = mybir.dt.bfloat16
U32 = mybir.dt.uint32
I32 = mybir.dt.int32
ALU = mybir.AluOpType
ACT = mybir.ActivationFunctionType
AX = mybir.AxisListType

P = 128
B, T, C = 2, 1024, 128
H, D = 16, 8
TPB = T // P
TT = B * TPB
HG = 4
NG = B * H // HG
CH = 4
NCH = TT // CH
CW = CH * P
NB = 32
NV = 3 * P
QK_ROWS = 9 * D
M_ROW = QK_ROWS
VW = 32
E_NUM, FF, F4, CAP = 8, 256, 64, 512
STACK_IN = 6 * 16
WARM_FIRST, WARM_STACK, WARM_SLOTS = 8, 8, 32
NBUF = 3
PBUF = 4
ROW = C + 4
SCALE = float(D) ** -0.5
LN_EPS, RMS_EPS = 1e-5, 1e-6
FAR = 1.0e6
BIG = 3.0e38

UNITS = [(0, 0), (0, 1), (0, 2), (0, 3), (1, 0), (1, 4), (1, 1), (1, 5), (1, 2), (1, 6), (1, 3), (1, 7)]
NU = len(UNITS)
SUNITS = [(0, (0, 1, 2, 3))] + [(t, hs) for t in (1, 2, 3) for hs in ((0, 1), (2, 3))] \
    + [(t, (g,)) for t in (4, 5, 6, 7) for g in range(HG)]
AV_LAG = 3
AV_AT = [0, 3, 1, 0, 4, 4, 3, 2, 3, 4, 3, 2]
Y_AT = (10, 4)
S_AT = [0, 0, 2, 3, 5, 7, 12, 13, 18, 21, 24, 25, 28, 30, 32, 34, 38, 40, 41, 44, 46, 48, 50]
M_AT = 58


def first_col(qb, kt):
    return max(0, kt - CH * qb) * P


def near(qb, kt):
    lo, hi = max(kt, CH * qb), min(kt + 2, CH * qb + CH)
    return (lo - CH * qb) * P, (hi - CH * qb) * P, (lo - kt) * P


NEAR = [n for n, u in enumerate(UNITS) if near(*u)[0] < near(*u)[1]]
NN = len(NEAR)


def s_offset(t, k):
    return k * (t + 1) * P if t < 2 else k * 512


SPANS = [(0, TPB), (TPB, TT)]
SPAN_ENDS = {end // CH - 1: i for i, (_, end) in enumerate(SPANS)}
SPAN_STARTS = {first: i for i, (first, _) in enumerate(SPANS)}
TOKENS_AT = {0: [("A", 0), ("A", 1)], 1: [("B", 0), ("B", 1)], 6: [("C", 0), ("C", 1)], 7: [("D", 0)],
             9: [("A", 2), ("X", 0), ("E", 0)], 10: [("NEAR", 10)], 11: [("NEAR", 11), ("B", 2)]}
LAST_NEAR = [10, 11]
N_FLIP = H * 2 * P // 512
TOKENS_LAST = [("A", 3), ("B", 3), ("F", 0), ("F", 1), ("C", 2), ("C", 3), ("D", 1), ("X", 1), ("E", 1),
               ("F", 2), ("F", 3), ("G", 0), ("G", 1), ("G", 2), ("G", 3)]


def exp_plan(last):
    out = []
    for u in range(NU):
        back = -1 if u < AV_LAG else 0
        tile = (u - AV_LAG) % NU
        items = [("ST", u, g) for g in range(HG)]
        av = [("AV", tile, back)]
        if tile == NU - 1 or tile == CH - 1:
            av.append(("EVAC", 1 if tile == NU - 1 else 0, back))
        items[AV_AT[u]:AV_AT[u]] = av
        if u == Y_AT[1]:
            items.append(("Y", 1, -1))
        if u == Y_AT[0] - 2 * last:
            items.append(("Y", 0, 0))
        out += items
    return out


def plan(prev, do_s, do_t, last):
    out = []
    for n, item in enumerate(exp_plan(last) + [None]):
        if do_s:
            out += [("S", su) for su in range(len(SUNITS)) if S_AT[su] == n]
            if n == M_AT:
                out.append(("M",))
        if n % 6 == 5 and n // 6 < N_FLIP and not do_t:
            out.append(("FLIP", n // 6))
        if item and do_t and (prev or item[0] == "ST" or item[-1] == 0):
            out.append(item)
        if last and item and item[0] == "ST" and item[2] == HG - 1:
            out += TOKENS_AT.get(item[1], [])
    if last:
        out += [("AV", t, 0) for t in range(NU - AV_LAG, NU)] + [("EVAC", 1, 0), ("Y", 1, 0)]
    return out


def positive(v):
    return not isinstance(v, int) or v > 0


def layer_kernel(nc, x, Wq, bq, Wk, bk, Wv, bv, Wp, bp, table, Wr, norm_w, Wg, Wu, Wd, f_norm,
                 fWg, fWu, fWd, c_wide, c_onehot, c_mask, c_rows, c_ones, out):
    ctx = ExitStack()
    with ctx:
        def sb(name, shape, dt=F32):
            return ctx.enter_context(nc.sbuf_tensor(name, shape, dt))

        def sem(name):
            return ctx.enter_context(nc.semaphore(name))

        q_parts = nc.dram_tensor("q_parts", [NG, 3, D, HG * T], BF16, kind="Internal")
        k_parts = nc.dram_tensor("k_parts", [NG, 3, D, HG * T], BF16, kind="Internal")
        g_vec = nc.dram_tensor("g_vec", [H, NV], F32, kind="Internal")
        r_vec = nc.dram_tensor("r_vec", [H, NV], BF16, kind="Internal")
        slots = nc.dram_tensor("slots", [E_NUM * CAP, ROW], F32, kind="Internal")

        ps_slot = ctx.enter_context(nc.psum_tensor("ps_slot", [P, 2, 1024], F32))
        ps_st = ctx.enter_context(nc.psum_tensor("ps_st", [P, 3, 512], F32))
        ps_av = ctx.enter_context(nc.psum_tensor("ps_av", [P, 512], F32))

        wide = sb("wide", [P, 2 * T + 5 * P + E_NUM + TT])
        cos_t, sin_t = wide[:, 0:T], wide[:, T:2 * T]
        ident = wide[:, 2 * T:2 * T + P]
        below = wide[:, 2 * T + P:2 * T + 2 * P]
        swap = wide[:, 2 * T + 2 * P:2 * T + 4 * P]
        flip = wide[:, 2 * T + 4 * P:2 * T + 5 * P]
        expert_no = wide[:, 2 * T + 5 * P:2 * T + 5 * P + E_NUM]
        token_no = wide[:, 2 * T + 5 * P + E_NUM:2 * T + 5 * P + E_NUM + TT]
        onehot = sb("onehot", [NB, 2 * NV])
        vmask = sb("vmask", [H, 2, NV])
        tab = sb("tab", [NB, H])
        ident_b = sb("ident_b", [P, P], BF16)
        flip_b = sb("flip_b", [P, P], BF16)
        below_b = sb("below_b", [P, P], BF16)
        ones_b = sb("ones_b", [P, P], BF16)
        x_sb = sb("x_sb", [P, TT, C])
        w_attn = sb("w_attn", [P, 8, C])
        bcol = sb("bcol", [P, 2])
        bcol_perm = sb("bcol_perm", [P, 4])
        bv_row = sb("bv_row", [P, C])
        bp_row = sb("bp_row", [P, C])
        stats = sb("stats", [P, TT, 6])
        mv = sb("mv", [P, TT, 2])
        rstd = sb("rstd", [P, 2, TT])
        newton = sb("newton", [P, 4, TT])
        q_stack = sb("q_stack", [P, NBUF, HG, T], BF16)
        k_stack = sb("k_stack", [P, NBUF, HG, T], BF16)
        v_all = sb("v_all", [P, NG, TPB * HG * D])
        v_grp = sb("v_grp", [P, NBUF, TPB, HG, VW])
        f_all = sb("f_all", [P, H * 2 * P])
        b_all = sb("b_all", [P, H * 2 * P], BF16)
        f_grp = sb("f_grp", [P, NBUF, HG, 2 * P])
        b_grp = sb("b_grp", [P, NBUF, HG, 2 * P], BF16)
        probs = sb("probs", [P, PBUF, HG, 512])
        neg_max = sb("neg_max", [P, HG, TPB])
        max_rest = sb("max_rest", [P, HG * TPB])
        max_parts = sb("max_parts", [P, 3, HG * TPB], BF16)
        max_rows = sb("max_rows", [3 * HG * TPB, P], BF16)
        y_raw = sb("y_raw", [P, 2, 512])
        y_rcp = sb("y_rcp", [P, 2, CH, HG])
        y_all = sb("y_all", [P, TT, H // HG, HG * D])

        pro = probs[:, :, :, :].rearrange("p a b c -> p (a b c)")
        xn = [pro[:, i * CW:(i + 1) * CW].rearrange("p (t c) -> p t c", t=CH) for i in range(2)]
        xnT = [pro[:, CW * (2 + i):CW * (3 + i)] for i in range(2)]
        rope_a, rope_b = pro[:, 4 * CW:5 * CW], pro[:, 5 * CW:6 * CW]
        qk_f = [pro[:, (6 + i) * CW:(7 + i) * CW] for i in range(2)]
        qk_rest = [pro[:, (8 + i) * CW:(9 + i) * CW] for i in range(2)]
        w = 3 * CW // 2
        part_f = [[pro[:, 10 * CW + (2 * i + j) * w:10 * CW + (2 * i + j + 1) * w].bitcast(BF16)
                   .rearrange("p (a n) -> p a n", n=CW) for j in range(2)] for i in range(2)]
        g_sb = y_raw[0:H, 0, 0:NV]
        r_sb = y_raw[0:H, 1, 0:NV // 2].bitcast(BF16)

        uT = wide[:, 0:TT * P]
        u_rows = f_all[:, 0:TT * ROW].rearrange("p (t c) -> p t c", c=ROW)
        small = f_all[:, TT * ROW:TT * ROW + 57 * TT]
        v_flat = v_all[:, :, :].rearrange("p a b -> p (a b)")
        yT = [v_flat[:, i * CW:(i + 1) * CW] for i in range(2)]
        f_act = [v_flat[:, (2 + i) * CW:(3 + i) * CW] for i in range(2)] + yT
        x1 = x_sb

        def stack_floats(st, buf, n):
            return st[:, buf, :, :].rearrange("p g t -> p (g t)").bitcast(F32).rearrange("p (e f) -> p e f", e=n)

        wg_all, wu_all = stack_floats(q_stack, 2, E_NUM), stack_floats(k_stack, 2, E_NUM)
        wd_all = stack_floats(k_stack, 0, 2 * E_NUM)

        def col(i, n=1):
            return small[:, i * TT:(i + n) * TT].rearrange("p (t k) -> p t k", k=n)

        wgu = [pro[:, i * 512:(i + 1) * 512] for i in range(2)]
        e0 = 1024
        slot_in = [pro[:, e0 + i * 4 * ROW:e0 + (i + 1) * 4 * ROW].rearrange("p (j c) -> p j c", c=ROW) for i in range(2)]
        e1 = e0 + 8 * ROW
        slotT = [pro[:, e1 + i * 512:e1 + (i + 1) * 512] for i in range(2)]
        e2 = e1 + 1024
        gated = [pro[:, e2 + i * 1024:e2 + (i + 1) * 1024].rearrange("p (c n) -> p c n", c=2) for i in range(2)]
        e3 = e2 + 2048
        e_out = [pro[:, e3 + i * 512:e3 + (i + 1) * 512].rearrange("p (j c) -> p j c", c=C) for i in range(2)]
        tmp_g = y_raw[:, :, :]
        fw = sb("fw", [P, 2 * F4 + C])
        router = sb("router", [P, E_NUM])
        e_norm = sb("e_norm", [P, E_NUM])
        e_wt = sb("e_wt", [P, 2, 3, 4])
        e_row_tok = sb("e_row_tok", [P, 2, 4])
        e_tok = sb("e_tok", [P, 2, 4], U32)
        fn_col = sb("fn_col", [P, 1])
        slot_no = sb("slot_no", [P, 2, TT], U32)
        mx8 = sb("mx8", [P, TT, 8])
        ix8 = sb("ix8", [P, TT, 8], U32)
        sel_b = sb("sel_b", [P, TT * E_NUM], BF16)

        x_in = [sem(f"x_in{i}") for i in range(NCH)]
        w_in = sem("w_in")
        c_in = sem("c_in")
        t_in = sem("t_in")
        rope_in = sem("rope_in")
        ones_in = sem("ones_in")
        late_in = sem("late_in")
        const_b = sem("const_b")
        swapped = sem("swapped")
        zeroed = sem("zeroed")
        fixed = sem("fixed")
        st_done = sem("st_done")
        mv_done = sem("mv_done")
        xn_done = sem("xn_done")
        xnT_ps = sem("xnT_ps")
        xnT_sb = sem("xnT_sb")
        qk_ps = sem("qk_ps")
        rope_half = sem("rope_half")
        rope_done = sem("rope_done")
        part_hi = sem("part_hi")
        rest_done = sem("rest_done")
        part_mid = sem("part_mid")
        part_lo = sem("part_lo")
        parts_out = [[sem(f"parts_out{i}{j}") for j in range(2)] for i in range(2)]
        v_ps = sem("v_ps")
        v_done = sem("v_done")
        bswap_ps = sem("bswap_ps")
        bswap_sb = sem("bswap_sb")
        vec_ps = sem("vec_ps")
        vec_exp = sem("vec_exp")
        vec_done = sem("vec_done")
        vec_out = sem("vec_out")
        toep_in = sem("toep_in")
        flip_ps = sem("flip_ps")
        flip_sb = sem("flip_sb")
        xb_done = sem("xb_done")
        stack_in = [sem(f"stack_in{i}") for i in range(NBUF)]
        factors_in = [sem(f"factors_in{i}") for i in range(NBUF)]
        slot_full = sem("slot_full")
        slot_used = sem("slot_used")
        scores = sem("scores")
        exp_done = sem("exp_done")
        near_done = sem("near_done")
        last_near_done = sem("last_near_done")
        av_done = sem("av_done")
        y_evac = sem("y_evac")
        y_rcp_done = sem("y_rcp_done")
        max_done = sem("max_done")
        msplit = sem("msplit")
        mrows_sb = sem("mrows_sb")
        mrows_in = sem("mrows_in")
        masked = sem("masked")
        v_copied = sem("v_copied")
        ln2 = sem("ln2")
        u_done = sem("u_done")
        in_order = sem("in_order")
        ex_ready = sem("ex_ready")
        ex_done = sem("ex_done")
        sel_done = sem("sel_done")
        rows_ready = sem("rows_ready")
        fw_in = sem("fw_in")
        fw_done = sem("fw_done")
        fgu_ps = sem("fgu_ps")
        f_gelu = sem("f_gelu")
        f_act_done = sem("f_act_done")
        f_ps = sem("f_ps")
        base1 = sem("base1")
        base_done = sem("base_done")
        init_out = sem("init_out")
        trash_out = sem("trash_out")
        dispatched = sem("dispatched")
        base_out = sem("base_out")
        ew_in = sem("ew_in")
        es_in = [sem(f"es_in{i}") for i in range(2)]
        ew_done = sem("ew_done")
        eT_ps = sem("eT_ps")
        eT_sb = sem("eT_sb")
        gu_ps = sem("gu_ps")
        e_gelu = sem("e_gelu")
        e_gated = sem("e_gated")
        eo_ps = sem("eo_ps")
        ewt = sem("ewt")
        ewt_done = sem("ewt_done")
        eo_done = sem("eo_done")
        added = sem("added")
        tile_seen = sem("tile_seen")
        stack_free = sem("stack_free")
        add_turn = sem("add_turn")
        slots_free = sem("slots_free")

        x_tiles = x.rearrange("b (t p) c -> p (b t) c", p=P)
        out_tiles = out[0:B * T, :].rearrange("(t p) c -> p t c", p=P)

        block = ctx.enter_context(nc.Block())

        def step_args(i):
            return [(2 + 3 * i + j, (2 + j) % NBUF, i + (2 + j) // NBUF) for j in range(3)]

        def slot_base(s):
            if isinstance(s, int) and s < 2:
                return 24 * s
            return 26 * s - 3

        def base_parity(s):
            return slot_base(s) % 2 if isinstance(s, int) else 1

        def flip_bank(j):
            return ps_st[:, j % 4, :] if j % 4 < 3 else ps_av[:, :]

        def load_tiles(eng, dst, vec):
            src = bass.AP(tensor=vec, offset=0, ap=[[1, P], [NV, H], [1, 2 * P]])
            eng.dma_start(dst[:, :].rearrange("p (h c) -> p h c", h=H), src).then_inc(toep_in, 16)

        def load_group(eng, dst, src, n, buf, sems):
            w = HG * 2 * P
            eng.dma_start(dst[:, buf, :, :].rearrange("p g c -> p (g c)"),
                          src[:, bass.ds((n % (H // HG)) * w, w)]).then_inc(sems[buf], 16)

        @block.sync
        def _(sp):
            for c in range(NCH):
                sp.dma_start(x_sb[:, c * CH:(c + 1) * CH, :], x_tiles[:, c * CH:(c + 1) * CH, :]).then_inc(x_in[c], 16)
                if c == 1:
                    for i, w in enumerate((Wq, Wk, Wv, Wp)):
                        sp.dma_start(w_attn[:, i, :], w[:, :]).then_inc(w_in, 16)

            def store_parts(c):
                for i, dst in enumerate((q_parts, k_parts)):
                    sp.wait_ge(part_lo, 2 * c + i + 1)
                    for a in range(3):
                        n0, tok = (c // 2) * 4, (c % 2) * CW
                        ap = bass.AP(tensor=dst, offset=(n0 * 3 + a) * HG * D * T + tok,
                                     ap=[[3 * HG * D * T, 4], [T, HG * D], [1, CW]])
                        sp.dma_start(ap, part_f[i][c % 2][:, a, :]).then_inc(parts_out[i][c % 2], 16)

            sp.dma_start(bp_row[:, :], bass.AP(tensor=bp.tensor, offset=0, ap=[[0, P], [1, C]])).then_inc(late_in, 16)
            sp.dma_start(e_norm[:, :], norm_w.rearrange("e h -> h e"), allow_slow_non_contiguous=True).then_inc(late_in, 16)
            sp.dma_start(router[:, :], Wr[:, :]).then_inc(late_in, 16)
            sp.dma_start(fn_col[:, :], f_norm.rearrange("(p a) -> p a", a=1)).then_inc(late_in, 16)
            sp.dma_start(fw[:, 0:F4], fWg[:, :]).then_inc(fw_in, 16)
            sp.dma_start(fw[:, F4:2 * F4], fWu[:, :]).then_inc(fw_in, 16)
            sp.dma_start(fw[0:F4, 2 * F4:2 * F4 + C], fWd[:, :]).then_inc(fw_in, 16)
            sp.wait_ge(vec_done, 2)
            for dst, vec in ((r_vec, r_sb), (g_vec, g_sb)):
                sp.dma_start(dst[:, :], vec).then_inc(vec_out, 16)
            sp.wait_ge(vec_out, 32)
            load_tiles(sp, b_all, r_vec)
            load_tiles(sp, f_all, g_vec)
            sp.wait_ge(zeroed, 2)
            sp.dma_start(k_stack[M_ROW:M_ROW + 3, :, :, :].rearrange("p a b c -> p (a b c)").bitcast(F32),
                         c_ones[0:3, :]).then_inc(ones_in, 16)
            store_parts(0)
            store_parts(1)

            def load_stack(n, buf):
                for a in range(3):
                    sp.dma_start(q_stack[24 * a:24 * a + 24, buf, :, :].rearrange("p g t -> p (g t)"),
                                 bass.AP(tensor=q_parts, offset=n * (3 * HG * D * T) + a * (HG * D * T),
                                         ap=[[0, 3], [HG * T, D], [1, HG * T]])).then_inc(stack_in[buf], 16)
                sp.dma_start(k_stack[0:QK_ROWS, buf, :, :].rearrange("p g t -> p (g t)"),
                             bass.AP(tensor=k_parts, offset=n * (3 * HG * D * T),
                                     ap=[[0, 3], [HG * T, 3 * D], [1, HG * T]])).then_inc(stack_in[buf], 16)
                sp.dma_start(q_stack[M_ROW:M_ROW + 3, buf, :, :].rearrange("p g t -> p (g t)").bitcast(F32),
                             c_ones[3:6, 0:HG * T // 2]).then_inc(stack_in[buf], 16)
                load_group(sp, b_grp, b_all, n, buf, stack_in)

            for i in range(2):
                for j in range(2):
                    sp.wait_ge(parts_out[i][j], 1 * 48)
            sp.wait_ge(toep_in, 32)
            load_stack(0, 0)
            load_stack(1, 1)
            store_parts(2)
            store_parts(3)
            for e in range(E_NUM):
                sp.dma_start(slots[e * CAP:(e + 1) * CAP, :], c_rows[:, :]).then_inc(init_out, 16)
            sp.dma_start(out[B * T:B * T + CAP, :], c_rows[:, 0:C]).then_inc(trash_out, 16)
            for i in range(2):
                for j in range(2):
                    sp.wait_ge(parts_out[i][j], 2 * 48)

            def step(s, buf, fill, more=True):
                if more:
                    if positive(48 * (s - 1)):
                        sp.wait_ge(near_done, NN * (s - 1))
                        sp.sem_inc(stack_free, 1)
                    load_stack((s + 1) % NG, (buf + 1) % NBUF)
                    load_group(sp, f_grp, f_all, s + 1, (buf + 1) % NBUF, factors_in)
                sp.wait_ge(mrows_sb, s + 1)
                sp.dma_start(q_stack[M_ROW:M_ROW + 3, buf, :, :].rearrange("a g (t p) -> a (g t) p", p=P),
                             max_rows[:, :]).then_inc(mrows_in, 16)

            step(0, 0, 0, more=False)
            sp.wait_ge(flip_sb, N_FLIP)
            step(1, 1, 0)
            for s in range(2, NG):
                step(s, s % NBUF, s // NBUF, more=(s + 1 < NG))

            sp.wait_ge(near_done, NN * (NG - 1))
            for dst, src in ((wg_all, Wg), (wu_all, Wu)):
                sp.dma_start(dst, src.rearrange("e h f -> h e f")).then_inc(ew_in, 16)
            sp.dma_start(wd_all, Wd.rearrange("e (c p) h -> p (e c) h", p=P)).then_inc(ew_in, 16)

            def load_slots(e, i):
                src = slots[bass.ds(e * CAP, CAP), :].rearrange("(p j) c -> p j c", j=4)
                sp.dma_start(slot_in[i], src).then_inc(es_in[i], 16)

            sp.wait_ge(dispatched, 2 * TT * 16)
            load_slots(0, 0)
            load_slots(1, 1)
            sp.wait_ge(base_done, TT)
            sp.dma_start(out_tiles, x1[:, :, :]).then_inc(base_out, 16)

            def more_slots(e, i):
                sp.wait_ge(ewt_done, 2 * (e - 1))
                sp.sem_inc(slots_free, 1)
                load_slots(e, i)

            with sp.Fori(0, E_NUM // 2 - 1) as k:
                for i in range(2):
                    more_slots(2 * k + 2 + i, i)

        @block.gpsimd
        def _(pool):
            pool.memset(ones_b[:, :], 1.0).then_inc(const_b, 1)
            flat = [st[:, :, :, :].rearrange("p a b c -> p (a b c)").bitcast(F32) for st in (q_stack, k_stack)]
            pool.memset(flat[0], 0.0).then_inc(zeroed, 1)
            pool.wait_ge(w_in, 64)
            for i in range(2):
                src = w_attn[:, i, :].rearrange("p (n g d) -> p n d g", g=HG, d=D)
                plain = w_attn[:, 4 + i, :].rearrange("p (n d g) -> p n d g", g=HG, d=D)
                other = w_attn[:, 6 + i, :].rearrange("p (n d g) -> p n d g", g=HG, d=D)
                pool.tensor_copy(plain, src).then_inc(swapped, 1)
                for a in range(2):
                    d0, d1 = a * D // 2, (1 - a) * D // 2
                    pool.tensor_copy(other[:, :, d0:d0 + D // 2, :], src[:, :, d1:d1 + D // 2, :]).then_inc(swapped, 1)
            pool.memset(flat[1], 0.0).then_inc(zeroed, 1)
            pool.memset(v_grp[:, :, :, :, :], 0.0).then_inc(zeroed, 1)
            pool.wait_ge(zeroed, 3)
            pool.memset(v_grp[:, :, :, :, D:D + 1], 1.0).then_inc(fixed, 1)

            for c in range(NCH):
                for i in range(2):
                    pool.wait_ge(part_hi, 2 * c + i + 1)
                    if c >= 1:
                        pool.wait_ge(part_lo, 2 * (c - 1) + i + 1)
                    pool.tensor_tensor(qk_rest[i], qk_f[i], part_f[i][c % 2][:, 0, :], ALU.subtract).then_inc(rest_done, 1)
                for i in range(2):
                    pool.wait_ge(part_mid, 2 * c + i + 1)
                    pool.tensor_tensor(part_f[i][c % 2][:, 2, :], qk_rest[i], part_f[i][c % 2][:, 1, :],
                                       ALU.subtract).then_inc(part_lo, 1)
            pool.wait_ge(late_in, 64)
            pool.wait_ge(xn_done, TT)
            bp_all = bass.AP(tensor=bp_row, offset=0, ap=[[C, P], [0, TT], [1, C]])
            pool.tensor_tensor(x_sb[:, :, :], x_sb[:, :, :], bp_all, ALU.add).then_inc(xb_done, 1)

            def step(s, buf, fill, last=False):
                fbuf = (buf - 1) % NBUF
                pool.wait_ge(factors_in[fbuf], 16 * (fill + 1))
                for r, u in enumerate(NEAR):
                    if last and u in LAST_NEAR:
                        continue
                    qb, kt = UNITS[u]
                    lo, hi, fo = near(qb, kt)
                    pr = probs[:, u % PBUF, :, lo:hi]
                    pool.wait_ge(exp_done, 48 * (s - 1) + HG * (u + 1))
                    if fo == 0:
                        diag = probs[:, u % PBUF, :, lo:lo + P]
                        pool.sem_inc(tile_seen, 1)
                        pool.affine_select(out=diag, in_=diag, compare_op=ALU.is_ge, fill=0.0, base=0,
                                           pattern=[[0, HG], [1, P]], channel_multiplier=-1).then_inc(masked, 1)
                        pool.wait_ge(masked, TPB * (s - 1) + kt + 1)
                    pool.tensor_tensor(pr, pr, f_grp[:, fbuf, :, fo:fo + hi - lo], ALU.mult).then_inc(near_done, 1)

            step(1, 1, 0)
            with pool.Fori(0, 2) as i:
                for j, (s, buf, _) in enumerate(step_args(i)):
                    step(s, buf, i + (1 + j) // NBUF)
            step(NG, NG % NBUF, (NG - 1) // NBUF, last=True)

            pool.wait_ge(init_out, 16 * E_NUM)
            for t in range(TT):
                if t in SPAN_STARTS:
                    pool.wait_ge(rows_ready, SPAN_STARTS[t] + 1)
                for k in range(2):
                    pool.indirect_dma_start(slots[:, :], bass.IndirectOffsetOnAxis(ap=slot_no[:, k, t:t + 1], axis=0),
                                            u_rows[:, t, :], None, bounds_check=E_NUM * CAP - 1,
                                            oob_is_err=False).then_inc(dispatched, 16)
            pool.wait_ge(base_out, 16)
            pool.wait_ge(trash_out, 16)

            def add_rows(e, i):
                pool.wait_ge(eo_done, 5 * (e + 1))
                if positive(e):
                    pool.wait_ge(added, 64 * e)
                    pool.sem_inc(add_turn, 1)
                for j in range(4):
                    pool.indirect_dma_start(out[:, :], bass.IndirectOffsetOnAxis(ap=e_tok[:, i, j:j + 1], axis=0),
                                            e_out[i][:, j, :], None, bounds_check=B * T + CAP - 1,
                                            oob_is_err=True, compute_op=ALU.add).then_inc(added, 16)

            add_rows(0, 0)
            add_rows(1, 1)
            with pool.Fori(1, E_NUM // 2) as k:
                for i in range(2):
                    add_rows(2 * k + i, i)
            pool.wait_ge(added, 64 * E_NUM)

        @block.scalar
        def _(act):
            act.dma_start(wide[:, 2 * T:], c_wide[:, 2 * T:]).then_inc(c_in, 16)
            act.dma_start(bcol[:, 0:1], bq.rearrange("(p a) -> p a", a=1)).then_inc(c_in, 16)
            act.dma_start(bcol[:, 1:2], bk.rearrange("(p a) -> p a", a=1)).then_inc(c_in, 16)
            act.dma_start(onehot[:, :], c_onehot[:, :]).then_inc(t_in, 16)
            act.dma_start(tab[:, :], table[:, :]).then_inc(t_in, 16)
            act.dma_start(vmask[:, :, :], c_mask[:, :, :]).then_inc(t_in, 16)
            act.dma_start(wide[:, 0:2 * T], c_wide[:, 0:2 * T]).then_inc(rope_in, 16)
            act.dma_start(bv_row[:, :], bass.AP(tensor=bv.tensor, offset=0, ap=[[0, P], [1, C]])).then_inc(rope_in, 16)
            def copy_xnT(c):
                act.wait_ge(xnT_ps, c + 1)
                if c >= 2:
                    act.wait_ge(v_ps, c - 1)
                act.activation(xnT[c % 2], ps_av[:, :], ACT.Copy).then_inc(xnT_sb, 1)

            act.wait_ge(vec_ps, 2)
            act.activation(g_sb, ps_st[0:H, 1, 0:NV], ACT.Exp, scale=SCALE).then_inc(vec_exp, 1)
            copy_xnT(0)
            for c in range(NCH):
                for i in range(2):
                    act.wait_ge(rope_done, 2 * c + i + 1)
                    if c >= 2:
                        act.wait_ge(parts_out[i][c % 2], 48 * (c // 2))
                    act.activation(part_f[i][c % 2][:, 0, :], qk_f[i], ACT.Copy).then_inc(part_hi, 1)
                    if i == 0 and c + 1 < NCH:
                        copy_xnT(c + 1)
                for i in range(2):
                    act.wait_ge(rest_done, 2 * c + i + 1)
                    act.activation(part_f[i][c % 2][:, 1, :], qk_rest[i], ACT.Copy).then_inc(part_mid, 1)

            def copy_v(n, buf):
                act.activation(v_grp[:, buf, :, :, 0:D],
                               v_all[:, bass.ds(n, 1), :].rearrange("p a (t g d) -> p (a t) g d", g=HG, d=D),
                               ACT.Copy).then_inc(v_copied, 1)

            def token_exp(b):
                act.wait_ge(ex_ready, b + 1)
                part = col(16, 9)[:, SPANS[b][0]:SPANS[b][1], :]
                act.activation(part, part, ACT.Exp).then_inc(ex_done, 1)

            def step(s, buf, fill, prev=True, do_s=True, last=False):
                for what in plan(prev, do_s, True, last):
                    if what[0] == "X":
                        token_exp(what[1])
                    if what[0] == "M":
                        copy_v(s, buf)
                    if what[0] == "ST":
                        u, g = what[1:]
                        qb, kt = UNITS[u]
                        c0 = first_col(qb, kt)
                        if g == 0 and (u >= PBUF or positive(NU * (s - 1))):
                            act.wait_ge(av_done, NU * (s - 1) + u - PBUF + 1)
                        n = HG * u + g
                        act.wait_ge(scores, 48 * (s - 1) + n + 1)
                        act.activation(probs[:, u % PBUF, g, c0:512], ps_st[:, n % 3, c0:512], ACT.Exp,
                                       scale=SCALE).then_inc(exp_done, 1)
                    if what[0] == "EVAC":
                        qb, back = what[1:]
                        act.wait_ge(av_done, NU * (s + back) - (NU - 4 if qb == 0 else 0))
                        old = 2 * (s + back - 1) + (1 if qb else -1)
                        if positive(old):
                            act.wait_ge(y_rcp_done, old)
                        act.activation(y_raw[:, qb, :], ps_av[:, :], ACT.Copy).then_inc(y_evac, 1)

            for j in range(N_FLIP):
                act.wait_ge(flip_ps, j + 1)
                act.activation(f_all[:, j * 512:(j + 1) * 512], flip_bank(j), ACT.Copy).then_inc(flip_sb, 1)
            act.wait_ge(flip_sb, N_FLIP)
            load_group(act, f_grp, f_all, 0, 0, factors_in)
            load_group(act, f_grp, f_all, 1, 1, factors_in)

            act.wait_ge(part_lo, 2 * NCH)
            for i in range(2):
                for j in range(2):
                    act.wait_ge(parts_out[i][j], 48 * NCH // 2)
            act.wait_ge(vec_out, 32)
            act.wait_ge(v_done, NCH)
            act.wait_ge(fixed, 1)
            copy_v(0, 0)
            step(1, 1, 0, prev=False)
            with act.Fori(0, 2) as i:
                for a in step_args(i):
                    step(*a)
            step(NG, NG % NBUF, 0, do_s=False, last=True)

            for kind, c in TOKENS_LAST:
                if kind == "X":
                    token_exp(c)
                elif kind == "F":
                    act.wait_ge(fgu_ps, c + 1)
                    if c >= 2:
                        act.wait_ge(f_act_done, c - 1)
                    act.activation(tmp_g[0:F4, c % 2, :], ps_st[0:F4, 2 * (c % 2), :], ACT.Gelu).then_inc(f_gelu, 1)

            def turned(e, i):
                act.wait_ge(eT_ps, e + 1)
                if positive(e - 1):
                    act.wait_ge(gu_ps, 2 * (e - 1))
                act.activation(slotT[i], ps_slot[:, 0, i * 512:(i + 1) * 512], ACT.Copy).then_inc(eT_sb, 1)

            def gelu(e, c):
                act.wait_ge(gu_ps, 2 * e + c + 1)
                if positive(2 * e + c - 1):
                    act.wait_ge(e_gated, 2 * e + c - 1)
                act.activation(tmp_g[:, c, :], ps_st[:, c, :], ACT.Gelu).then_inc(e_gelu, 1)

            act.wait_ge(f_act_done, NCH)
            turned(0, 0)
            gelu(0, 0)
            turned(1, 1)
            gelu(0, 1)
            gelu(1, 0)
            turned(2, 0)
            gelu(1, 1)
            with act.Fori(1, E_NUM // 2 - 1) as k:
                for i in range(2):
                    gelu(2 * k + i, 0)
                    turned(2 * k + i + 1, 1 - i)
                    gelu(2 * k + i, 1)
            gelu(E_NUM - 2, 0)
            turned(E_NUM - 1, 1)
            gelu(E_NUM - 2, 1)
            gelu(E_NUM - 1, 0)
            gelu(E_NUM - 1, 1)

        @block.tensor
        def _(pe):
            def keep_warm(n):
                some = wide[:, 2 * T:2 * T + 2 * P].bitcast(BF16)
                with pe.Fori(0, n):
                    pe.matmul(ps_av[:, :], ones_b[:, :], some, start=True, stop=True)

            pe.wait_ge(c_in, 48)
            pe.wait_ge(const_b, 4)
            keep_warm(WARM_FIRST)
            pe.wait_ge(t_in, 48)
            for v in range(2):
                pe.matmul(ps_st[0:H, 1 + v, 0:NV], tab[:, :], onehot[:, v * NV:(v + 1) * NV],
                          start=True, stop=True).then_inc(vec_ps, 1)
            pe.wait_ge(c_in, 48)
            for i in range(2):
                mm = pe.matmul(ps_st[:, 0, 2 * i:2 * i + 2], swap[:, i * P:(i + 1) * P], bcol[:, :], start=True, stop=True)
            mm.then_inc(bswap_ps, 1)
            pe.wait_ge(swapped, 6)
            pe.wait_ge(bswap_sb, 1)

            def turn_xn(c):
                pe.wait_ge(xn_done, CH * (c + 1))
                if c >= 1:
                    pe.wait_ge(xnT_sb, c)
                for t in range(CH):
                    mm = pe.transpose(ps_av[:, t * P:(t + 1) * P], xn[c % 2][:, t, :], ident)
                mm.then_inc(xnT_ps, 1)

            turn_xn(0)
            for c in range(NCH):
                pe.wait_ge(xnT_sb, c + 1)
                for i in range(2):
                    if c >= 1:
                        pe.wait_ge(rope_half, 4 * (c - 1) + 2 * i + 2)
                    pe.matmul(ps_slot[:, i, 0:512], w_attn[:, 4 + i, :], xnT[c % 2], start=True, stop=True)
                    pe.matmul(ps_slot[:, i, 512:1024], w_attn[:, 6 + i, :], xnT[c % 2], start=True,
                              stop=True).then_inc(qk_ps, 1)
                if c + 1 < NCH:
                    turn_xn(c + 1)
                if c >= 1:
                    pe.wait_ge(v_done, c)
                for t in range(CH):
                    mm = pe.matmul(ps_st[:, 0, t * P:(t + 1) * P], xnT[c % 2][:, t * P:(t + 1) * P], w_attn[:, 2, :],
                                   start=True, stop=True)
                mm.then_inc(v_ps, 1)

            def s_unit(s, buf, k, slot, su):
                t, heads = SUNITS[su]
                w = (t + 1) * P
                if positive(k - 1):
                    pe.wait_ge(slot_used, k - 1)
                for j, g in enumerate(heads):
                    o = s_offset(t, j)
                    b0 = max(0, (t - 1) * P)
                    for lo in range(0, w, 512):
                        hi = min(w, lo + 512)
                        nlo, nhi = max(lo, b0), hi
                        pe.matmul(ps_slot[:, slot, o + lo:o + hi], q_stack[:, buf, g, t * P:(t + 1) * P],
                                  k_stack[:, buf, g, lo:hi], start=True, stop=(nlo >= nhi))
                        if nlo < nhi:
                            f0 = nlo - (t - 1) * P
                            mm = pe.matmul(ps_slot[:, slot, o + nlo:o + nhi], flip_b[:, :],
                                           b_grp[:, buf, g, f0:f0 + nhi - nlo], start=False, stop=True)
                mm.then_inc(slot_full, 1)

            unit_at = {}

            def token_unit(what, k, slot):
                kind, c = what
                unit_at[what] = k
                pe.wait_ge(slot_used, k - 1)
                if kind == "A":
                    if c >= 2:
                        pe.wait_ge(slot_used, unit_at["Y", c % 2] + 1)
                    for t in range(CH):
                        mm = pe.transpose(ps_slot[:, slot, t * P:(t + 1) * P],
                                          y_all[:, c * CH + t, :, :].rearrange("p a c -> p (a c)"), ident)
                elif kind == "B":
                    pe.wait_ge(slot_used, unit_at["A", c] + 1)
                    for t in range(CH):
                        mm = pe.matmul(ps_slot[:, slot, t * P:(t + 1) * P], yT[c % 2][:, t * P:(t + 1) * P],
                                       w_attn[:, 3, :], start=True, stop=True)
                elif kind == "C":
                    pe.wait_ge(u_done, CH * (c + 1))
                    for t in range(CH):
                        mm = pe.transpose(ps_slot[:, slot, t * P:(t + 1) * P], u_rows[:, c * CH + t, 0:C], ident)
                elif kind == "D":
                    first, end = SPANS[c]
                    for t in range(end - first):
                        tile = first + t
                        if tile % CH == 0:
                            pe.wait_ge(slot_used, unit_at["C", tile // CH] + 1)
                        mm = pe.matmul(ps_slot[:, slot, t * E_NUM:(t + 1) * E_NUM], uT[:, tile * P:(tile + 1) * P],
                                       router[:, :], start=True, stop=True)
                else:
                    pe.wait_ge(sel_done, c + 1)
                    first, end = SPANS[c]
                    w = (end - first) * E_NUM
                    pe.matmul(ps_slot[:, slot, 0:w], below_b[:, :], sel_b[:, first * E_NUM:end * E_NUM],
                              start=True, stop=False)
                    for t in range(1, end):
                        lo = max(first, t)
                        mm = pe.matmul(ps_slot[:, slot, (lo - first) * E_NUM:w], ones_b[:, :],
                                       sel_b[:, (lo - t) * E_NUM:(end - t) * E_NUM], start=False, stop=(t == end - 1))
                mm.then_inc(slot_full, 1)

            def step(s, buf, fill, prev=True, do_s=True, do_t=True, last=False):
                tbuf = (buf - 1) % NBUF
                k, slot = slot_base(s), base_parity(s)
                n_slot = 0
                if do_s:
                    pe.wait_ge(stack_in[buf], STACK_IN * (fill + 1))
                for what in plan(prev, do_s, do_t, last):
                    if what[0] == "ST":
                        u, g = what[1:]
                        qb, kt = UNITS[u]
                        c0 = first_col(qb, kt)
                        n = HG * u + g
                        if n == 0:
                            pe.wait_ge(mrows_in, 16 * s)
                        if n >= 3 or positive(48 * (s - 1)):
                            pe.wait_ge(exp_done, 48 * (s - 1) + n - 2)
                        pe.matmul(ps_st[:, n % 3, c0:512], k_stack[:, tbuf, g, kt * P:(kt + 1) * P],
                                  q_stack[:, tbuf, g, qb * 512 + c0:qb * 512 + 512],
                                  start=True, stop=True).then_inc(scores, 1)
                    elif what[0] == "AV":
                        u, back = what[1:]
                        qb, kt = UNITS[u]
                        c0 = first_col(qb, kt)
                        vb = (tbuf + back) % NBUF
                        n = s - 1 + back
                        if last and back == 0 and u in LAST_NEAR:
                            pe.wait_ge(last_near_done, LAST_NEAR.index(u) + 1)
                        elif u in NEAR:
                            others = sum(v < u for v in LAST_NEAR) if last and back == 0 else 0
                            pe.wait_ge(near_done, NN * n + NEAR.index(u) + 1 - others)
                        else:
                            pe.wait_ge(exp_done, 48 * n + HG * (u + 1))
                        if u in (0, 4) and positive(2 * n + (u == 4)):
                            pe.wait_ge(y_evac, 2 * n + (1 if u == 4 else 0))
                        if u == 0:
                            pe.wait_ge(v_copied, n + 1)
                        for g in range(HG):
                            mm = pe.matmul(ps_av[32 * g:32 * g + VW, c0:512], v_grp[:, vb, kt, g, :],
                                           probs[:, u % PBUF, g, c0:512], start=(u in (0, 4)), stop=(u in (3, 11)),
                                           skip_group_check=True)
                        mm.then_inc(av_done, 1)
                    elif what[0] == "FLIP":
                        j = what[1]
                        if j >= 4:
                            pe.wait_ge(flip_sb, j - 3)
                        pe.matmul(flip_bank(j), flip, f_all[:, j * 512:(j + 1) * 512], start=True, stop=True).then_inc(flip_ps, 1)
                    elif what[0] == "S":
                        s_unit(s, buf, k + n_slot, (slot + n_slot) % 2, what[1])
                        n_slot += 1
                    elif what[0] == "Y":
                        qb, back = what[1:]
                        if last and back == 0:
                            unit_at["Y", qb] = k + n_slot
                        pe.wait_ge(y_evac, 2 * (s - 1 + back) + qb + 1)
                        pe.wait_ge(slot_used, k + n_slot - 1)
                        for t in range(CH):
                            mm = pe.transpose(ps_slot[:, (slot + n_slot) % 2, t * P:(t + 1) * P],
                                              y_raw[:, qb, t * P:(t + 1) * P], ident)
                        mm.then_inc(slot_full, 1)
                        n_slot += 1
                    elif what[0] in "ABCDE":
                        token_unit(what, k + n_slot, (slot + n_slot) % 2)
                        n_slot += 1
                    elif what[0] == "M":
                        pe.wait_ge(msplit, 4 * (s + 1))
                        pe.wait_ge(slot_used, k + n_slot - 1)
                        pe.transpose(ps_slot[0:3 * HG * TPB, (slot + n_slot) % 2, 0:P // 2].bitcast(BF16),
                                     max_parts[:, :, :].rearrange("p a n -> p (a n)"), ident_b[:, :]).then_inc(slot_full, 1)
                        n_slot += 1
                return k + n_slot

            pe.wait_ge(rope_half, 4 * NCH)
            pe.wait_ge(v_done, NCH)
            pe.wait_ge(vec_done, 2)
            pe.wait_ge(toep_in, 32)
            pe.wait_ge(ones_in, 16)
            pe.wait_ge(xnT_sb, NCH)
            keep_warm(WARM_STACK)
            step(0, 0, 0, prev=False, do_t=False)
            pe.wait_ge(flip_sb, N_FLIP)
            step(1, 1, 0, prev=False)
            with pe.Fori(0, 2) as i:
                for a in step_args(i):
                    step(*a)
            k = step(NG, NG % NBUF, 0, do_s=False, last=True)

            for what in TOKENS_LAST:
                kind, c = what
                if kind == "F":
                    if c == 0:
                        pe.wait_ge(fw_done, 1)
                        pe.wait_ge(exp_done, 48 * NG)
                        pe.wait_ge(y_evac, 2 * NG)
                        pe.wait_ge(slot_used, unit_at["C", 1] + 1)
                    if c >= 2:
                        pe.wait_ge(f_act_done, c - 1)
                    up = ps_st[0:F4, 1, :] if c % 2 == 0 else ps_av[0:F4, :]
                    pe.matmul(ps_st[0:F4, 2 * (c % 2), :], fw[:, 0:F4], uT[:, c * CW:(c + 1) * CW], start=True, stop=True)
                    pe.matmul(up, fw[:, F4:2 * F4], uT[:, c * CW:(c + 1) * CW], start=True, stop=True).then_inc(fgu_ps, 1)
                elif kind == "G":
                    pe.wait_ge(slot_used, k)
                    pe.wait_ge(f_act_done, c + 1)
                    for t in range(CH):
                        tile = c * CH + t
                        mm = pe.matmul(ps_slot[:, tile // 8, (tile % 8) * C:(tile % 8 + 1) * C],
                                       f_act[c][0:F4, t * P:(t + 1) * P], fw[0:F4, 2 * F4:2 * F4 + C],
                                       start=True, stop=True)
                    mm.then_inc(f_ps, 1)
                elif kind != "X":
                    token_unit(what, k, k % 2)
                    k += 1

            def turn(e, i, n):
                pe.wait_ge(es_in[i], 16 * (n + 1))
                if positive(e - 1):
                    pe.wait_ge(eT_sb, e - 1)
                for j in range(4):
                    mm = pe.transpose(ps_slot[:, 0, i * 512 + j * P:i * 512 + (j + 1) * P], slot_in[i][:, j, 0:C], ident)
                mm.then_inc(eT_ps, 1)

            def gate_up(e, i, c):
                pe.wait_ge(eT_sb, e + 1)
                pe.wait_ge(ew_done, 2 * (e + 1))
                if positive(2 * e + c - 1):
                    pe.wait_ge(e_gated, 2 * e + c - 1)
                pe.matmul(ps_st[:, c, :], wgu[i][:, c * P:(c + 1) * P], slotT[i], start=True, stop=True)
                up = ps_st[:, 2, :] if c == 0 else ps_av[:, :]
                pe.matmul(up, wgu[i][:, FF + c * P:FF + (c + 1) * P], slotT[i], start=True,
                          stop=True).then_inc(gu_ps, 1)

            def down(e, i):
                pe.wait_ge(e_gated, 2 * (e + 1))
                for j in range(4):
                    for c in range(2):
                        mm = pe.matmul(ps_slot[:, 1, i * 512 + j * C:i * 512 + (j + 1) * C],
                                       gated[i][:, c, j * P:(j + 1) * P],
                                       wd_all[:, bass.ds(2 * e + c, 1), :].rearrange("p a c -> p (a c)"),
                                       start=(c == 0), stop=(c == 1))
                mm.then_inc(eo_ps, 1)

            keep_warm(WARM_SLOTS)
            pe.wait_ge(base_done, TT // 2)
            turn(0, 0, 0)
            gate_up(0, 0, 0)
            turn(1, 1, 0)
            gate_up(0, 0, 1)
            pe.wait_ge(base_done, TT)
            with pe.Fori(0, E_NUM // 2 - 1) as k:
                gate_up(2 * k + 1, 1, 0)
                down(2 * k, 0)
                turn(2 * k + 2, 0, k + 1)
                gate_up(2 * k + 1, 1, 1)
                gate_up(2 * k + 2, 0, 0)
                down(2 * k + 1, 1)
                turn(2 * k + 3, 1, k + 1)
                gate_up(2 * k + 2, 0, 1)
            gate_up(E_NUM - 1, 1, 0)
            down(E_NUM - 2, 0)
            gate_up(E_NUM - 1, 1, 1)
            down(E_NUM - 1, 1)

        @block.vector
        def _(dve):
            dve.wait_ge(c_in, 48)
            dve.tensor_copy(ident_b[:, :], ident).then_inc(const_b, 1)
            dve.tensor_copy(flip_b[:, :], flip).then_inc(const_b, 1)
            dve.tensor_copy(below_b[:, :], below).then_inc(const_b, 1)

            own = [0]

            def after(ins):
                own[0] += 1
                ins.then_inc(in_order, 1)
                dve.wait_ge(in_order, own[0])

            def rsqrt(dst, v, t):
                after(dve.tensor_scalar(dst.bitcast(U32), v.bitcast(U32), 1, None, ALU.logical_shift_right))
                after(dve.tensor_scalar(dst.bitcast(I32), dst.bitcast(I32), -1.0, float(0x5F3759DF), ALU.mult, ALU.add))
                for _ in range(3):
                    after(dve.tensor_tensor(t, dst, dst, ALU.mult))
                    after(dve.scalar_tensor_tensor(out=t, in0=t, scalar=-0.5, in1=v, op0=ALU.mult, op1=ALU.mult))
                    after(dve.scalar_tensor_tensor(out=dst, in0=t, scalar=1.5, in1=dst, op0=ALU.add, op1=ALU.mult))

            stat_count = [0]

            def norm_stats(src, tiles):
                for t in tiles:
                    dve.bn_stats(stats[:, t, :], src[:, t, :]).then_inc(st_done, 1)
                stat_count[0] += len(tiles)
                dve.wait_ge(st_done, stat_count[0])
                for t in tiles:
                    dve.bn_aggr(mv[:, t, :], stats[:, t, :]).then_inc(mv_done, 1)
                dve.wait_ge(mv_done, stat_count[0])

            def first_norm(tiles):
                norm_stats(x_sb, tiles)
                r, n = slice(tiles[0], tiles[-1] + 1), len(tiles)
                after(dve.tensor_scalar(newton[:, 0, 0:n], mv[:, r, 1], LN_EPS, None, ALU.add))
                rsqrt(rstd[:, 0, r], newton[:, 0, 0:n], newton[:, 1, 0:n])

            def normalise(c):
                if c >= 2:
                    dve.wait_ge(xnT_ps, c - 1)
                for t in range(CH):
                    tile = c * CH + t
                    dve.tensor_scalar(xn[c % 2][:, t, :], x_sb[:, tile, :], mv[:, tile, 0:1], rstd[:, 0, tile:tile + 1],
                                      ALU.subtract, ALU.mult).then_inc(xn_done, 1)

            dve.wait_ge(x_in[0], 16)
            dve.wait_ge(x_in[1], 16)
            first_norm(range(TPB))
            normalise(0)
            normalise(1)
            dve.wait_ge(vec_exp, 1)
            dve.wait_ge(t_in, 48)
            dve.tensor_tensor(g_sb, g_sb, vmask[:, 0, :], ALU.mult).then_inc(vec_done, 1)
            dve.tensor_tensor(r_sb, ps_st[0:H, 2, 0:NV], vmask[:, 1, :], ALU.add).then_inc(vec_done, 1)
            dve.wait_ge(bswap_ps, 1)
            dve.tensor_copy(bcol_perm[:, :], ps_st[:, 0, 0:4]).then_inc(bswap_sb, 1)
            dve.wait_ge(x_in[2], 16)
            dve.wait_ge(x_in[3], 16)
            first_norm(range(TPB, TT))
            dve.wait_ge(bswap_sb, 1)
            dve.wait_ge(rope_in, 32)
            for c in range(NCH):
                tok = (c % 2) * CW
                for i in range(2):
                    n = 2 * c + i
                    dve.wait_ge(qk_ps, n + 1)
                    if n >= 1:
                        dve.wait_ge(rope_done, n)
                    dve.scalar_tensor_tensor(out=rope_a, in0=ps_slot[:, i, 0:512], scalar=bcol_perm[:, i:i + 1],
                                             in1=cos_t[:, tok:tok + CW], op0=ALU.add, op1=ALU.mult).then_inc(rope_half, 1)
                    dve.scalar_tensor_tensor(out=rope_b, in0=ps_slot[:, i, 512:1024], scalar=bcol_perm[:, 2 + i:3 + i],
                                             in1=sin_t[:, tok:tok + CW], op0=ALU.add, op1=ALU.mult).then_inc(rope_half, 1)
                    dve.wait_ge(rope_half, 2 * n + 2)
                    if c >= 1:
                        dve.wait_ge(rest_done, 2 * (c - 1) + i + 1)
                    dve.tensor_tensor(qk_f[i], rope_a, rope_b, ALU.add).then_inc(rope_done, 1)
                if c + 2 < NCH:
                    normalise(c + 2)
                dve.wait_ge(v_ps, c + 1)
                b, kt = c // 2, (c % 2) * CH
                dst = v_all[:, b * 4:b * 4 + 4, kt * HG * D:(kt + CH) * HG * D].rearrange("p n (t c) -> p t n c", t=CH)
                dve.tensor_tensor(dst, ps_st[:, 0, :].rearrange("p (t n c) -> p t n c", t=CH, n=4),
                                  bass.AP(tensor=bv_row, offset=0, ap=[[C, P], [0, CH], [HG * D, 4], [1, HG * D]]),
                                  ALU.add).then_inc(v_done, 1)

            def step(s, buf, fill, prev=True, do_s=True, do_t=True, last=False):
                k, slot = slot_base(s), base_parity(s)
                n_slot, n_max = 0, 0
                for what in plan(prev, do_s, do_t, last):
                    if what[0] == "NEAR":
                        u = what[1]
                        lo, hi, fo = near(*UNITS[u])
                        dve.wait_ge(exp_done, 48 * (s - 1) + HG * (u + 1))
                        pr = probs[:, u % PBUF, :, lo:hi]
                        dve.scalar_tensor_tensor(out=pr, in0=pr, scalar=BIG,
                                                 in1=f_grp[:, (buf - 1) % NBUF, :, fo:fo + hi - lo],
                                                 op0=ALU.min, op1=ALU.mult).then_inc(last_near_done, 1)
                    if what[0] not in "SYMABCDE":
                        continue
                    here = (slot + n_slot) % 2
                    if what[0] in "ABCDE":
                        token_unit(what, k + n_slot, here)
                    elif what[0] == "S":
                        t, heads = SUNITS[what[1]]
                        w = (t + 1) * P
                        pitch = s_offset(t, 1)
                        src = ps_slot[:, here, 0:pitch * len(heads)].rearrange("p (g w) -> p g w", w=pitch)[:, :, 0:w] \
                            if len(heads) > 1 else ps_slot[:, here, 0:w]
                        dve.wait_ge(slot_full, k + n_slot + 1)
                        dve.tensor_reduce(neg_max[:, heads[0]:heads[-1] + 1, t], src, AX.X, ALU.max,
                                          negate=True).then_inc(slot_used, 1)
                        n_max += 1
                        if n_max == len(SUNITS):
                            flat = neg_max[:, :, :].rearrange("p g t -> p (g t)")
                            dve.wait_ge(slot_used, k + n_slot + 1)
                            dve.tensor_copy(max_parts[:, 0, :], flat).then_inc(msplit, 1)
                            dve.wait_ge(msplit, 4 * s + 1)
                            dve.tensor_tensor(max_rest[:, :], flat, max_parts[:, 0, :], ALU.subtract).then_inc(msplit, 1)
                            dve.wait_ge(msplit, 4 * s + 2)
                            dve.tensor_copy(max_parts[:, 1, :], max_rest[:, :]).then_inc(msplit, 1)
                            dve.wait_ge(msplit, 4 * s + 3)
                            dve.tensor_tensor(max_parts[:, 2, :], max_rest[:, :], max_parts[:, 1, :],
                                              ALU.subtract).then_inc(msplit, 1)
                    elif what[0] == "M":
                        dve.wait_ge(slot_full, k + n_slot + 1)
                        if positive(16 * s):
                            dve.wait_ge(mrows_in, 16 * s)
                        dve.tensor_copy(max_rows[:, :], ps_slot[0:3 * HG * TPB, here, 0:P // 2].bitcast(BF16))\
                           .then_inc(mrows_sb, 1)
                        dve.wait_ge(mrows_sb, s + 1)
                        dve.sem_inc(slot_used, 1)
                    else:
                        qb, back = what[1:]
                        n = s - 1 + back
                        src = ps_slot[:, here, 0:512].rearrange("p (t g c) -> p t g c", t=CH, g=HG)
                        dve.wait_ge(slot_full, k + n_slot + 1)
                        dve.reciprocal(y_rcp[:, qb, :, :], src[:, :, :, D]).then_inc(y_rcp_done, 1)
                        dve.wait_ge(y_rcp_done, 2 * n + qb + 1)
                        hg = n % (H // HG)
                        dst = y_all[:, bass.ds((n // (H // HG)) * TPB + CH * qb, CH), bass.ds(hg, 1), :]
                        rc = y_rcp[:, qb, :, :].rearrange("p t (g a) -> p t g a", a=1)
                        rc = bass.AP(tensor=rc.tensor, offset=rc.offset, ap=[list(a) for a in rc.ap[:-1]] + [[0, D]])
                        dve.tensor_tensor(dst.rearrange("p t a (g d) -> p t (a g) d", g=HG), src[:, :, :, 0:D], rc,
                                          ALU.mult).then_inc(slot_used, 1)
                    n_slot += 1
                return k + n_slot

            def wide_col(a, n):
                return bass.AP(tensor=a.tensor, offset=a.offset, ap=[list(d) for d in a.ap[:-1]] + [[0, n]])

            RINV, W1, W2, S1, OVF, IDX1, IDX2, BASE1, BASE2, POS1, POS2, O1, O2, SUM = range(14)
            EXPS, ONE1, ONE2, LG = 16, 25, 33, 41

            def token_unit(what, k, slot):
                kind, c = what
                src = ps_slot[:, slot, 0:CW]
                dve.wait_ge(slot_full, k + 1)
                if kind == "A":
                    dve.tensor_copy(yT[c % 2], src).then_inc(slot_used, 1)
                elif kind == "B":
                    x_c = x_sb[:, c * CH:(c + 1) * CH, :]
                    dve.wait_ge(xb_done, 1)
                    dve.tensor_tensor(x_c, src.rearrange("p (t c) -> p t c", t=CH), x_c, ALU.add).then_inc(slot_used, 1)
                    dve.wait_ge(slot_used, k + 1)
                    norm_stats(x_sb, range(c * CH, (c + 1) * CH))
                    if c in SPAN_ENDS:
                        second_norm(*SPANS[SPAN_ENDS[c]])
                elif kind == "C":
                    dve.tensor_copy(uT[:, c * CW:(c + 1) * CW], src).then_inc(slot_used, 1)
                elif kind == "D":
                    choose(c, k, ps_slot[:, slot, 0:(SPANS[c][1] - SPANS[c][0]) * E_NUM])
                    if c == 1:
                        probabilities(c)
                else:
                    if c == 0:
                        probabilities(c)
                    positions(c, k, ps_slot[:, slot, 0:(SPANS[c][1] - SPANS[c][0]) * E_NUM])

            def second_norm(first, end):
                r, n = slice(first, end), end - first

                v, t = newton[:, 0:2, 0:n], newton[:, 2:4, 0:n]
                dve.tensor_scalar(v[:, 0, :], mv[:, r, 1], LN_EPS, None, ALU.add)
                after(dve.tensor_scalar(v[:, 1, :], mv[:, r, 1], 1.0 + RMS_EPS, LN_EPS * RMS_EPS, ALU.mult, ALU.add))
                rsqrt(rstd[:, :, r], v, t)
                for i in range(first, end):
                    dve.tensor_scalar(u_rows[:, i, 0:C], x_sb[:, i, :], mv[:, i, 0:1], rstd[:, 1, i:i + 1],
                                      ALU.subtract, ALU.mult).then_inc(u_done, 1)
                rinv = small[:, RINV * TT:(RINV + 1) * TT][:, r]
                after(dve.tensor_tensor(t[:, 0, :], rstd[:, 0, r], rstd[:, 1, r], ALU.mult))
                after(dve.tensor_tensor(rinv, t[:, 0, :], v[:, 1, :], ALU.mult))

            def views(b):
                r = slice(*SPANS[b])
                return (lambda i: small[:, i * TT:(i + 1) * TT][:, r],
                        lambda i: small[:, i * TT:(i + 1) * TT][:, r].rearrange("p (t a) -> p t a", a=1),
                        lambda i: col(i, 8)[:, r, :])

            def choose(b, k, logits):
                arr, arr3, arr8 = views(b)
                r = slice(*SPANS[b])
                ins = dve.tensor_tensor(arr8(LG), logits.rearrange("p (t e) -> p t e", e=E_NUM),
                                        wide_col(arr3(RINV), E_NUM), ALU.mult)
                ins.then_inc(slot_used, 1)
                dve.wait_ge(slot_used, k + 1)
                first, end = SPANS[b]
                for t in range(first, end):
                    ins = dve.max(mx8[:, t, :], arr8(LG)[:, t - first, :])
                after(ins)
                for t in range(first, end):
                    ins = dve.max_index(ix8[:, t, :], mx8[:, t, :], arr8(LG)[:, t - first, :])
                ex = col(EXPS, 9)[:, r, :]
                dve.tensor_tensor(ex[:, :, 0:8], arr8(LG), wide_col(mx8[:, r, 0:1], E_NUM), ALU.subtract)
                after(dve.tensor_tensor(ex[:, :, 8:9], mx8[:, r, 1:2], mx8[:, r, 0:1], ALU.subtract))
                dve.sem_inc(ex_ready, 1)
                dve.tensor_copy(arr3(IDX1), ix8[:, r, 0:1])
                after(dve.tensor_copy(arr3(IDX2), ix8[:, r, 1:2]))
                eno = bass.AP(tensor=expert_no.tensor, offset=expert_no.offset,
                              ap=[list(expert_no.ap[0]), [0, end - first], [1, E_NUM]])
                dve.tensor_tensor(arr8(ONE1), wide_col(arr3(IDX1), E_NUM), eno, ALU.is_equal)
                after(dve.tensor_tensor(arr8(ONE2), wide_col(arr3(IDX2), E_NUM), eno, ALU.is_equal))
                dve.tensor_tensor(sel_b[:, first * E_NUM:end * E_NUM].rearrange("p (t e) -> p t e", e=E_NUM),
                                  arr8(ONE1), arr8(ONE2), ALU.add).then_inc(sel_done, 1)
                urow = u_rows[:, r, :]
                for idx_i in (IDX1, IDX2):
                    dve.tensor_scalar(arr(idx_i + 2), arr(idx_i), float(CAP), None, ALU.mult)
                dve.tensor_copy(urow[:, :, C + 2:C + 3], arr3(IDX1))
                dve.tensor_copy(urow[:, :, C + 3:C + 4], token_no[:, r].rearrange("p (t a) -> p t a", a=1))

            def probabilities(b):
                arr, arr3, arr8 = views(b)
                r = slice(*SPANS[b])
                dve.wait_ge(ex_done, b + 1)
                after(dve.tensor_reduce(arr(SUM), col(EXPS, 9)[:, r, 0:8], AX.X, ALU.add))
                after(dve.reciprocal(arr(W1), arr(SUM)))
                after(dve.tensor_tensor(arr3(W2), col(EXPS, 9)[:, r, 8:9], arr3(W1), ALU.mult))

            def positions(b, k, counts):
                arr, arr3, arr8 = views(b)
                r = slice(*SPANS[b])
                pos = counts.rearrange("p (t e) -> p t e", e=E_NUM)
                dve.tensor_tensor(arr8(ONE1), arr8(ONE1), pos, ALU.mult)
                after(dve.tensor_tensor(arr8(ONE2), arr8(ONE2), pos, ALU.mult))
                dve.sem_inc(slot_used, 1)
                dve.tensor_reduce(arr(POS1), arr8(ONE1), AX.X, ALU.add)
                after(dve.tensor_reduce(arr(POS2), arr8(ONE2), AX.X, ALU.add))
                dve.tensor_scalar(arr(O1), arr(POS1), float(CAP), None, ALU.is_ge)
                dve.tensor_scalar(arr(O2), arr(POS2), float(CAP), None, ALU.is_ge)
                dve.tensor_tensor(arr(BASE1), arr(BASE1), arr(POS1), ALU.add)
                after(dve.tensor_tensor(arr(BASE2), arr(BASE2), arr(POS2), ALU.add))
                dve.tensor_tensor(arr(OVF), arr(O1), arr(O2), ALU.max)
                dve.scalar_tensor_tensor(out=slot_no[:, 0, r], in0=arr(O1), scalar=FAR, in1=arr(BASE1),
                                         op0=ALU.mult, op1=ALU.add)
                after(dve.scalar_tensor_tensor(out=slot_no[:, 1, r], in0=arr(O2), scalar=FAR, in1=arr(BASE2),
                                               op0=ALU.mult, op1=ALU.add))
                urow = u_rows[:, r, :]
                for n, w_i in enumerate((W1, W2)):
                    ins = dve.scalar_tensor_tensor(out=urow[:, :, C + n:C + n + 1], in0=arr3(OVF), scalar=0.0,
                                                   in1=arr3(w_i), op0=ALU.is_equal, op1=ALU.mult)
                after(ins)
                dve.sem_inc(rows_ready, 1)

            step(0, 0, 0, prev=False, do_t=False)
            step(1, 1, 0, prev=False)
            with dve.Fori(0, 2) as i:
                for a in step_args(i):
                    step(*a)

            dve.wait_ge(v_copied, NG)
            dve.wait_ge(factors_in[(NG - 1) % NBUF], 16 * ((NG - 1) // NBUF + 1))
            dve.wait_ge(fw_in, 48)
            dve.wait_ge(late_in, 64)
            dve.tensor_scalar(fw[:, 0:2 * F4], fw[:, 0:2 * F4], fn_col[:, 0:1], None, ALU.mult).then_inc(fw_done, 1)
            k = step(NG, NG % NBUF, 0, do_s=False, last=True)
            for what in TOKENS_LAST:
                if what[0] in "ABCDE":
                    token_unit(what, k, k % 2)
                    k += 1

            def arr(i):
                return small[:, i * TT:(i + 1) * TT]

            def arr3(i):
                return small[:, i * TT:(i + 1) * TT].rearrange("p (t a) -> p t a", a=1)

            def fallback_act(c):
                dve.wait_ge(f_gelu, c + 1)
                up = ps_st[0:F4, 1, :] if c % 2 == 0 else ps_av[0:F4, :]
                dve.tensor_tensor(f_act[c][0:F4, :], tmp_g[0:F4, c % 2, :], up, ALU.mult).then_inc(f_act_done, 1)

            for c in (0, 1):
                fallback_act(c)
            after(dve.tensor_tensor(arr3(S1), u_rows[:, :, C:C + 1], u_rows[:, :, C + 1:C + 2], ALU.add))
            after(dve.tensor_scalar(arr(S1), arr(S1), 1.0, None, ALU.add))
            after(dve.tensor_tensor(arr(S1), arr(S1), arr(RINV), ALU.mult))
            for t in range(TT):
                dve.scalar_tensor_tensor(out=x1[:, t, :], in0=u_rows[:, t, 0:C], scalar=arr(S1)[:, t:t + 1],
                                         in1=x1[:, t, :], op0=ALU.mult, op1=ALU.add).then_inc(base1, 1)
                if t in (CH, 2 * CH):
                    fallback_act(1 + t // CH)
            dve.wait_ge(f_ps, NCH)
            for t in range(TT):
                dve.wait_ge(base1, t + 1)
                dve.scalar_tensor_tensor(out=x1[:, t, :], in0=ps_slot[:, t // 8, (t % 8) * C:(t % 8 + 1) * C],
                                         scalar=arr(OVF)[:, t:t + 1], in1=x1[:, t, :], op0=ALU.mult,
                                         op1=ALU.add).then_inc(base_done, 1)

            def fold_norm(e, i):
                if positive(e - 1):
                    dve.wait_ge(gu_ps, 2 * (e - 1))
                for half, src in ((0, wg_all), (1, wu_all)):
                    dve.tensor_scalar(wgu[i][:, half * FF:(half + 1) * FF],
                                      src[:, bass.ds(e, 1), :].rearrange("p a f -> p (a f)"),
                                      e_norm[:, bass.ds(e, 1)], None, ALU.mult).then_inc(ew_done, 1)

            def weights_of_rows(e, i, n):
                dve.wait_ge(es_in[i], 16 * (n + 1))
                dve.wait_ge(eT_ps, e + 1)
                if positive(e - 1):
                    dve.wait_ge(eo_done, 5 * (e - 1))
                a1, a2 = slot_in[i][:, :, C], slot_in[i][:, :, C + 1]
                dve.tensor_copy(e_row_tok[:, i, :], slot_in[i][:, :, C + 3]).then_inc(ewt, 1)
                dve.tensor_scalar(e_wt[:, i, 0, :], slot_in[i][:, :, C + 2], expert_no[:, bass.ds(e, 1)], None,
                                  ALU.is_equal).then_inc(ewt, 1)
                dve.tensor_tensor(e_wt[:, i, 1, :], a1, a2, ALU.subtract).then_inc(ewt, 1)
                dve.wait_ge(ewt, 3 * e + 3)
                dve.tensor_tensor(e_wt[:, i, 2, :], e_wt[:, i, 0, :], e_wt[:, i, 1, :], ALU.mult).then_inc(ewt_done, 1)
                dve.wait_ge(ewt_done, 2 * e + 1)
                dve.tensor_tensor(e_wt[:, i, 2, :], e_wt[:, i, 2, :], a2, ALU.add).then_inc(ewt_done, 1)
                dve.wait_ge(ewt_done, 2 * e + 2)

            def gate(e, i, c):
                dve.wait_ge(e_gelu, 2 * e + c + 1)
                up = ps_st[:, 2, :] if c == 0 else ps_av[:, :]
                dve.tensor_tensor(gated[i][:, c, :], tmp_g[:, c, :], up, ALU.mult).then_inc(e_gated, 1)

            def scale_rows(e, i):
                dve.wait_ge(eo_ps, e + 1)
                if positive(e - 1):
                    dve.wait_ge(added, 64 * (e - 1))
                dve.tensor_copy(e_tok[:, i, :], e_row_tok[:, i, :]).then_inc(eo_done, 1)
                for j in range(4):
                    dve.tensor_scalar(e_out[i][:, j, :], ps_slot[:, 1, i * 512 + j * C:i * 512 + (j + 1) * C], e_wt[:, i, 2, j:j + 1], None,
                                      ALU.mult).then_inc(eo_done, 1)

            dve.wait_ge(ew_in, 48)
            fold_norm(0, 0)
            fold_norm(1, 1)
            weights_of_rows(0, 0, 0)
            gate(0, 0, 0)
            weights_of_rows(1, 1, 0)
            gate(0, 0, 1)
            fold_norm(2, 0)
            gate(1, 1, 0)
            scale_rows(0, 0)
            gate(1, 1, 1)
            weights_of_rows(2, 0, 1)
            fold_norm(3, 1)
            gate(2, 0, 0)
            scale_rows(1, 1)
            gate(2, 0, 1)
            weights_of_rows(3, 1, 1)
            with dve.Fori(1, E_NUM // 2 - 1) as k:
                fold_norm(2 * k + 2, 0)
                gate(2 * k + 1, 1, 0)
                scale_rows(2 * k, 0)
                gate(2 * k + 1, 1, 1)
                weights_of_rows(2 * k + 2, 0, k + 1)
                fold_norm(2 * k + 3, 1)
                gate(2 * k + 2, 0, 0)
                scale_rows(2 * k + 1, 1)
                gate(2 * k + 2, 0, 1)
                weights_of_rows(2 * k + 3, 1, k + 1)
            gate(E_NUM - 1, 1, 0)
            scale_rows(E_NUM - 2, 0)
            gate(E_NUM - 1, 1, 1)
            scale_rows(E_NUM - 1, 1)


def shape_constants():
    import math

    import numpy as np

    inv = (1.0 / np.float32(10000.0) ** (np.arange(0, D, 2, dtype=np.float32) / np.float32(D))).astype(np.float32)
    ang = np.arange(T, dtype=np.float32)[None, :] * inv[:, None]
    d_of = (np.arange(P) % (HG * D)) // HG
    ang = ang[d_of % (D // 2)]
    sign = np.where(d_of < D // 2, -1.0, 1.0)[:, None]
    k, m = np.arange(P)[:, None], np.arange(P)[None, :]
    head = m // (HG * D) * HG + m % HG
    d_m = (m % (HG * D)) // HG
    plain, swap = k == head * D + d_m, k == head * D + (d_m + D // 2) % D
    wide = np.concatenate([np.cos(ang), np.sin(ang) * sign, k == m, k < m, plain, swap, k + m == P - 1,
                           np.broadcast_to(np.arange(E_NUM), (P, E_NUM)),
                           np.arange(TT)[None, :] * P + k], axis=1).astype(np.float32)

    def bucket(n):
        big = 16 + int(math.log(max(n, 1) / 16) / math.log(8) * 16) if n >= 16 else n
        return min(big, NB - 1)

    onehot = np.zeros((NB, 2, NV), np.float32)
    mask = np.zeros((H, 2, NV), np.float32)
    for y in range(NV):
        for v, n in ((0, y - (P - 1)), (1, 2 * P - 1 - y)):
            if n >= 0:
                onehot[bucket(n), v, y] += 1
                onehot[NB - 1, v, y] -= 1
                mask[:, v, y] = 1 - v
            else:
                mask[:, v, y] = -1e30 * v
    rows = np.zeros((CAP, ROW), np.float32)
    rows[:, C + 2] = -1
    rows[:, C + 3] = B * T + np.arange(CAP)
    ones = np.repeat(np.array([0x3F803F80, 0], np.uint32), 3)[:, None]
    ones = np.ascontiguousarray(np.broadcast_to(ones, (6, NBUF * HG * T // 2))).view(np.float32)
    return {"c_wide": wide, "c_onehot": onehot.reshape(NB, 2 * NV), "c_mask": mask, "c_rows": rows, "c_ones": ones}


_INS = ["L0_attn_x", "L0_attn_Wq", "L0_attn_bq", "L0_attn_Wk", "L0_attn_bk", "L0_attn_Wv", "L0_attn_bv",
        "L0_attn_Wp", "L0_attn_bp", "L0_attn_rel_bias_table", "L0_ffn_Wr", "L0_ffn_norm_w", "L0_ffn_Wg",
        "L0_ffn_Wu", "L0_ffn_Wd", "L0_ffn_f_norm", "L0_ffn_fWg", "L0_ffn_fWu", "L0_ffn_fWd"]


def kernel(**inputs):
    import numpy as _np
    import concourse.bacc as _bacc
    from concourse import mybir as _mybir
    from concourse.bass_utils import run_bass_kernel_spmd as _run

    nc = _bacc.Bacc("TRN2", target_bir_lowering=False, num_devices=1)
    arrays, args = {}, []
    for name, a in [(n, inputs[n]) for n in _INS] + list(shape_constants().items()):
        a = _np.ascontiguousarray(a)
        arrays[f"in_{name}_dram"] = a
        args.append(nc.dram_tensor(f"in_{name}_dram", a.shape, _mybir.dt.from_np(a.dtype), kind="ExternalInput").ap())
    args.append(nc.dram_tensor("out_0_dram", (B * T + CAP, C), _mybir.dt.float32, kind="ExternalOutput").ap())
    layer_kernel(nc, *args)
    r = _run(nc, [arrays], core_ids=[0])
    return r.results[0]["out_0_dram"][0:B * T].reshape(B, T, C)
```
